# Optimizing a Trainium2 kernel written in Bass

```python
import numpy as np
import jax
import jax.numpy as jnp

def _softmax(x, axis=-1):
    return jax.nn.softmax(x, axis=axis)

def _gelu(x):
    return jax.nn.gelu(x, approximate=True)

def _silu(x):
    return jax.nn.silu(x)

def _sigmoid(x):
    return jax.nn.sigmoid(x)

def _layernorm(x, axis=-1, eps=1e-05):
    m = jnp.mean(x, axis=axis, keepdims=True)
    v = jnp.var(x, axis=axis, keepdims=True)
    return (x - m) / jnp.sqrt(v + eps)

def _scatter_add(tgt, idx, src, axis=0):
    return tgt.at[idx].add(src)

def _segment_sum(src, seg, n):
    return jax.ops.segment_sum(src, seg, n)
kernel_name = 'mk_seq_postln_d2_jaxref_r8_ff1b58'

def setup_inputs(seed: int=0):
    np.random.seed(seed)
    _w = jnp.asarray

    def _L0_attn_setup():
        import jax, jax.numpy as jnp
        import numpy as np
        HIDDEN = 512
        HEAD_DIM = 128
        N_Q_HEADS = 32
        N_KV_HEADS = 8
        SLIDING_WINDOW = 128
        ROPE_THETA = 10000.0
        BATCH, SEQ = (1, 256)

        def _rope(t, pos):
            d = t.shape[-1]
            half = d // 2
            inv_freq = ROPE_THETA ** (-jnp.arange(half, dtype=jnp.float32) / half)
            ang = pos[:, None].astype(jnp.float32) * inv_freq[None, :]
            cos = jnp.cos(ang)[None, :, None, :]
            sin = jnp.sin(ang)[None, :, None, :]
            t1, t2 = (t[..., :half], t[..., half:])
            return jnp.concatenate([t1 * cos - t2 * sin, t1 * sin + t2 * cos], axis=-1)
        key = jax.random.key(seed)
        ks = jax.random.split(key, 5)
        w_scale = HIDDEN ** (-0.5)
        return {'x': jax.random.normal(ks[0], (BATCH, SEQ, HIDDEN), jnp.float32), 'wq': jax.random.normal(ks[1], (HIDDEN, N_Q_HEADS * HEAD_DIM), jnp.float32) * w_scale, 'wk': jax.random.normal(ks[2], (HIDDEN, N_KV_HEADS * HEAD_DIM), jnp.float32) * w_scale, 'wv': jax.random.normal(ks[3], (HIDDEN, N_KV_HEADS * HEAD_DIM), jnp.float32) * w_scale, 'wo': jax.random.normal(ks[4], (N_Q_HEADS * HEAD_DIM, HIDDEN), jnp.float32) * w_scale}
    _L0_attn_in = _L0_attn_setup()

    def _L0_ffn_setup():
        import jax, jax.numpy as jnp
        import numpy as np
        HID, INTER = (512, 1792)
        B, S = (2, 256)

        def _binary_diff_weight(w, base):
            d = w - base
            coeff = jnp.mean(jnp.abs(d))
            return base + coeff * jnp.sign(d)
        key = jax.random.key(seed)
        ks = jax.random.split(key, 7)
        return {'hidden_states': jax.random.normal(ks[0], (B, S, HID), dtype=jnp.float32), 'w1': jax.random.normal(ks[1], (INTER, HID), dtype=jnp.float32) * 0.02, 'mean_w1': jax.random.normal(ks[2], (INTER, HID), dtype=jnp.float32) * 0.02, 'w2': jax.random.normal(ks[3], (HID, INTER), dtype=jnp.float32) * 0.02, 'mean_w2': jax.random.normal(ks[4], (HID, INTER), dtype=jnp.float32) * 0.02, 'w3': jax.random.normal(ks[5], (INTER, HID), dtype=jnp.float32) * 0.02, 'mean_w3': jax.random.normal(ks[6], (INTER, HID), dtype=jnp.float32) * 0.02}
    _L0_ffn_in = _L0_ffn_setup()

    def _L1_attn_setup():
        import jax, jax.numpy as jnp
        import numpy as np
        H = 32
        HKV = 8
        D = 512
        HD = D // H
        S = 128
        MASK_OUT = 0.9
        MIN_REMAIN = 128
        THETA = 10000.0

        def rope_tables(seq_len, hd):
            inv_freq = 1.0 / THETA ** (jnp.arange(0, hd, 2, dtype=jnp.float32) / hd)
            t = jnp.arange(seq_len, dtype=jnp.float32)
            freqs = jnp.outer(t, inv_freq)
            emb = jnp.concatenate([freqs, freqs], axis=-1)
            return (jnp.cos(emb), jnp.sin(emb))

        def rotate_half(x):
            x1, x2 = jnp.split(x, 2, axis=-1)
            return jnp.concatenate([-x2, x1], axis=-1)

        def apply_rope(x, cos, sin):
            return x * cos + rotate_half(x) * sin
        key = jax.random.key(seed)
        k0, k1, k2, k3, k4 = jax.random.split(key, 5)
        hidden_states = jax.random.normal(k0, (1, S, D), jnp.float32)
        Wq = jax.random.normal(k1, (D, D), jnp.float32) * 0.02
        Wk = jax.random.normal(k2, (HKV * HD, D), jnp.float32) * 0.02
        Wv = jax.random.normal(k3, (HKV * HD, D), jnp.float32) * 0.02
        Wo = jax.random.normal(k4, (D, D), jnp.float32) * 0.02
        return {'hidden_states': hidden_states, 'Wq': Wq, 'Wk': Wk, 'Wv': Wv, 'Wo': Wo}
    _L1_attn_in = _L1_attn_setup()

    def _L1_ffn_setup():
        import jax, jax.numpy as jnp
        import numpy as np
        HIDDEN = 512
        INTER = 1376
        SPARSITY = 0.5

        def _ternary_weight(key, out_dim, in_dim, sparsity):
            k_mask, k_sign = jax.random.split(key)
            nonzero = jax.random.bernoulli(k_mask, 1.0 - sparsity, (out_dim, in_dim))
            sign = jnp.where(jax.random.bernoulli(k_sign, 0.5, (out_dim, in_dim)), 1.0, -1.0)
            return (nonzero * sign).astype(jnp.float32)
        key = jax.random.key(seed)
        kx, kg, ku, kd, ksg, ksu, ksd = jax.random.split(key, 7)
        x = jax.random.normal(kx, (4, 256, HIDDEN), dtype=jnp.float32)
        Wg = _ternary_weight(kg, INTER, HIDDEN, SPARSITY)
        Wu = _ternary_weight(ku, INTER, HIDDEN, SPARSITY)
        Wd = _ternary_weight(kd, HIDDEN, INTER, SPARSITY)
        ag = jax.random.uniform(ksg, (INTER,), dtype=jnp.float32, minval=0.5, maxval=1.5) / np.sqrt(HIDDEN)
        au = jax.random.uniform(ksu, (INTER,), dtype=jnp.float32, minval=0.5, maxval=1.5) / np.sqrt(HIDDEN)
        ad = jax.random.uniform(ksd, (HIDDEN,), dtype=jnp.float32, minval=0.5, maxval=1.5) / np.sqrt(INTER)
        return {'x': x, 'Wg': Wg, 'Wu': Wu, 'Wd': Wd, 'ag': ag, 'au': au, 'ad': ad}
    _L1_ffn_in = _L1_ffn_setup()
    _d = {'L0_attn_x': _L0_attn_in['x'], 'L0_attn_wq': _L0_attn_in['wq'], 'L0_attn_wk': _L0_attn_in['wk'], 'L0_attn_wv': _L0_attn_in['wv'], 'L0_attn_wo': _L0_attn_in['wo'], 'L0_ffn_w1': _L0_ffn_in['w1'], 'L0_ffn_mean_w1': _L0_ffn_in['mean_w1'], 'L0_ffn_w2': _L0_ffn_in['w2'], 'L0_ffn_mean_w2': _L0_ffn_in['mean_w2'], 'L0_ffn_w3': _L0_ffn_in['w3'], 'L0_ffn_mean_w3': _L0_ffn_in['mean_w3'], 'L1_attn_Wq': _L1_attn_in['Wq'], 'L1_attn_Wk': _L1_attn_in['Wk'], 'L1_attn_Wv': _L1_attn_in['Wv'], 'L1_attn_Wo': _L1_attn_in['Wo'], 'L1_ffn_Wg': _L1_ffn_in['Wg'], 'L1_ffn_Wu': _L1_ffn_in['Wu'], 'L1_ffn_Wd': _L1_ffn_in['Wd'], 'L1_ffn_ag': _L1_ffn_in['ag'], 'L1_ffn_au': _L1_ffn_in['au'], 'L1_ffn_ad': _L1_ffn_in['ad']}
    _x0 = _d['L0_attn_x']
    _d['L0_attn_x'] = jax.random.normal(jax.random.fold_in(jax.random.key(seed), 1), (2, 512, 512), dtype=_x0.dtype)
    del _x0
    return _d

def reference(L0_attn_x, L0_attn_wq, L0_attn_wk, L0_attn_wv, L0_attn_wo, L0_ffn_w1, L0_ffn_mean_w1, L0_ffn_w2, L0_ffn_mean_w2, L0_ffn_w3, L0_ffn_mean_w3, L1_attn_Wq, L1_attn_Wk, L1_attn_Wv, L1_attn_Wo, L1_ffn_Wg, L1_ffn_Wu, L1_ffn_Wd, L1_ffn_ag, L1_ffn_au, L1_ffn_ad):

    def _L0_attn_ref(x, wq, wk, wv, wo):
        import jax, jax.numpy as jnp
        import numpy as np
        HIDDEN = 512
        HEAD_DIM = 128
        N_Q_HEADS = 32
        N_KV_HEADS = 8
        SLIDING_WINDOW = 128
        ROPE_THETA = 10000.0
        BATCH, SEQ = (1, 256)

        def _rope(t, pos):
            d = t.shape[-1]
            half = d // 2
            inv_freq = ROPE_THETA ** (-jnp.arange(half, dtype=jnp.float32) / half)
            ang = pos[:, None].astype(jnp.float32) * inv_freq[None, :]
            cos = jnp.cos(ang)[None, :, None, :]
            sin = jnp.sin(ang)[None, :, None, :]
            t1, t2 = (t[..., :half], t[..., half:])
            return jnp.concatenate([t1 * cos - t2 * sin, t1 * sin + t2 * cos], axis=-1)
        B, S, _ = x.shape
        G = N_Q_HEADS // N_KV_HEADS
        sm_scale = HEAD_DIM ** (-0.5)
        q = (x @ wq).reshape(B, S, N_Q_HEADS, HEAD_DIM)
        k = (x @ wk).reshape(B, S, N_KV_HEADS, HEAD_DIM)
        v = (x @ wv).reshape(B, S, N_KV_HEADS, HEAD_DIM)
        pos = jnp.arange(S)
        q = _rope(q, pos)
        k = _rope(k, pos)
        qg = q.reshape(B, S, N_KV_HEADS, G, HEAD_DIM)
        scores = jnp.einsum('bqhgd,bshd->bhgqs', qg, k) * sm_scale
        i = pos[:, None]
        j = pos[None, :]
        allowed = (j <= i) & (j > i - SLIDING_WINDOW)
        neg = jnp.finfo(scores.dtype).min
        scores = jnp.where(allowed[None, None, None], scores, neg)
        attn = jax.nn.softmax(scores, axis=-1)
        out = jnp.einsum('bhgqs,bshd->bqhgd', attn, v).reshape(B, S, N_Q_HEADS * HEAD_DIM)
        return out @ wo

    def _L0_ffn_ref(hidden_states, w1, mean_w1, w2, mean_w2, w3, mean_w3):
        import jax, jax.numpy as jnp
        import numpy as np
        HID, INTER = (512, 1792)
        B, S = (2, 256)

        def _binary_diff_weight(w, base):
            d = w - base
            coeff = jnp.mean(jnp.abs(d))
            return base + coeff * jnp.sign(d)
        W1 = _binary_diff_weight(w1, mean_w1)
        W2 = _binary_diff_weight(w2, mean_w2)
        W3 = _binary_diff_weight(w3, mean_w3)
        gate = jnp.einsum('bsh,ih->bsi', hidden_states, W1)
        up = jnp.einsum('bsh,ih->bsi', hidden_states, W3)
        h = jax.nn.silu(gate) * up
        return jnp.einsum('bsi,hi->bsh', h, W2)

    def _L1_attn_ref(hidden_states, Wq, Wk, Wv, Wo):
        import jax, jax.numpy as jnp
        import numpy as np
        H = 32
        HKV = 8
        D = 512
        HD = D // H
        S = 128
        MASK_OUT = 0.9
        MIN_REMAIN = 128
        THETA = 10000.0

        def rope_tables(seq_len, hd):
            inv_freq = 1.0 / THETA ** (jnp.arange(0, hd, 2, dtype=jnp.float32) / hd)
            t = jnp.arange(seq_len, dtype=jnp.float32)
            freqs = jnp.outer(t, inv_freq)
            emb = jnp.concatenate([freqs, freqs], axis=-1)
            return (jnp.cos(emb), jnp.sin(emb))

        def rotate_half(x):
            x1, x2 = jnp.split(x, 2, axis=-1)
            return jnp.concatenate([-x2, x1], axis=-1)

        def apply_rope(x, cos, sin):
            return x * cos + rotate_half(x) * sin
        B, Sq, Dm = hidden_states.shape
        dtype = hidden_states.dtype
        neg = jnp.finfo(dtype).min
        q = (hidden_states @ Wq.T).reshape(B, Sq, H, HD).transpose(0, 2, 1, 3)
        k = (hidden_states @ Wk.T).reshape(B, Sq, HKV, HD).transpose(0, 2, 1, 3)
        v = (hidden_states @ Wv.T).reshape(B, Sq, HKV, HD).transpose(0, 2, 1, 3)
        rep = H // HKV
        k = jnp.repeat(k, rep, axis=1)
        v = jnp.repeat(v, rep, axis=1)
        cos, sin = rope_tables(Sq, HD)
        qr = apply_rope(q, cos, sin)
        kr = apply_rope(k, cos, sin)
        draft = jnp.einsum('bhqd,bhkd->bhqk', qr, kr)
        qi = jnp.arange(Sq)
        ki = jnp.arange(Sq)
        causal_future = qi[:, None] < ki[None, :]
        draft = draft + jnp.where(causal_future, neg, jnp.asarray(0.0, dtype))
        num_remain = max(min(Sq, MIN_REMAIN), Sq - int(Sq * MASK_OUT))
        _, draft_indices = jax.lax.top_k(draft, num_remain)
        mask = jnp.full((B, H, Sq, Sq), neg, dtype)
        b_idx = jnp.arange(B)[:, None, None, None]
        h_idx = jnp.arange(H)[None, :, None, None]
        s_idx = jnp.arange(Sq)[None, None, :, None]
        mask = mask.at[b_idx, h_idx, s_idx, draft_indices].set(0.0)
        mask = jnp.where(causal_future[None, None, :, :], neg, mask)
        scores = jnp.einsum('bhqd,bhkd->bhqk', qr, kr) / np.sqrt(HD).astype(np.float32) + mask
        attn = jax.nn.softmax(scores, axis=-1)
        out = jnp.einsum('bhqk,bhkd->bhqd', attn, v)
        out = out.transpose(0, 2, 1, 3).reshape(B, Sq, Dm)
        return out @ Wo.T

    def _L1_ffn_ref(x, Wg, Wu, Wd, ag, au, ad):
        import jax, jax.numpy as jnp
        import numpy as np
        HIDDEN = 512
        INTER = 1376
        SPARSITY = 0.5

        def _ternary_weight(key, out_dim, in_dim, sparsity):
            k_mask, k_sign = jax.random.split(key)
            nonzero = jax.random.bernoulli(k_mask, 1.0 - sparsity, (out_dim, in_dim))
            sign = jnp.where(jax.random.bernoulli(k_sign, 0.5, (out_dim, in_dim)), 1.0, -1.0)
            return (nonzero * sign).astype(jnp.float32)
        gate = jnp.einsum('bsh,ih->bsi', x, Wg) * ag
        up = jnp.einsum('bsh,ih->bsi', x, Wu) * au
        h = jax.nn.silu(gate) * up
        out = jnp.einsum('bsi,hi->bsh', h, Wd) * ad
        return out
    x = L0_attn_x
    x = _layernorm(x + _L0_attn_ref(x, L0_attn_wq, L0_attn_wk, L0_attn_wv, L0_attn_wo), axis=-1)
    x = _layernorm(x + _L0_ffn_ref(x, L0_ffn_w1, L0_ffn_mean_w1, L0_ffn_w2, L0_ffn_mean_w2, L0_ffn_w3, L0_ffn_mean_w3), axis=-1)
    x = _layernorm(x + _L1_attn_ref(x, L1_attn_Wq, L1_attn_Wk, L1_attn_Wv, L1_attn_Wo), axis=-1)
    x = _layernorm(x + _L1_ffn_ref(x, L1_ffn_Wg, L1_ffn_Wu, L1_ffn_Wd, L1_ffn_ag, L1_ffn_au, L1_ffn_ad), axis=-1)
    return x

_drawn_inputs = setup_inputs


def setup_inputs(seed=0):
    import zlib

    import numpy as np

    out = dict(_drawn_inputs(seed))
    spreads = {}
    factors = {'L1_attn_Wq': 4.056, 'L1_attn_Wk': 4.002}
    for name, (base, spread) in spreads.items():
        noise = np.random.default_rng([zlib.crc32(name.encode()), seed]).standard_normal(out[name].shape)
        drawn = base * np.exp(spread * noise) if base else spread * noise
        out[name] = jnp.asarray(drawn.astype(out[name].dtype))
    for name, factor in factors.items():
        out[name] = (out[name] * factor).astype(out[name].dtype)
    return out
```

```python
from contextlib import ExitStack

import numpy as np
import concourse.bass as bass
from concourse import mybir

F32 = mybir.dt.float32
F32R = mybir.dt.float32r
ALU = mybir.AluOpType
ACT = mybir.ActivationFunctionType
AX = mybir.AxisListType

P = 128
D = 512
DC = D // P
BATCH, SEQ = 2, 512
TOK = BATCH * SEQ
TT = TOK // P
QT = SEQ // P
KVH0, G0, HD0 = 8, 4, 128
SCALE0 = float(HD0) ** -0.5
WQ0, WK0, WV0, WO0 = 0, 2048, 2560, 3072
WCOLS = 5120
KVH1, G1, HD1 = 8, 4, 16
SCALE1 = 0.25
TOPK = 128
INT0, INT1 = 1792, 1376
NT0 = INT0 // P
NT1 = -(-INT1 // P)
FCOLS = 3 * D
MCH = 448
NEG = -3.4028234663852886e38
DROPPED = -1.6e38
TAKEN = -3.0e38
EPS = 1e-5
MAGIC_PASSES = ((0, 0), (0, 1), (1, 0))


def build_kernel(nc, x, attn0_w, ffn0_w, mean_w, attn1_w, ffn1_w, ad_rows, consts, rope0, rope1, out,
                 stop_after=99):
    ctx = ExitStack()
    with ctx:
        def sem(name):
            return ctx.enter_context(nc.semaphore(name))

        AR = ctx.enter_context(nc.sbuf_tensor("AR", [P, 33792], F32R))
        AF = ctx.enter_context(nc.sbuf_tensor("AF", [P, 19300], F32))
        PS = ctx.enter_context(nc.psum_tensor("PS", [P, 8, 512], F32))
        scr = nc.dram_tensor("rope_scratch", (BATCH, 5, 2, P, SEQ), F32, kind="Internal").ap()

        def f32(view):
            return view.bitcast(F32)

        y = AF[:, 0:4096].rearrange("p (t d) -> p t d", t=TT)
        ident = AF[:, 4096:4224]
        eps = AF[:, 4224:4225]
        zeros = AF[:, 4225:4226]
        sums = AF[:, 4228:4231]
        coeff = AF[:, 4232:4235]
        part = AF[:, 4236:4242]
        stats = AF[:, 4244:4244 + 48].rearrange("p (t s) -> p t s", t=TT)
        mv = AF[:, 4292:4308].rearrange("p (t s) -> p t s", t=TT)
        var = AF[:, 4308:4316]
        sd = AF[:, 4316:4324]
        rstd = AF[:, 4324:4332]
        nwt = AF[:, 4332:4340]
        negmax = AF[:, 4340:4356]
        rsum = AF[:, 4356:4372]
        rinv = AF[:, 4372:4388]
        top8 = AF[:, 4388:4396]
        ones = AF[:, 4396:4524]
        base = 4608
        raw = AF[:, base:base + WCOLS]
        o = base + WCOLS
        ctab, stab = AF[:, o:o + 512], AF[:, o + 512:o + 1024]
        mask0 = AF[:, o + 1024:o + 1280]
        o += 1280
        Sm = AF[:, o:o + 2048].rearrange("p (r h k) -> p r h k", r=2, h=4)
        o += 2048
        qs = AF[:, o:o + 1024].rearrange("p (r k) -> p r k", r=2)
        tcos, rot = AF[:, o + 1024:o + 1536], AF[:, o + 1536:o + 2048]
        vtmp = AF[:, o + 2048:o + 2560]
        mch = AF[:, o + 2560:o + 2560 + 4 * MCH].rearrange("p (r w k) -> p r w k", r=2, w=2)
        assert o + 2560 + 4 * MCH <= 19300
        raww = AF[:, base:base + 4 * FCOLS].rearrange("p (r w k) -> p r w k", r=2, w=2)
        raww_flat = AF[:, base:base + 4 * FCOLS].rearrange("p (r k) -> p r k", r=2)
        scale_g, scale_u = raww[:, :, 1, 0:1], raww[:, :, 1, 1:2]
        o = base + 4 * FCOLS
        sg = AF[:, o:o + 1024].rearrange("p (b k) -> p b k", b=2)
        hh = AF[:, o + 1024:o + 2048].rearrange("p (b k) -> p b k", b=2)
        adrow = AF[:, o + 2048:o + 2560]
        S1 = AF[:, base:base + 8192].rearrange("p (h k) -> p h k", h=16)
        o = base + 8192
        P1 = AF[:, o:o + 4096].rearrange("p (r h k) -> p r h k", r=2, h=4)
        mask1 = AF[:, o + 4096:o + 4608]
        work = AF[:, o + 4608:o + 5120]
        assert o + 5120 <= 19300
        mask1_tmp = mask1
        rope1_at = base + WCOLS
        xT = AR[:, 0:8192].rearrange("p (s c k) -> p s c k", s=2, c=DC)
        Wq = AR[:, 8192:12288].rearrange("p (s h c k) -> p s h c k", s=2, h=4, c=DC)
        Wk = AR[:, 12288:13312].rearrange("p (s c k) -> p s c k", s=2, c=DC)
        Wv = AR[:, 13312:14336].rearrange("p (s c k) -> p s c k", s=2, c=DC)
        Wo = AR[:, 14336:18432].rearrange("p (s h k) -> p s h k", s=2, h=4)
        qT = AR[:, 18432:26624].rearrange("p (r s h k) -> p r s h k", r=2, s=2, h=4)
        kT = AR[:, 26624:28672].rearrange("p (r s k) -> p r s k", r=2, s=2)
        V = AR[:, 28672:30720].rearrange("p (r s j k) -> p r s j k", r=2, s=2, j=QT)
        PT = AR[:, 30720:32768].rearrange("p (s j k) -> p s j k", s=2, j=2)
        OT = AR[:, 32768:33792].rearrange("p (s h k) -> p s h k", s=2, h=4)
        W13 = AR[:, 8192:12288].rearrange("p (r s m c k) -> p r s m c k", r=2, s=2, m=2, c=DC)
        W2 = AR[:, 12288:14336].rearrange("p (r s k) -> p r s k", r=2, s=2)
        hT = AR[:, 14336:18432].rearrange("p (r s k) -> p r s k", r=2, s=2)
        qst = AR[:, 0:8192].rearrange("p (r h k) -> p r h k", r=2, h=32)
        kst = AR[:, 8192:12288].rearrange("p (h k) -> p h k", h=KVH1)
        rq = AR[:, 18432:20480].rearrange("p (r s k) -> p r s k", r=2, s=2)
        Vc = AR[:, 20480:22528].rearrange("p (s t k) -> p s t k", s=2, t=TT)
        Vz = AR[:, 22528:31744].rearrange("p (s j k) -> p s j k", s=2, j=QT)
        PT1 = AR[:, 31744:32768 + 1024].rearrange("p (r s k) -> p r s k", r=2, s=2)
        OT1 = AR[:, 18432:19456].rearrange("p (s h k) -> p s h k", s=2, h=4)

        s_const = sem("s_const")
        s_ready = sem("s_ready")
        s_x = sem("s_x")
        s_out = sem("s_out")

        def wait(eng, s, v):
            if isinstance(v, int) and v <= 0:
                return
            eng.wait_ge(s, v)

        def mm3(dst, lhs, rhs, n, flags=True, more=False, first=True):
            k = 0
            last = None
            for c in range(n):
                for a, m in MAGIC_PASSES:
                    last = nc.tensor.matmul(dst, lhs(a, c), rhs(m, c), start=(first and k == 0),
                                            stop=(k == 3 * n - 1 and not more))
                    k += 1
            return last

        def names(tag, *ns):
            return {n: sem(f"{tag}_{n}") for n in ns}

        def turn_pe(pe, k):
            for t in range(TT):
                pe.wait_ge(T["fed"], TT * k + t + 1)
                wait(pe, T["low"], TT * k + t - 1 if t >= 2 else TT * k)
                for c in range(DC):
                    last = nc.tensor.transpose(PS[:, t % 2, c * P:(c + 1) * P], y[:, t, c * P:(c + 1) * P], ident)
                last.then_inc(T["turned"], 1)
            pe.wait_ge(T["low"], TT * (k + 1))

        def turn_act(act, k):
            for t in range(TT):
                act.wait_ge(T["turned"], TT * k + t + 1)
                nc.scalar.activation(xT[:, 0, :, t * P:(t + 1) * P],
                                     PS[:, t % 2, :].rearrange("p (c k) -> p c k", c=DC),
                                     ACT.Copy).then_inc(T["high"], 1)

        def turn_dve(dve, k, t):
            dve.wait_ge(T["high"], TT * k + t + 1)
            nc.vector.tensor_tensor(xT[:, 1, :, t * P:(t + 1) * P],
                                    PS[:, t % 2, :].rearrange("p (c k) -> p c k", c=DC),
                                    f32(xT[:, 0, :, t * P:(t + 1) * P]), ALU.subtract).then_inc(T["low"], 1)

        def norm_dve(dve, k, sem_added, n_added, turns=True):
            a, v = TT * (k - 1), 6 * (k - 1)
            dve.wait_ge(sem_added, n_added)
            for t in range(TT):
                nc.vector.bn_stats(stats[:, t, :], y[:, t, :]).then_inc(N["stats"], 1)
            for t in range(TT):
                dve.wait_ge(N["stats"], a + t + 1)
                nc.vector.bn_aggr(mv[:, t, :], stats[:, t, :]).then_inc(N["aggr"], 1)
            dve.wait_ge(N["aggr"], a + TT)
            nc.vector.tensor_scalar(var, mv[:, :, 1], EPS, None, ALU.add).then_inc(N["var"], 1)
            dve.wait_ge(N["sqrt"], k)
            nc.vector.reciprocal(rstd, sd).then_inc(N["var"], 1)
            dve.wait_ge(N["var"], v + 2)
            nc.vector.tensor_tensor(nwt, rstd, rstd, ALU.mult).then_inc(N["var"], 1)
            dve.wait_ge(N["var"], v + 3)
            nc.vector.tensor_tensor(nwt, nwt, var, ALU.mult).then_inc(N["var"], 1)
            dve.wait_ge(N["var"], v + 4)
            nc.vector.tensor_scalar(nwt, nwt, -0.5, 1.5, ALU.mult, ALU.add).then_inc(N["var"], 1)
            dve.wait_ge(N["var"], v + 5)
            nc.vector.tensor_tensor(rstd, rstd, nwt, ALU.mult).then_inc(N["var"], 1)
            dve.wait_ge(N["var"], v + 6)
            for t in range(TT):
                nc.vector.tensor_scalar(y[:, t, :], y[:, t, :], mv[:, t, 0:1], rstd[:, t:t + 1],
                                        ALU.subtract, ALU.mult).then_inc(T["fed"], 1)
                if t >= 1 and turns:
                    turn_dve(dve, k, t - 1)
            if turns:
                turn_dve(dve, k, TT - 1)

        def norm_act(act, k):
            act.wait_ge(N["var"], 6 * (k - 1) + 1)
            nc.scalar.activation(sd, var, ACT.Sqrt).then_inc(N["sqrt"], 1)

        T = names("turn", "fed", "turned", "high", "low")
        N = names("norm", "stats", "aggr", "var", "sqrt")

        A0 = names("a0", "raw_qkv", "raw_wo", "wq_hi", "wq_lo", "wk_hi", "wk_lo", "wv_hi", "wv_lo", "wo_hi", "wo_lo",
                   "scores", "masked", "maxed", "negmax", "exp", "rinv", "pnorm", "turned", "pt_hi", "pt_lo", "pv",
                   "o_hi", "o_lo", "yproj", "yadd", "vproj", "vcopy", "vturned", "v_hi", "v_lo",
                   "mean_in0", "mean_in1", "mean_d", "mean_abs", "mean_sum", "coeff_ps", "coeff")
        R0 = names("r0", "proj", "swap", "cos", "sin", "rot", "hi", "lo")
        NU = BATCH * QT

        def head_item(h):
            return 0 if h == 0 else h + 1

        def w_piece(kind, h):
            if kind == "q":
                return raw[:, WQ0 + h * 512:WQ0 + (h + 1) * 512].rearrange("p (c k) -> p c k", c=DC), Wq[:, :, h]
            if kind == "k":
                return raw[:, WK0:WK0 + 512].rearrange("p (c k) -> p c k", c=DC), Wk
            if kind == "v":
                return raw[:, WV0:WV0 + 512].rearrange("p (c k) -> p c k", c=DC), Wv
            return raw[:, WO0:WO0 + 2048].rearrange("p (h k) -> p h k", h=4), Wo

        def split_hi(act, A, kind, g, h=0):
            src, dst = w_piece(kind, h)
            wait(act, A["raw_wo"] if kind == "o" else A["raw_qkv"], 16 * (g + 1))
            if A is A0:
                if kind == "q":
                    wait(act, R0["proj"], 10 * g - 5 + head_item(h) + 1)
                elif kind == "k":
                    wait(act, R0["proj"], 10 * g - 5 + 1 + 1)
                elif kind == "v":
                    wait(act, A0["vproj"], 2 * g)
                else:
                    wait(act, A0["yproj"], NU * g)
            nc.scalar.activation(dst[:, 0], src, ACT.Copy).then_inc(A[f"w{kind}_hi"], 1)

        def split_lo(pool, A, kind, g, h=0):
            src, dst = w_piece(kind, h)
            pool.wait_ge(A[f"w{kind}_hi"], (4 * g + h if kind == "q" else g) + 1)
            nc.gpsimd.tensor_tensor(dst[:, 1], src, f32(dst[:, 0]), ALU.subtract).then_inc(A[f"w{kind}_lo"], 1)

        PIECES = {0: [("o", 0, 0)], 1: [("q", 0, 1), ("k", 0, 1)], 2: [("q", 1, 1), ("v", 0, 1)],
                  3: [("q", 2, 1)], 4: [("q", 3, 1)]}

        def groups(eng, body):
            body(0, True, False)
            with eng.Fori(1, KVH0 - 1) as g:
                body(g, False, False)
            body(KVH0 - 1, False, True)

        def items0(bb, j):
            its = [(5 * bb + head_item(j), "q", j)]
            if j == 0:
                its.append((5 * bb + 1, "k", 0))
            return its

        def rope_act1(act, r, src, slot):
            act.wait_ge(R0["proj"], r + 1)
            wait(act, R0["rot"], r - 1)
            nc.scalar.activation(qs[0:64, slot, :], src[64:128, :], ACT.Copy)
            nc.scalar.activation(qs[64:128, slot, :], src[0:64, :], ACT.Copy).then_inc(R0["swap"], 1)

        def slot_of(k, b, j):
            return (5 * b + (1 if k == "k" else head_item(j))) % 2

        def src0(k):
            return PS[:, 6, :] if k == "q" else PS[:, 7, :]

        def dst0(k, b, j, s):
            return qT[:, b, s, j, :] if k == "q" else kT[:, b, s, :]

        def pe_proj_item(pe, g, bb, b, k, j, r):
            if k == "q":
                pe.wait_ge(A0["wq_lo"], 4 * g + j + 1)
                if j == 0:
                    wait(pe, R0["swap"], r)
                    wait(pe, R0["cos"], r)
                elif j == 1:
                    wait(pe, R0["swap"], r - 1)
                    wait(pe, R0["cos"], r - 1)
                else:
                    wait(pe, R0["swap"], r)
                    wait(pe, R0["cos"], r)
            else:
                pe.wait_ge(A0["wk_lo"], g + 1)
                wait(pe, A0["v_lo"], bb)
            w = Wq[:, :, j] if k == "q" else Wk
            mm3(src0(k), lambda a, c: w[:, a, c, :], lambda m, c: xT[:, m, c, b * SEQ:(b + 1) * SEQ], DC)\
                .then_inc(R0["proj"], 1)

        def pe_v(pe, g, bb, b, r):
            pe.wait_ge(A0["wv_lo"], g + 1)
            pe.wait_ge(R0["swap"], 5 * bb + 2)
            pe.wait_ge(R0["cos"], 5 * bb + 2)
            mm3(PS[:, 7, :], lambda a, c: Wv[:, a, c, :], lambda m, c: xT[:, m, c, b * SEQ:(b + 1) * SEQ], DC)\
                .then_inc(A0["vproj"], 1)

        def pe_vturn(pe, bb):
            pe.wait_ge(A0["vcopy"], bb + 1)
            for j in range(QT):
                last = nc.tensor.transpose(PS[:, 7, j * P:(j + 1) * P], vtmp[:, j * P:(j + 1) * P], ident)
            last.then_inc(A0["vturned"], 1)

        def pe_attn0(pe):
            def body(g, first, last_group):
                for u in range(NU):
                    b, i = u // QT, u % QT
                    n = NU * g + u
                    bb = 2 * g + b
                    pe.wait_ge(R0["lo"], 5 * bb + 5)
                    wait(pe, A0["masked"], n)
                    lo = 1 if i == 0 else 0
                    for h in range(G0):
                        dst = PS[:, h // 2, (h % 2) * 256 + lo * P:(h % 2) * 256 + 256]
                        last = mm3(dst, lambda a, c: qT[:, b, a, h, i * P:(i + 1) * P],
                                   lambda m, c: kT[:, b, m, (i - 1 + lo) * P:(i + 1) * P], 1)
                    last.then_inc(A0["scores"], 1)
                    if not (first and u == 0):
                        turn_p(n - 1, (u - 1) % QT)
                    nb, j = (b + 1) % 2, i
                    ng = g if b == 0 else g + 1
                    has_next = not (last_group and b == 1)
                    if has_next:
                        pe_proj_item(pe, ng, bb + 1, nb, "q", j, 5 * (bb + 1) + head_item(j))
                    if not (first and u == 0):
                        pv(n - 1, (u - 1) % QT, ((u - 1) // QT) % 2)
                    if has_next:
                        if j == 0:
                            pe_proj_item(pe, ng, bb + 1, nb, "k", 0, 5 * (bb + 1) + 1)
                        if j == 1:
                            pe_v(pe, ng, bb + 1, nb, 0)
                        if j == 2:
                            pe_vturn(pe, bb + 1)
                    if not (first and u == 0):
                        oproj(n - 1, g if u > 0 else g - 1)

            def turn_p(n, i):
                pe.wait_ge(A0["pnorm"], n + 1)
                for kb in range(1 if i == 0 else 0, 2):
                    for h in range(G0):
                        last = nc.tensor.transpose(PS[:, 2 + kb, h * P:(h + 1) * P],
                                                   Sm[:, par2(i), h, kb * P:(kb + 1) * P], ident)
                last.then_inc(A0["turned"], 1)

            def par2(i):
                return i % 2

            def pv(n, i, b):
                pe.wait_ge(A0["pt_lo"], n + 1)
                wait(pe, A0["o_lo"], n)
                k0 = 1 if i == 0 else 0
                mm3(PS[:, 4, :], lambda a, c: V[:, b, a, i - 1 + k0 + c, :], lambda m, c: PT[:, m, k0 + c, :],
                    2 - k0).then_inc(A0["pv"], 1)

            def oproj(n, g):
                pe.wait_ge(A0["wo_lo"], g + 1)
                pe.wait_ge(A0["o_lo"], n + 1)
                wait(pe, A0["yadd"], n)
                mm3(PS[:, 5, :], lambda a, c: OT[:, a, c, :], lambda m, c: Wo[:, m, c, :], G0)\
                    .then_inc(A0["yproj"], 1)

            for j in range(G0):
                pe_proj_item(pe, 0, 0, 0, "q", j, head_item(j))
                if j == 0:
                    pe_proj_item(pe, 0, 0, 0, "k", 0, 1)
                if j == 1:
                    pe_v(pe, 0, 0, 0, 0)
                if j == 2:
                    pe_vturn(pe, 0)
            pe.wait_ge(A0["v_lo"], 1)
            groups(pe, body)
            n = NU * KVH0
            turn_p(n - 1, QT - 1)
            pv(n - 1, QT - 1, 1)
            oproj(n - 1, KVH0 - 1)
            pe.wait_ge(A0["mean_sum"], 6 * KVH0 + 1)
            nc.tensor.matmul(PS[:, 6, 0:3], ones, sums, start=True, stop=True).then_inc(A0["coeff_ps"], 1)

        def act_attn0(act):
            def rope_hi(r, k, b, j):
                act.wait_ge(R0["rot"], r + 1)
                nc.scalar.activation(dst0(k, b, j, 0), rot, ACT.Copy).then_inc(R0["hi"], 1)

            def vcopy(bb):
                act.wait_ge(A0["vproj"], bb + 1)
                nc.scalar.activation(vtmp, PS[:, 7, :], ACT.Copy).then_inc(A0["vcopy"], 1)

            def v_hi(bb, b):
                act.wait_ge(A0["vturned"], bb + 1)
                nc.scalar.activation(V[:, b, 0], PS[:, 7, :].rearrange("p (j k) -> p j k", j=QT), ACT.Copy)\
                    .then_inc(A0["v_hi"], 1)

            def pt_hi(n, i):
                act.wait_ge(A0["turned"], n + 1)
                k0 = 1 if i == 0 else 0
                nc.scalar.activation(PT[:, 0, k0:2, :], PS[:, 2 + k0:4, :], ACT.Copy).then_inc(A0["pt_hi"], 1)

            def o_hi(n):
                act.wait_ge(A0["pv"], n + 1)
                nc.scalar.activation(OT[:, 0], PS[:, 4, :].rearrange("p (h k) -> p h k", h=4), ACT.Copy)\
                    .then_inc(A0["o_hi"], 1)

            def mean_abs(g, s):
                act.wait_ge(A0["mean_d"], 6 * g + s + 1)
                wait(act, A0["mean_sum"], 6 * (g - 1) + s + 1 + 1)
                nc.scalar.activation(mch[:, s % 2, 0, :], mch[:, s % 2, 0, :], ACT.Abs,
                                     accum_out=part[:, s:s + 1]).then_inc(A0["mean_abs"], 1)

            for h in range(G0):
                split_hi(act, A0, "q", 0, h)
            for k in ("k", "v", "o"):
                split_hi(act, A0, k, 0)
            for j in range(G0):
                for r, k, h in items0(0, j):
                    rope_act1(act, r, src0(k), slot_of(k, 0, j))
                    rope_hi(r, k, 0, j)
                if j == 1:
                    vcopy(0)
                if j == 2:
                    v_hi(0, 0)

            def body(g, first, last_group):
                for u in range(NU):
                    b, i = u // QT, u % QT
                    n = NU * g + u
                    bb = 2 * g + b
                    nb, j = (b + 1) % 2, i
                    has_next = not (last_group and b == 1)
                    if not (first and u == 0):
                        pt_hi(n - 1, (u - 1) % QT)
                    its = items0(bb + 1, j) if has_next else []
                    if its:
                        rope_act1(act, its[0][0], src0("q"), slot_of("q", nb, j))
                    if not (first and u == 0):
                        o_hi(n - 1)
                    act.wait_ge(A0["negmax"], n + 1)
                    k0 = 1 if i == 0 else 0
                    for h in range(G0):
                        sl = Sm[:, u % 2, h, k0 * P:256]
                        last = nc.scalar.activation(sl, sl, ACT.Exp, bias=negmax[:, h:h + 1], scale=SCALE0,
                                                    accum_out=rsum[:, h:h + 1])
                    last.then_inc(A0["exp"], 1)
                    if its:
                        rope_hi(its[0][0], "q", nb, j)
                    if len(its) > 1:
                        rope_act1(act, its[1][0], src0("k"), slot_of("k", nb, j))
                        rope_hi(its[1][0], "k", nb, j)
                    if has_next and j == 1:
                        vcopy(bb + 1)
                    if has_next and j == 2:
                        v_hi(bb + 1, nb)
                    for kind, h, ahead in PIECES.get(u, []):
                        if (ahead and last_group) or (first and not ahead):
                            continue
                        split_hi(act, A0, kind, g + ahead, h)
                    if u < 6:
                        mean_abs(g, u)

            groups(act, body)
            n = NU * KVH0
            pt_hi(n - 1, QT - 1)
            o_hi(n - 1)

        def pool_attn0(pool):
            def rope_sin(r, slot):
                pool.wait_ge(R0["swap"], r + 1)
                nc.gpsimd.tensor_tensor(qs[:, slot, :], qs[:, slot, :], stab, ALU.mult).then_inc(R0["sin"], 1)

            def pnorm(n, i):
                pool.wait_ge(A0["rinv"], n + 1)
                k0 = 1 if i == 0 else 0
                sl = Sm[:, i % 2, :, k0 * P:256]
                nc.gpsimd.tensor_tensor(sl, sl, rinv[:, 0:4].unsqueeze(2).to_broadcast([P, G0, (2 - k0) * P]),
                                        ALU.mult).then_inc(A0["pnorm"], 1)

            def mean(g, s):
                pool.wait_ge(A0[f"mean_in{s % 2}"], 16 * (3 * g + s // 2 + 1))
                nc.gpsimd.tensor_tensor(mch[:, s % 2, 0, :], mch[:, s % 2, 0, :], mch[:, s % 2, 1, :],
                                        ALU.subtract).then_inc(A0["mean_d"], 1)

            def mean_add(g, s):
                m = s // 2
                pool.wait_ge(A0["mean_abs"], 6 * g + s + 1)
                pool.wait_ge(A0["mean_sum"], 6 * g + s + 1)
                nc.gpsimd.tensor_tensor(sums[:, m:m + 1], sums[:, m:m + 1], part[:, s:s + 1], ALU.add)\
                    .then_inc(A0["mean_sum"], 1)

            nc.gpsimd.memset(sums, 0.0).then_inc(A0["mean_sum"], 1)
            pool.wait_ge(s_const, CONST_DMAS * 16)
            for h in range(G0):
                split_lo(pool, A0, "q", 0, h)
            for k in ("k", "v", "o"):
                split_lo(pool, A0, k, 0)
            for j in range(G0):
                for r, k, h in items0(0, j):
                    rope_sin(r, slot_of(k, 0, j))

            def body(g, first, last_group):
                for u in range(NU):
                    b, i = u // QT, u % QT
                    n = NU * g + u
                    bb = 2 * g + b
                    nb, j = (b + 1) % 2, i
                    has_next = not (last_group and b == 1)
                    its = items0(bb + 1, j) if has_next else []
                    if its:
                        rope_sin(its[0][0], slot_of("q", nb, j))
                    pnorm(n, i)
                    if len(its) > 1:
                        rope_sin(its[1][0], slot_of("k", nb, j))
                    for kind, h, ahead in PIECES.get(u, []):
                        if (ahead and last_group) or (first and not ahead):
                            continue
                        split_lo(pool, A0, kind, g + ahead, h)
                    if u < 6:
                        mean(g, u)
                    if 1 <= u < 7:
                        mean_add(g, u - 1)

            groups(pool, body)

        def dve_attn0(dve):
            def rope_cos(r, k):
                dve.wait_ge(R0["swap"], r + 1)
                wait(dve, R0["rot"], r)
                nc.vector.tensor_tensor(tcos, src0(k), ctab, ALU.mult).then_inc(R0["cos"], 1)

            def rope_rot(r, slot):
                dve.wait_ge(R0["sin"], r + 1)
                dve.wait_ge(R0["cos"], r + 1)
                wait(dve, R0["hi"], r)
                wait(dve, R0["lo"], r)
                nc.vector.tensor_tensor(rot, tcos, qs[:, slot, :], ALU.add).then_inc(R0["rot"], 1)

            def rope_lo(r, k, b, j):
                dve.wait_ge(R0["hi"], r + 1)
                nc.vector.tensor_tensor(dst0(k, b, j, 1), rot, f32(dst0(k, b, j, 0)), ALU.subtract)\
                    .then_inc(R0["lo"], 1)

            def v_lo(bb, b):
                dve.wait_ge(A0["v_hi"], bb + 1)
                nc.vector.tensor_tensor(V[:, b, 1], PS[:, 7, :].rearrange("p (j k) -> p j k", j=QT),
                                        f32(V[:, b, 0]), ALU.subtract).then_inc(A0["v_lo"], 1)

            def yadd(n, t):
                dve.wait_ge(A0["yproj"], n + 1)
                nc.vector.tensor_tensor(y[:, t, :], PS[:, 5, :], y[:, t, :], ALU.add).then_inc(A0["yadd"], 1)

            def pt_lo(n, i):
                dve.wait_ge(A0["pt_hi"], n + 1)
                k0 = 1 if i == 0 else 0
                nc.vector.tensor_tensor(PT[:, 1, k0:2, :], PS[:, 2 + k0:4, :], f32(PT[:, 0, k0:2, :]),
                                        ALU.subtract).then_inc(A0["pt_lo"], 1)

            def o_lo(n):
                dve.wait_ge(A0["o_hi"], n + 1)
                nc.vector.tensor_tensor(OT[:, 1], PS[:, 4, :].rearrange("p (h k) -> p h k", h=4), f32(OT[:, 0]),
                                        ALU.subtract).then_inc(A0["o_lo"], 1)

            for j in range(G0):
                for r, k, h in items0(0, j):
                    rope_cos(r, k)
                    rope_rot(r, slot_of(k, 0, j))
                    rope_lo(r, k, 0, j)
                if j == 2:
                    v_lo(0, 0)

            def body(g, first, last_group):
                for u in range(NU):
                    b, i = u // QT, u % QT
                    n = NU * g + u
                    bb = 2 * g + b
                    nb, j = (b + 1) % 2, i
                    has_next = not (last_group and b == 1)
                    its = items0(bb + 1, j) if has_next else []
                    if not (first and u < 2):
                        yadd(n - 2, (u - 2) % NU)
                    k0 = 1 if i == 0 else 0
                    dve.wait_ge(A0["scores"], n + 1)
                    src = PS[:, 0:2, :].rearrange("p a (h k) -> p (a h) k", h=2)[:, :, k0 * P:256]
                    nc.vector.tensor_tensor(Sm[:, u % 2, :, k0 * P:256], src,
                                            mask0[:, k0 * P:256].unsqueeze(1).to_broadcast([P, G0, (2 - k0) * P]),
                                            ALU.add).then_inc(A0["masked"], 1)
                    if not (first and u == 0):
                        pt_lo(n - 1, (u - 1) % QT)
                    dve.wait_ge(A0["masked"], n + 1)
                    wait(dve, A0["exp"], n)
                    nc.vector.tensor_reduce(negmax[:, 0:4], Sm[:, u % 2, :, k0 * P:256], AX.X, ALU.max)\
                        .then_inc(A0["maxed"], 1)
                    if its:
                        rope_cos(its[0][0], "q")
                    dve.wait_ge(A0["maxed"], n + 1)
                    nc.vector.tensor_scalar(negmax[:, 0:4], negmax[:, 0:4], -SCALE0, None, ALU.mult)\
                        .then_inc(A0["negmax"], 1)
                    if not (first and u == 0):
                        o_lo(n - 1)
                    if its:
                        rope_rot(its[0][0], slot_of("q", nb, j))
                    dve.wait_ge(A0["exp"], n + 1)
                    wait(dve, A0["pnorm"], n)
                    nc.vector.reciprocal(rinv[:, 0:4], rsum[:, 0:4]).then_inc(A0["rinv"], 1)
                    if its:
                        rope_lo(its[0][0], "q", nb, j)
                    if len(its) > 1:
                        rope_cos(its[1][0], "k")
                        rope_rot(its[1][0], slot_of("k", nb, j))
                        rope_lo(its[1][0], "k", nb, j)
                    if has_next and j == 2:
                        v_lo(bb + 1, nb)

            groups(dve, body)
            n = NU * KVH0
            yadd(n - 2, NU - 2)
            pt_lo(n - 1, QT - 1)
            o_lo(n - 1)
            yadd(n - 1, NU - 1)
            dve.wait_ge(A0["coeff_ps"], 1)
            nc.vector.tensor_scalar(coeff, PS[:, 6, 0:3], 1.0 / (INT0 * D), None, ALU.mult).then_inc(A0["coeff"], 1)

        def sp_attn0(sp):
            def mean(g, s):
                wait(sp, A0["mean_abs"], 6 * g + s - 1)
                sp.dma_start(mch[:, s % 2], mean_w[slice_at(6 * g + s)].rearrange("o p w k -> p (o w) k"))\
                    .then_inc(A0[f"mean_in{s % 2}"], 16)

            def slice_at(v):
                return bass.ds(v, 1)

            def weights(g):
                wait(sp, A0["wq_lo"], 4 * g)
                wait(sp, A0["wk_lo"], g)
                wait(sp, A0["wv_lo"], g)
                sp.dma_start(raw[:, 0:WO0], attn0_w[slice_at(g), :, 0:WO0].rearrange("o p k -> p (o k)"))\
                    .then_inc(A0["raw_qkv"], 16)
                wait(sp, A0["wo_lo"], g)
                sp.dma_start(raw[:, WO0:WCOLS], attn0_w[slice_at(g), :, WO0:WCOLS].rearrange("o p k -> p (o k)"))\
                    .then_inc(A0["raw_wo"], 16)

            weights(0)

            def body(g, first, last_group):
                mean(g, 0)
                mean(g, 1)
                if not last_group:
                    weights(g + 1)
                for s in range(2, 6):
                    mean(g, s)

            groups(sp, body)

        def ffn_sems(tag):
            return names(tag, "raw0", "raw1", "d", "sign", "w", "w13_hi", "w13_lo", "w2_hi", "w2_lo", "gate", "silu", "h",
                         "h_hi", "h_lo", "down", "yadd", "ad")

        F0, F1 = ffn_sems("f0"), ffn_sems("f1")

        def tiles(eng, nt, body):
            body(0, 0, True)
            body(1, 1, False)
            body(2, 0, False)
            pairs = (nt - 1) // 2
            with eng.Fori(1, pairs) as p:
                body(2 * p + 1, 1, False)
                body(2 * p + 2, 0, False)
            if (nt - 1) % 2:
                body(nt - 1, (nt - 1) % 2, False)

        def sp_ffn(sp, F, nt, wdram, diff, before):
            before(sp)

            def load(j, s, first):
                if not first:
                    if diff:
                        wait(sp, F["w2_lo"], j - 1)
                    else:
                        wait(sp, F["h_lo"], 2 * (j - 1))
                sp.dma_start(raww_flat[:, s, 0:wdram.shape[2]], wdram[bass.ds(j, 1)].rearrange("o p k -> p (o k)"))\
                    .then_inc(F[f"raw{s}"], 16)

            load(0, 0, True)
            load(1, 1, True)
            pairs = (nt - 2) // 2
            with sp.Fori(1, 1 + pairs) as p:
                load(2 * p, 0, False)
                load(2 * p + 1, 1, False)
            if nt % 2:
                load(nt - 1, 0, False)

        def pool_ffn(pool, F, nt, diff):
            def loaded(pool, j, s):
                n = 8 * (j + 2 - s)
                pool.wait_ge(F[f"raw{s}"], n)

            def prep(j, s):
                if diff:
                    loaded(pool, j, s)
                    nc.gpsimd.tensor_tensor(raww[:, s, 0], raww[:, s, 0], raww[:, s, 1], ALU.subtract)\
                        .then_inc(F["d"], 1)
                else:
                    loaded(pool, j, s)
                    nc.gpsimd.tensor_tensor(raww[:, s, 0, 1024:1536], raww[:, s, 0, 1024:1536], adrow, ALU.mult)\
                        .then_inc(F["w"], 1)

            def w13_lo(j, s):
                pool.wait_ge(F["w13_hi"], j + 1)
                nc.gpsimd.tensor_tensor(W13[:, s, 1].rearrange("p m c k -> p (m c k)"), raww[:, s, 0, 0:1024],
                                        f32(W13[:, s, 0].rearrange("p m c k -> p (m c k)")), ALU.subtract)\
                    .then_inc(F["w13_lo"], 1)

            def w2_lo(j, s):
                pool.wait_ge(F["w2_hi"], j + 1)
                nc.gpsimd.tensor_tensor(W2[:, s, 1], raww[:, s, 0, 1024:1536], f32(W2[:, s, 0]), ALU.subtract)\
                    .then_inc(F["w2_lo"], 1)

            def h_lo(j, s, b):
                pool.wait_ge(F["h_hi"], 2 * j + b + 1)
                sl = slice(b * SEQ, (b + 1) * SEQ)
                nc.gpsimd.tensor_tensor(hT[:, s, 1, sl], hh[:, b], f32(hT[:, s, 0, sl]), ALU.subtract)\
                    .then_inc(F["h_lo"], 1)

            prep(0, 0)
            w13_lo(0, 0)

            def body(j, s, first, last=False):
                w2_lo(j, s)
                if not last:
                    prep(j + 1, 1 - s)
                h_lo(j, s, 0)
                if not last:
                    w13_lo(j + 1, 1 - s)
                h_lo(j, s, 1)

            tiles(pool, nt - 1, body)
            body(nt - 1, (nt - 1) % 2, False, True)

        def act_ffn(act, F, nt, diff):
            def sign(j, s):
                if diff:
                    act.wait_ge(F["d"], j + 1)
                    nc.scalar.activation(raww[:, s, 0], raww[:, s, 0], ACT.Sign).then_inc(F["sign"], 1)

            def w13_hi(j, s):
                act.wait_ge(F["w"], j + 1)
                wait(act, F["gate"], 2 * (j - 1))
                nc.scalar.activation(W13[:, s, 0].rearrange("p m c k -> p (m c k)"), raww[:, s, 0, 0:1024],
                                     ACT.Copy).then_inc(F["w13_hi"], 1)

            def w2_hi(j, s):
                wait(act, F["down"], TT * (j - 1))
                nc.scalar.activation(W2[:, s, 0], raww[:, s, 0, 1024:1536], ACT.Copy).then_inc(F["w2_hi"], 1)

            def silu(j, b, tile_scale):
                act.wait_ge(F["gate"], 2 * j + b + 1)
                wait(act, F["h"], 2 * (j - 1) + b + 1)
                nc.scalar.activation(sg[:, b], PS[:, 2 * b, :], ACT.Silu, scale=tile_scale).then_inc(F["silu"], 1)

            def h_hi(j, s, b):
                act.wait_ge(F["h"], 2 * j + b + 1)
                wait(act, F["down"], TT * (j - 1))
                nc.scalar.activation(hT[:, s, 0, b * SEQ:(b + 1) * SEQ], hh[:, b], ACT.Copy).then_inc(F["h_hi"], 1)

            sign(0, 0)
            w13_hi(0, 0)

            def body(j, s, first, last=False):
                w2_hi(j, s)
                sc = 1.0 if diff else scale_g[:, s]
                silu(j, 0, sc)
                if not last:
                    sign(j + 1, 1 - s)
                h_hi(j, s, 0)
                silu(j, 1, sc)
                if not last:
                    w13_hi(j + 1, 1 - s)
                h_hi(j, s, 1)

            tiles(act, nt - 1, body)
            body(nt - 1, (nt - 1) % 2, False, True)

        def dve_ffn(dve, F, nt, diff):
            def combine(j, s):
                if diff:
                    dve.wait_ge(F["sign"], j + 1)
                    for m in range(3):
                        sl = slice(512 * m, 512 * (m + 1))
                        last = nc.vector.scalar_tensor_tensor(raww[:, s, 0, sl], raww[:, s, 0, sl], coeff[:, m:m + 1],
                                                              raww[:, s, 1, sl], ALU.mult, ALU.add)
                    last.then_inc(F["w"], 1)

            def h(j, s, b):
                dve.wait_ge(F["silu"], 2 * j + b + 1)
                wait(dve, F["h_lo"], 2 * (j - 1) + b + 1)
                if diff:
                    ins = nc.vector.tensor_tensor(hh[:, b], PS[:, 2 * b + 1, :], sg[:, b], ALU.mult)
                else:
                    ins = nc.vector.scalar_tensor_tensor(hh[:, b], PS[:, 2 * b + 1, :], scale_u[:, s],
                                                         sg[:, b], ALU.mult, ALU.mult)
                ins.then_inc(F["h"], 1)

            def yadd(j, t):
                dve.wait_ge(F["down"], TT * j + t + 1)
                nc.vector.tensor_tensor(y[:, t, :], PS[:, 4 + t % 4, :], y[:, t, :], ALU.add).then_inc(F["yadd"], 1)

            if diff:
                dve.wait_ge(A0["coeff"], 1)
            combine(0, 0)

            def body(j, s, first, last=False):
                h(j, s, 0)
                h(j, s, 1)
                if not last:
                    combine(j + 1, 1 - s)
                if not first:
                    for t in range(TT):
                        yadd(j - 1, t)

            tiles(dve, nt - 1, body)
            body(nt - 1, (nt - 1) % 2, False, True)
            for t in range(TT):
                yadd(nt - 1, t)

        def pe_ffn(pe, F, nt):
            def gate(j, s, b):
                pe.wait_ge(F["w13_lo"], j + 1)
                wait(pe, F["h"], 2 * (j - 1) + b + 1)
                for m in range(2):
                    last = mm3(PS[:, 2 * b + m, :], lambda a, c: W13[:, s, a, m, c, :],
                               lambda q, c: xT[:, q, c, b * SEQ:(b + 1) * SEQ], DC)
                last.then_inc(F["gate"], 1)

            def down(j, s):
                pe.wait_ge(F["w2_lo"], j + 1)
                pe.wait_ge(F["h_lo"], 2 * j + 2)
                for t in range(TT):
                    wait(pe, F["yadd"], TT * j + t - 3)
                    mm3(PS[:, 4 + t % 4, :], lambda a, c: hT[:, s, a, t * P:(t + 1) * P],
                        lambda q, c: W2[:, s, q, :], 1).then_inc(F["down"], 1)

            def body(j, s, first):
                gate(j, s, 0)
                gate(j, s, 1)
                if not first:
                    down(j - 1, 1 - s)

            tiles(pe, nt, body)
            down(nt - 1, (nt - 1) % 2)

        A1 = names("a1", "raw_qkv", "raw_wo", "wq_hi", "wq_lo", "wk_hi", "wk_lo", "wv_hi", "wv_lo", "wo_hi", "wo_lo",
                   "tables", "vproj", "v_hi", "v_lo", "vz0", "vz", "stored0", "stored1", "kst", "qst0", "qst1", "mask", "scores", "smask",
                   "pick", "maxed", "negmax", "exp", "rinv", "pnorm", "turned", "pt_hi", "pt_lo", "pv", 
                   "o_hi", "o_lo", "yproj", "yadd")
        R1 = names("r1", "proj", "swap", "cos", "sin", "rot", "hi", "lo")
        NI = 5 * BATCH

        def sp_attn1(sp):
            sp.wait_ge(F0["yadd"], TT * NT0)
            sp.wait_ge(T["fed"], TT * 2 + 1)
            sp.dma_start(raw[:, 0:WO0], attn1_w[:, 0:WO0]).then_inc(A1["raw_qkv"], 16)
            sp.dma_start(raw[:, WO0:WCOLS], attn1_w[:, WO0:WCOLS]).then_inc(A1["raw_wo"], 16)
            sp.dma_start(AF[:, rope1_at:rope1_at + 1024], rope1).then_inc(A1["tables"], 16)
            for r in range(NI):
                b, j = r // 5, r % 5
                sp.wait_ge(R1["lo"], r + 1)
                for s in range(2):
                    sp.dma_start(scr[b, j, s], f32(rq[:, r % 2, s, :])).then_inc(A1[f"stored{r % 2}"], 16)
            sp.wait_ge(A1["v_lo"], TT)
            for s in range(2):
                sp.wait_ge(A1[f"stored{s}"], 16 * NI)
            for n in range(TT):
                b, i = n // QT, n % QT
                if i == 0:
                    if b > 0:
                        sp.wait_ge(A1["scores"], QT * 16)
                    else:
                        sp.dma_start(mask1, consts[:, 384:896]).then_inc(A1["mask"], 16)
                    for a, s in enumerate((0, 1, 0)):
                        src = scr[b, 4, s].rearrange("(c h) t -> c h t", c=HD1)
                        sp.dma_start(f32(kst[a * HD1:(a + 1) * HD1]), src).then_inc(A1["kst"], 16)
                if n >= 2:
                    sp.wait_ge(A1["scores"], 16 * (n - 1))
                for j in range(4):
                    for a, s in enumerate((0, 0, 1)):
                        src = scr[b, j, s].rearrange("(c h) t -> c h t", c=HD1)[:, :, i * P:(i + 1) * P]
                        sp.dma_start(f32(qst[a * HD1:(a + 1) * HD1, n % 2, 8 * j:8 * j + 8]), src)\
                            .then_inc(A1[f"qst{n % 2}"], 16)

        def pe_attn1(pe):
            for r in range(NI):
                b, j = r // 5, r % 5
                if j < 4:
                    pe.wait_ge(A1["wq_lo"], j + 1)
                else:
                    pe.wait_ge(A1["wk_lo"], 1)
                wait(pe, R1["swap"], r - 1)
                wait(pe, R1["cos"], r - 1)
                w = Wq[:, :, j] if j < 4 else Wk
                mm3(PS[:, 6 + r % 2, :], lambda a, c: w[:, a, c, :], lambda m, c: xT[:, m, c, b * SEQ:(b + 1) * SEQ],
                    DC).then_inc(R1["proj"], 1)
            pe.wait_ge(A1["wv_lo"], 1)
            for t in range(TT):
                wait(pe, A1["v_lo"], t - 1)
                mm3(PS[:, 4 + t % 2, 0:P], lambda a, c: xT[:, a, c, t * P:(t + 1) * P], lambda m, c: Wv[:, m, c, :],
                    DC).then_inc(A1["vproj"], 1)
            for n in range(TT):
                b, i = n // QT, n % QT
                nk = i + 1
                for hf in range(2):
                    if hf == 0:
                        pe.wait_ge(A1["kst"], 48 * (b + 1))
                        pe.wait_ge(A1[f"qst{n % 2}"], 16 * 12 * (n // 2 + 1))
                    for pr in range(8):
                        sp_ = n * 16 + hf * 8 + pr
                        wait(pe, A1["smask"], sp_ - 1)
                        for k in range(2):
                            head = hf * 16 + 2 * pr + k
                            last = nc.tensor.matmul(PS[:, 2 * (pr % 2) + k, 0:nk * P], qst[0:48, n % 2, head, :],
                                                    kst[0:48, head // G1, 0:nk * P], start=True, stop=True)
                        last.then_inc(A1["scores"], 1)
                    for q in range(4):
                        kv = hf * 4 + q
                        un = n * 8 + kv
                        pe.wait_ge(A1["pnorm"], un + 1)
                        for kb in range(nk):
                            tn = tcount(n, kv, kb)
                            wait(pe, A1["pt_lo"], tn - 1)
                            for h in range(G1):
                                last = nc.tensor.transpose(PS[:, 4 + tn % 2, h * P:(h + 1) * P],
                                                           P1[:, q % 2, h, kb * P:(kb + 1) * P], ident)
                            last.then_inc(A1["turned"], 1)
                            if kb >= 1:
                                pv1(pe, n, kv, kb - 1, nk)
                        pv1(pe, n, kv, nk - 1, nk)
                pe.wait_ge(A1["o_lo"], n + 1)
                pe.wait_ge(A1["wo_lo"], 1)
                wait(pe, A1["yadd"], n)
                mm3(PS[:, 7, :], lambda a, c: OT1[:, a, c, :], lambda m, c: Wo[:, m, c, :], G1)\
                    .then_inc(A1["yproj"], 1)

        def tcount(n, kv, kb):
            b, i = n // QT, n % QT
            return b * 8 * 10 + 8 * (i * (i + 1) // 2) + kv * (i + 1) + kb

        def pv1(pe, n, kv, kb, nk):
            tn = tcount(n, kv, kb)
            pe.wait_ge(A1["pt_lo"], tn + 1)
            first, fin = kv == 0 and kb == 0, kv == KVH1 - 1 and kb == nk - 1
            if first:
                pe.wait_ge(A1["vz"], 2 * (n // QT + 1))
                wait(pe, A1["o_lo"], n)
            last = mm3(PS[:, 6, :], lambda a, c: Vz[:, a, kb, kv * P:(kv + 1) * P], lambda m, c: PT1[:, tn % 2, m, :],
                       1, more=not fin, first=first)
            last.then_inc(A1["pv"], 1)

        def act_attn1(act):
            for h in range(4):
                split_hi(act, A1, "q", 0, h)
            for k in ("k", "v", "o"):
                split_hi(act, A1, k, 0)
            for r in range(NI):
                src = PS[:, 6 + r % 2, :]
                act.wait_ge(R1["proj"], r + 1)
                wait(act, R1["rot"], r - 1)
                nc.scalar.activation(qs[0:64, r % 2, :], src[64:128, :], ACT.Copy)
                nc.scalar.activation(qs[64:128, r % 2, :], src[0:64, :], ACT.Copy).then_inc(R1["swap"], 1)
                act.wait_ge(R1["rot"], r + 1)
                wait(act, A1[f"stored{r % 2}"], 32 * (r // 2))
                nc.scalar.activation(rq[:, r % 2, 0, :], rot, ACT.Copy).then_inc(R1["hi"], 1)
            for t in range(TT):
                act.wait_ge(A1["vproj"], t + 1)
                nc.scalar.activation(Vc[:, 0, t, :], PS[:, 4 + t % 2, 0:P], ACT.Copy).then_inc(A1["v_hi"], 1)
            for n in range(TT):
                i = n % QT
                nk = i + 1
                for hf in range(2):
                    for q in range(4):
                        kv = hf * 4 + q
                        un = n * 8 + kv
                        act.wait_ge(A1["negmax"], un + 1)
                        if un >= 2:
                            act.wait_ge(A1["turned"], tcount((un - 2) // 8, (un - 2) % 8, (un - 2) // 8 % QT) + 1)
                        for h in range(G1):
                            last = nc.scalar.activation(P1[:, q % 2, h, 0:nk * P], S1[:, 4 * q + h, 0:nk * P], ACT.Exp,
                                                        bias=negmax[:, 4 * q + h:4 * q + h + 1], scale=SCALE1,
                                                        accum_out=rsum[:, 4 * q + h:4 * q + h + 1])
                        last.then_inc(A1["exp"], 1)
                        for kb in range(nk):
                            tn = tcount(n, kv, kb)
                            act.wait_ge(A1["turned"], tn + 1)
                            wait(act, A1["pv"], tn - 1)
                            nc.scalar.activation(PT1[:, tn % 2, 0, :], PS[:, 4 + tn % 2, :], ACT.Copy)\
                                .then_inc(A1["pt_hi"], 1)
                act.wait_ge(A1["pv"], tcount(n, 7, i) + 1)
                wait(act, A1["yproj"], n)
                if n == 0:
                    for s in range(2):
                        act.wait_ge(A1[f"stored{s}"], 16 * NI)
                nc.scalar.activation(OT1[:, 0], PS[:, 6, :].rearrange("p (h k) -> p h k", h=4), ACT.Copy)\
                    .then_inc(A1["o_hi"], 1)

        def pool_attn1(pool):
            for h in range(4):
                split_lo(pool, A1, "q", 0, h)
            for k in ("k", "v", "o"):
                split_lo(pool, A1, k, 0)
            pool.wait_ge(A1["tables"], 16)
            for r in range(NI):
                pool.wait_ge(R1["swap"], r + 1)
                nc.gpsimd.tensor_tensor(qs[:, r % 2, :], qs[:, r % 2, :], stab, ALU.mult).then_inc(R1["sin"], 1)

        def dve_attn1(dve):
            nc.vector.memset(f32(Vz[:, 0]), 0.0)
            nc.vector.memset(f32(Vz[:, 1]), 0.0).then_inc(A1["vz0"], 1)
            dve.wait_ge(A1["tables"], 16)
            for r in range(NI):
                dve.wait_ge(R1["swap"], r + 1)
                wait(dve, R1["rot"], r)
                nc.vector.tensor_tensor(tcos, PS[:, 6 + r % 2, :], ctab, ALU.mult).then_inc(R1["cos"], 1)
                dve.wait_ge(R1["sin"], r + 1)
                dve.wait_ge(R1["cos"], r + 1)
                wait(dve, R1["hi"], r)
                wait(dve, R1["lo"], r)
                nc.vector.tensor_tensor(rot, tcos, qs[:, r % 2, :], ALU.add).then_inc(R1["rot"], 1)
                dve.wait_ge(R1["hi"], r + 1)
                nc.vector.tensor_tensor(rq[:, r % 2, 1, :], rot, f32(rq[:, r % 2, 0, :]), ALU.subtract)\
                    .then_inc(R1["lo"], 1)
            for t in range(TT):
                dve.wait_ge(A1["v_hi"], t + 1)
                nc.vector.tensor_tensor(Vc[:, 1, t, :], PS[:, 4 + t % 2, 0:P], f32(Vc[:, 0, t, :]), ALU.subtract)\
                    .then_inc(A1["v_lo"], 1)
            dve.wait_ge(A1["vz0"], 1)
            dve.wait_ge(A1["v_lo"], TT)
            dve.wait_ge(A1["wo_lo"], 1)
            dve.wait_ge(A1["mask"], 16)
            for n in range(TT):
                b, i = n // QT, n % QT
                nk = i + 1
                W = nk * P
                if i == 0:
                    if b > 0:
                        dve.wait_ge(A1["pv"], tcount(n, 0, 0))
                    for s in range(2):
                        dst = Vz[:, s].rearrange("p j (v c) -> p j v c", c=P + HD1)[:, :, :, 0:HD1]
                        src = f32(Vc[:, s, b * QT:(b + 1) * QT, :]).rearrange("p j (v c) -> p j v c", c=HD1)
                        nc.vector.tensor_copy(dst, src).then_inc(A1["vz"], 1)
                for hf in range(2):
                    for pr in range(8):
                        sn = n * 16 + hf * 8 + pr
                        dve.wait_ge(A1["scores"], sn + 1)
                        if pr % 2 == 0 and (n, hf) != (0, 0):
                            dve.wait_ge(A1["exp"], (2 * n + hf - 1) * 4 + pr // 2 + 1)
                        nc.vector.tensor_tensor(S1[:, 2 * pr:2 * pr + 2, 0:W],
                                                PS[:, 2 * (pr % 2):2 * (pr % 2) + 2, 0:W],
                                                mask1[:, 512 - W:512].unsqueeze(1).to_broadcast([P, 2, W]),
                                                ALU.add).then_inc(A1["smask"], 1)
                    for q in range(4):
                        un = n * 8 + hf * 4 + q
                        sl = S1[:, 4 * q:4 * q + 4, 0:W]
                        dve.wait_ge(A1["smask"], n * 16 + hf * 8 + 2 * q + 2)
                        nc.vector.tensor_reduce(negmax[:, 4 * q:4 * q + 4], sl, AX.X, ALU.max)\
                            .then_inc(A1["maxed"], 1)
                        if i > 0:
                            for h in range(G1):
                                row = S1[:, 4 * q + h, 0:W]
                                wk = work[:, 0:W]
                                c = pick_state
                                for rd in range(TOPK // 8):
                                    nc.vector.max(top8, row if rd == 0 else wk).then_inc(A1["pick"], 1)
                                    c["n"] += 1
                                    dve.wait_ge(A1["pick"], c["n"])
                                    nc.vector.match_replace(wk, top8, row if rd == 0 else wk, TAKEN)\
                                        .then_inc(A1["pick"], 1)
                                    c["n"] += 1
                                    dve.wait_ge(A1["pick"], c["n"])
                                nc.vector.tensor_scalar(wk, wk, TAKEN, DROPPED, ALU.not_equal, ALU.mult)\
                                    .then_inc(A1["pick"], 1)
                                c["n"] += 1
                                dve.wait_ge(A1["pick"], c["n"])
                                nc.vector.tensor_tensor(row, row, wk, ALU.add).then_inc(A1["pick"], 1)
                                c["n"] += 1
                            dve.wait_ge(A1["pick"], c["n"])
                        dve.wait_ge(A1["maxed"], un + 1)
                        nc.vector.tensor_scalar(negmax[:, 4 * q:4 * q + 4], negmax[:, 4 * q:4 * q + 4], -SCALE1, None,
                                                ALU.mult).then_inc(A1["negmax"], 1)
                        dve.wait_ge(A1["exp"], un + 1)
                        nc.vector.reciprocal(rinv[:, 4 * q:4 * q + 4], rsum[:, 4 * q:4 * q + 4])\
                            .then_inc(A1["rinv"], 1)
                        dve.wait_ge(A1["rinv"], un + 1)
                        for h in range(G1):
                            last = nc.vector.tensor_scalar(P1[:, q % 2, h, 0:W], P1[:, q % 2, h, 0:W],
                                                           rinv[:, 4 * q + h:4 * q + h + 1], None, ALU.mult)
                        last.then_inc(A1["pnorm"], 1)
                        for kb in range(nk):
                            tn = tcount(n, hf * 4 + q, kb)
                            dve.wait_ge(A1["pt_hi"], tn + 1)
                            nc.vector.tensor_tensor(PT1[:, tn % 2, 1, :], PS[:, 4 + tn % 2, :],
                                                    f32(PT1[:, tn % 2, 0, :]), ALU.subtract).then_inc(A1["pt_lo"], 1)
                dve.wait_ge(A1["o_hi"], n + 1)
                nc.vector.tensor_tensor(OT1[:, 1], PS[:, 6, :].rearrange("p (h k) -> p h k", h=4), f32(OT1[:, 0]),
                                        ALU.subtract).then_inc(A1["o_lo"], 1)
                dve.wait_ge(A1["yproj"], n + 1)
                nc.vector.tensor_tensor(y[:, n, :], PS[:, 7, :], y[:, n, :], ALU.add).then_inc(A1["yadd"], 1)

        pick_state = {"n": 0}
        CONST_DMAS = 3

        block = ctx.enter_context(nc.Block())

        @block.sync
        def _(sp):
            for t in range(TT):
                sp.dma_start(y[:, t, :], x[t * P:(t + 1) * P, :]).then_inc(s_x, 16)
            sp.dma_start(ident, consts[:, 0:128]).then_inc(s_const, 16)
            sp.dma_start(mask0, consts[:, 128:384]).then_inc(s_const, 16)
            sp.dma_start(AF[:, base + WCOLS:base + WCOLS + 1024], rope0).then_inc(s_const, 16)
            sp_attn0(sp)

            def free0(sp):
                sp.wait_ge(A0["mean_abs"], 6 * KVH0)
                sp.wait_ge(A0["yadd"], NU * KVH0)
            if stop_after >= 2:
                sp_ffn(sp, F0, NT0, ffn0_w, True, free0)
            if stop_after >= 3:
                sp_attn1(sp)

            def free1(sp):
                sp.wait_ge(A1["yadd"], TT)
                sp.dma_start(adrow, ad_rows).then_inc(F1["ad"], 16)
            if stop_after >= 4:
                sp_ffn(sp, F1, NT1, ffn1_w, False, free1)
            for t in range(TT):
                sp.wait_ge(T["fed"], TT * min(stop_after, 4) + t + 1)
                sp.dma_start(out[t * P:(t + 1) * P, :], y[:, t, :]).then_inc(s_out, 16)
            sp.wait_ge(s_out, 16 * TT)

        @block.tensor
        def _(pe):
            pe.wait_ge(s_const, 16 * CONST_DMAS)
            turn_pe(pe, 0)
            pe.wait_ge(s_ready, 1)
            pe_attn0(pe)
            turn_pe(pe, 1)
            if stop_after >= 2:
                pe_ffn(pe, F0, NT0)
                turn_pe(pe, 2)
            if stop_after >= 3:
                pe_attn1(pe)
                turn_pe(pe, 3)
            if stop_after >= 4:
                pe_ffn(pe, F1, NT1)

        @block.scalar
        def _(act):
            turn_act(act, 0)
            act_attn0(act)
            norm_act(act, 1)
            turn_act(act, 1)
            if stop_after >= 2:
                act_ffn(act, F0, NT0, True)
                norm_act(act, 2)
                turn_act(act, 2)
            if stop_after >= 3:
                act_attn1(act)
                norm_act(act, 3)
                turn_act(act, 3)
            if stop_after >= 4:
                act.wait_ge(F1["ad"], 16)
                act_ffn(act, F1, NT1, False)
                norm_act(act, 4)

        @block.gpsimd
        def _(pool):
            pool_attn0(pool)
            if stop_after >= 2:
                pool_ffn(pool, F0, NT0, True)
            if stop_after >= 3:
                pool_attn1(pool)
            if stop_after >= 4:
                pool.wait_ge(F1["ad"], 16)
                pool_ffn(pool, F1, NT1, False)

        @block.vector
        def _(dve):
            nc.vector.memset(ones, 1.0).then_inc(s_ready, 1)
            for t in range(TT):
                dve.wait_ge(s_x, 16 * TT)
                nc.vector.tensor_copy(nwt[:, 0:1], y[:, t, 0:1]).then_inc(T["fed"], 1)
                dve.wait_ge(T["fed"], t + 1)
            for t in range(TT):
                turn_dve(dve, 0, t)
            dve_attn0(dve)

            norm_dve(dve, 1, A0["yadd"], NU * KVH0)
            if stop_after >= 2:
                dve_ffn(dve, F0, NT0, True)

                norm_dve(dve, 2, F0["yadd"], TT * NT0)
            if stop_after >= 3:
                dve_attn1(dve)

                norm_dve(dve, 3, A1["yadd"], TT)
            if stop_after >= 4:
                dve.wait_ge(F1["ad"], 16)
                dve_ffn(dve, F1, NT1, False)

                norm_dve(dve, 4, F1["yadd"], TT * NT1, turns=False)


def _constants():
    i = np.arange(P)
    ident = np.eye(P, dtype=np.float32)
    neg = np.float32(NEG)
    prev = np.where(i[None, :] > i[:, None], np.float32(0), neg)
    diag = np.where(i[None, :] <= i[:, None], np.float32(0), neg)
    consts = np.concatenate([ident, prev, diag, np.zeros((P, 384), np.float32),
                             np.maximum(diag, np.float32(DROPPED))], axis=1).astype(np.float32)

    def table(inv_freq, freq_of_row):
        ang = np.arange(SEQ, dtype=np.float32)[None, :] * inv_freq[freq_of_row][:, None]
        sign = np.where(np.arange(P) < 64, np.float32(-1), np.float32(1))[:, None]
        return np.concatenate([np.cos(ang), np.sin(ang) * sign], axis=1).astype(np.float32)

    half0 = HD0 // 2
    f0 = (np.float32(10000.0) ** (-np.arange(half0, dtype=np.float32) / np.float32(half0))).astype(np.float32)
    f1 = (np.float32(1.0) / np.float32(10000.0) ** (np.arange(0, HD1, 2, dtype=np.float32) / np.float32(HD1)))
    rope0 = table(f0, np.arange(P) % half0)
    rope1 = table(f1.astype(np.float32), (np.arange(P) % 64) // 8)
    return consts, rope0, rope1


def _chunks(w):
    n = w.shape[1] // P
    return w.reshape(DC, P, n, P).transpose(2, 1, 0, 3)


def _layout(i):
    wq, wk, wv = (_chunks(np.asarray(i[k])) for k in ("L0_attn_wq", "L0_attn_wk", "L0_attn_wv"))
    wo = np.asarray(i["L0_attn_wo"]).reshape(KVH0, G0, P, D).transpose(0, 2, 1, 3).reshape(KVH0, P, G0 * D)
    wq = wq.reshape(KVH0, G0, P, DC * P).transpose(0, 2, 1, 3).reshape(KVH0, P, G0 * DC * P)
    attn0 = np.concatenate([wq, wk.reshape(KVH0, P, -1), wv.reshape(KVH0, P, -1), wo], axis=2)

    def ffn(w1, w3, w2, nt):
        pad = nt * P - w1.shape[0]
        w1, w3 = (np.pad(w, ((0, pad), (0, 0))) for w in (w1, w3))
        w2 = np.pad(w2, ((0, 0), (0, pad)))
        g, u = (_chunks(w.T).reshape(nt, P, D) for w in (w1, w3))
        return np.concatenate([g, u, w2.T.reshape(nt, P, D)], axis=2)

    a = lambda n: np.asarray(i[n])
    ffn0 = np.stack([ffn(a("L0_ffn_w1"), a("L0_ffn_w3"), a("L0_ffn_w2"), NT0),
                     ffn(a("L0_ffn_mean_w1"), a("L0_ffn_mean_w3"), a("L0_ffn_mean_w2"), NT0)], axis=2).reshape(NT0, P, 2 * FCOLS)
    ffn1 = ffn(a("L1_ffn_Wg"), a("L1_ffn_Wu"), a("L1_ffn_Wd"), NT1)
    pairs = [np.stack([a(f"L0_ffn_{w}").reshape(KVH0, 2, P, MCH), a(f"L0_ffn_mean_{w}").reshape(KVH0, 2, P, MCH)], axis=3)
             for w in ("w1", "w3", "w2")]
    mean = np.stack(pairs, axis=1).reshape(KVH0 * 6, P, 2, MCH)

    def heads_last(w, n):
        return w.reshape(n // 8, 8, HD1, D).transpose(0, 2, 1, 3).reshape(n // 8 * P, D)
    q1 = _chunks(heads_last(a("L1_attn_Wq"), 32).T).transpose(1, 0, 2, 3).reshape(P, 4 * D)
    k1 = _chunks(heads_last(a("L1_attn_Wk"), 8).T).transpose(1, 0, 2, 3).reshape(P, D)
    v1 = _chunks(a("L1_attn_Wv").T).transpose(1, 0, 2, 3).reshape(P, D)
    o1 = a("L1_attn_Wo").T.reshape(KVH1, G1, HD1, D).transpose(0, 2, 1, 3).reshape(P, G1 * D)
    attn1 = np.concatenate([q1, k1, v1, o1], axis=1)

    pad = NT1 * P - INT1
    scales = [np.pad(a(n), (0, pad)).reshape(NT1, P, 1) for n in ("L1_ffn_ag", "L1_ffn_au")]
    ffn1 = np.concatenate([ffn1] + scales, axis=2)
    rows = np.broadcast_to(a("L1_ffn_ad")[None, :], (P, D))
    consts, rope0, rope1 = _constants()
    return {"x": a("L0_attn_x").reshape(TOK, D), "attn0_w": attn0, "ffn0_w": ffn0, "mean_w": mean, "attn1_w": attn1,
            "ffn1_w": ffn1, "ad_rows": rows, "consts": consts, "rope0": rope0, "rope1": rope1}


STOP = 99


def kernel(**inputs):
    import concourse.bacc as _bacc
    from concourse.bass_utils import run_bass_kernel_spmd as _run

    nc = _bacc.Bacc("TRN2", target_bir_lowering=False, num_devices=1)
    arrays, args = {}, []
    for name, a in _layout(inputs).items():
        a = np.ascontiguousarray(a)
        arrays[f"in_{name}"] = a
        args.append(nc.dram_tensor(f"in_{name}", a.shape, mybir.dt.from_np(a.dtype), kind="ExternalInput").ap())
    args.append(nc.dram_tensor("out_0", (TOK, D), F32, kind="ExternalOutput").ap())
    build_kernel(nc, *args, stop_after=STOP)
    r = _run(nc, [arrays], core_ids=[0])
    return r.results[0]["out_0"].reshape(BATCH, SEQ, D)
```

```python
from contextlib import ExitStack

import math

import numpy as np
import concourse.bass as bass
from concourse import mybir

F32 = mybir.dt.float32
F32R = mybir.dt.float32r
ALU = mybir.AluOpType
ACT = mybir.ActivationFunctionType
AX = mybir.AxisListType

P = 128
D = 512
DC = D // P
BATCH, SEQ = 2, 512
TOK = BATCH * SEQ
TT = TOK // P
QT = SEQ // P
KVH0, G0, HD0 = 8, 4, 128
SCALE0 = float(HD0) ** -0.5
WQ0, WK0, WV0, WO0 = 0, 2048, 2560, 3072
WCOLS = 5120
KVH1, G1, HD1 = 8, 4, 16
SCALE1 = 0.25
TOPK = 128
RESOLVED = P * 16
WINDOW = 15
AIM = TOPK - (WINDOW + 1) // 2
ROUNDS = 4
INT0, INT1 = 1792, 1376
NT0 = INT0 // P
NT1 = -(-INT1 // P)
FCOLS = 3 * D
MCH = 448
NEG = -3.4028234663852886e38
DROPPED = -1.6e38
TAKEN = -3.0e38
EPS = 1e-5
MAGIC_PASSES = ((0, 0), (0, 1), (1, 0))


def build_kernel(nc, x, attn0_w, ffn0_w, mean_w, attn1_w, ffn1_w, ad_rows, quant, consts, rope0, rope1, out,
                 stop_after=99):
    ctx = ExitStack()
    with ctx:
        def sem(name):
            return ctx.enter_context(nc.semaphore(name))

        XT = ctx.enter_context(nc.sbuf_tensor("XT", [P, 8192], F32R))
        AF = ctx.enter_context(nc.sbuf_tensor("AF", [P, 19300], F32))
        with nc.sbuf_tensor("AR", [P, 25600], F32R) as AR:
            pass
        AR1 = ctx.enter_context(nc.sbuf_tensor("AR1", [P, 10240], F32R))
        BF = ctx.enter_context(nc.sbuf_tensor("BF", [P, 15360], F32))
        PS = ctx.enter_context(nc.psum_tensor("PS", [P, 8, 512], F32))
        scr = nc.dram_tensor("rope_scratch", (BATCH, 5, 2, P, SEQ), F32, kind="Internal").ap()

        def f32(view):
            return view.bitcast(F32)

        y = AF[:, 0:4096].rearrange("p (t d) -> p t d", t=TT)
        ident = AF[:, 4096:4224]
        eps = AF[:, 4224:4225]
        zeros = AF[:, 4225:4226]
        sums = AF[:, 4228:4231]
        coeff = AF[:, 4232:4235]
        part = AF[:, 4236:4242]
        stats = AF[:, 4244:4244 + 48].rearrange("p (t s) -> p t s", t=TT)
        mv = AF[:, 4292:4308].rearrange("p (t s) -> p t s", t=TT)
        var = AF[:, 4308:4316]
        sd = AF[:, 4316:4324]
        rstd = AF[:, 4324:4332]
        nwt = AF[:, 4332:4340]
        negmax = AF[:, 4340:4356]
        rsum = AF[:, 4356:4372]
        rinv = AF[:, 4372:4388]
        top8 = AF[:, 4388:4396]
        ones = AF[:, 4396:4524]
        base = 4608
        raw = AF[:, base:base + WCOLS]
        o = base + WCOLS
        ctab, stab = AF[:, o:o + 512], AF[:, o + 512:o + 1024]
        mask0 = AF[:, o + 1024:o + 1280]
        o += 1280
        Sm = AF[:, o:o + 2048].rearrange("p (r h k) -> p r h k", r=2, h=4)
        o += 2048
        qs = AF[:, o:o + 1024].rearrange("p (r k) -> p r k", r=2)
        tcos, rot = AF[:, o + 1024:o + 1536], AF[:, o + 1536:o + 2048]
        vtmp = AF[:, o + 2048:o + 2560]
        mch = AF[:, o + 2560:o + 2560 + 4 * MCH].rearrange("p (r w k) -> p r w k", r=2, w=2)
        assert o + 2560 + 4 * MCH <= 19300
        raww = AF[:, base:base + 4 * FCOLS].rearrange("p (r w k) -> p r w k", r=2, w=2)
        raww_flat = AF[:, base:base + 4 * FCOLS].rearrange("p (r k) -> p r k", r=2)
        scale_g, scale_u = raww[:, :, 1, 0:1], raww[:, :, 1, 1:2]
        o = base + 4 * FCOLS
        sg = AF[:, o:o + 1024].rearrange("p (b k) -> p b k", b=2)
        hh = AF[:, o + 1024:o + 2048].rearrange("p (b k) -> p b k", b=2)
        adrow = AF[:, o + 2048:o + 2560]
        rope1_at = base + WCOLS
        xT = XT[:, 0:8192].rearrange("p (s c k) -> p s c k", s=2, c=DC)
        Wq = AR[:, 0:4096].rearrange("p (s h c k) -> p s h c k", s=2, h=4, c=DC)
        Wk = AR[:, 4096:5120].rearrange("p (s c k) -> p s c k", s=2, c=DC)
        Wv = AR[:, 5120:6144].rearrange("p (s c k) -> p s c k", s=2, c=DC)
        Wo = AR[:, 6144:10240].rearrange("p (s h k) -> p s h k", s=2, h=4)
        qT = AR[:, 10240:18432].rearrange("p (r s h k) -> p r s h k", r=2, s=2, h=4)
        kT = AR[:, 18432:20480].rearrange("p (r s k) -> p r s k", r=2, s=2)
        V = AR[:, 20480:22528].rearrange("p (r s j k) -> p r s j k", r=2, s=2, j=QT)
        PT = AR[:, 22528:24576].rearrange("p (s j k) -> p s j k", s=2, j=2)
        OT = AR[:, 24576:25600].rearrange("p (s h k) -> p s h k", s=2, h=4)
        W13 = AR[:, 0:4096].rearrange("p (r s m c k) -> p r s m c k", r=2, s=2, m=2, c=DC)
        W2 = AR[:, 4096:6144].rearrange("p (r s k) -> p r s k", r=2, s=2)
        hT = AR[:, 6144:10240].rearrange("p (r s k) -> p r s k", r=2, s=2)
        W1 = {"q": AR1[:, 0:4096].rearrange("p (s h c k) -> p s h c k", s=2, h=4, c=DC),
              "k": AR1[:, 4096:5120].rearrange("p (s c k) -> p s c k", s=2, c=DC),
              "v": AR1[:, 5120:6144].rearrange("p (s c k) -> p s c k", s=2, c=DC),
              "o": AR1[:, 6144:10240].rearrange("p (s h k) -> p s h k", s=2, h=4)}
        qst = XT[:, 0:8192].rearrange("p (r h k) -> p r h k", r=2, h=32)
        kst = AR1[:, 0:4096].rearrange("p (h k) -> p h k", h=KVH1)
        OT1 = AR1[:, 4096:5120].rearrange("p (s h k) -> p s h k", s=2, h=4)
        ident_r, mask_r = AR1[:, 5120:5248], AR1[:, 5248:5376]
        S1 = [AF[:, base:base + 8192].rearrange("p (h k) -> p h k", h=16),
              BF[:, 0:8192].rearrange("p (h k) -> p h k", h=16)]
        rq = BF[:, 0:2048].bitcast(F32R).rearrange("p (r s k) -> p r s k", r=2, s=2)
        Vz = BF[:, 8192:12800].rearrange("p (j k) -> p j k", j=QT)
        X1 = BF[:, 12800:13824].rearrange("p (r k) -> p r k", r=2)
        o = base + 8192
        P1 = AF[:, o:o + 4096].rearrange("p (r h k) -> p r h k", r=2, h=4)
        PT1 = AF[:, o + 4096:o + 5120].rearrange("p (r k) -> p r k", r=2)
        Vc = AF[:, o + 5120:o + 6144].rearrange("p (t k) -> p t k", t=TT)
        assert o + 6144 <= 19300
        small = BF[:, 13824:15360]
        names16 = ("slope", "tl", "th", "al", "ah", "bad", "diff", "over", "under", "step", "tmp")
        st = {n: small[:, 16 * k:16 * k + 16] for k, n in enumerate(names16)}
        st.update(msum=st["tl"], mdiff=st["al"], vsum=st["ah"], recip=st["th"], spread=st["over"])
        o = 16 * len(names16)
        for n in ("thr", "nthr", "acc", "rmax", "nmax", "tau"):
            st[n] = small[:, o:o + 32].rearrange("p (r h) -> p r h", r=2)
            o += 32
        stat6 = small[:, o:o + 96].rearrange("p (h s) -> p h s", h=16)
        ztab = small[:, o + 96:o + 102]
        iota16 = small[:, o + 104:o + 120]
        best = small[:, o + 128:o + 384].rearrange("p (h s) -> p h s", h=16)
        hit = small[:, o + 384:o + 640].rearrange("p (h s) -> p h s", h=16)
        val = small[:, o + 640:o + 896].rearrange("p (h s) -> p h s", h=16)
        flag_row = small[:, o + 896:o + 897]
        flag_int = small[0:1, o + 897:o + 898].bitcast(mybir.dt.int32)
        assert o + 898 <= 1280
        junk = [AF[:, base + 14336:base + 14592].bitcast(mybir.dt.bfloat16), small[:, 1280:1536].bitcast(mybir.dt.bfloat16)]
        rsum1, rinv1 = AF[:, 4528:4544], AF[:, 4544:4560]

        s_const = sem("s_const")
        s_ready = sem("s_ready")
        s_x = sem("s_x")
        s_out = sem("s_out")

        def wait(eng, s, v):
            if isinstance(v, int) and v <= 0:
                return
            eng.wait_ge(s, v)

        def mm3(dst, lhs, rhs, n, flags=True, more=False, first=True):
            k = 0
            last = None
            for c in range(n):
                for a, m in MAGIC_PASSES:
                    last = nc.tensor.matmul(dst, lhs(a, c), rhs(m, c), start=(first and k == 0),
                                            stop=(k == 3 * n - 1 and not more))
                    k += 1
            return last

        def names(tag, *ns):
            return {n: sem(f"{tag}_{n}") for n in ns}

        def turn_pe(pe, k):
            for t in range(TT):
                pe.wait_ge(T["fed"], TT * k + t + 1)
                wait(pe, T["low"], TT * k + t - 1 if t >= 2 else TT * k)
                for c in range(DC):
                    last = nc.tensor.transpose(PS[:, t % 2, c * P:(c + 1) * P], y[:, t, c * P:(c + 1) * P], ident)
                last.then_inc(T["turned"], 1)
            pe.wait_ge(T["low"], TT * (k + 1))

        def turn_act(act, k):
            for t in range(TT):
                act.wait_ge(T["turned"], TT * k + t + 1)
                nc.scalar.activation(xT[:, 0, :, t * P:(t + 1) * P],
                                     PS[:, t % 2, :].rearrange("p (c k) -> p c k", c=DC),
                                     ACT.Copy).then_inc(T["high"], 1)

        def turn_dve(dve, k, t):
            dve.wait_ge(T["high"], TT * k + t + 1)
            nc.vector.tensor_tensor(xT[:, 1, :, t * P:(t + 1) * P],
                                    PS[:, t % 2, :].rearrange("p (c k) -> p c k", c=DC),
                                    f32(xT[:, 0, :, t * P:(t + 1) * P]), ALU.subtract).then_inc(T["low"], 1)

        def norm_dve(dve, k, sem_added, n_added, turns=True):
            a, v = TT * (k - 1), 6 * (k - 1)
            dve.wait_ge(sem_added, n_added)
            for t in range(TT):
                nc.vector.bn_stats(stats[:, t, :], y[:, t, :]).then_inc(N["stats"], 1)
            for t in range(TT):
                dve.wait_ge(N["stats"], a + t + 1)
                nc.vector.bn_aggr(mv[:, t, :], stats[:, t, :]).then_inc(N["aggr"], 1)
            dve.wait_ge(N["aggr"], a + TT)
            nc.vector.tensor_scalar(var, mv[:, :, 1], EPS, None, ALU.add).then_inc(N["var"], 1)
            dve.wait_ge(N["sqrt"], k)
            nc.vector.reciprocal(rstd, sd).then_inc(N["var"], 1)
            dve.wait_ge(N["var"], v + 2)
            nc.vector.tensor_tensor(nwt, rstd, rstd, ALU.mult).then_inc(N["var"], 1)
            dve.wait_ge(N["var"], v + 3)
            nc.vector.tensor_tensor(nwt, nwt, var, ALU.mult).then_inc(N["var"], 1)
            dve.wait_ge(N["var"], v + 4)
            nc.vector.tensor_scalar(nwt, nwt, -0.5, 1.5, ALU.mult, ALU.add).then_inc(N["var"], 1)
            dve.wait_ge(N["var"], v + 5)
            nc.vector.tensor_tensor(rstd, rstd, nwt, ALU.mult).then_inc(N["var"], 1)
            dve.wait_ge(N["var"], v + 6)
            for t in range(TT):
                nc.vector.tensor_scalar(y[:, t, :], y[:, t, :], mv[:, t, 0:1], rstd[:, t:t + 1],
                                        ALU.subtract, ALU.mult).then_inc(T["fed"], 1)
                if t >= 1 and turns:
                    turn_dve(dve, k, t - 1)
            if turns:
                turn_dve(dve, k, TT - 1)

        def norm_act(act, k):
            act.wait_ge(N["var"], 6 * (k - 1) + 1)
            nc.scalar.activation(sd, var, ACT.Sqrt).then_inc(N["sqrt"], 1)

        T = names("turn", "fed", "turned", "high", "low")
        N = names("norm", "stats", "aggr", "var", "sqrt")

        A0 = names("a0", "raw_qkv", "raw_wo", "wq_hi", "wq_lo", "wk_hi", "wk_lo", "wv_hi", "wv_lo", "wo_hi", "wo_lo",
                   "scores", "masked", "maxed", "negmax", "exp", "rinv", "pnorm", "turned", "pt_hi", "pt_lo", "pv",
                   "o_hi", "o_lo", "yproj", "yadd", "vproj", "vcopy", "vturned", "v_hi", "v_lo",
                   "mean_in0", "mean_in1", "mean_d", "mean_abs", "mean_sum", "coeff_ps", "coeff")
        R0 = names("r0", "proj", "swap", "cos", "sin", "rot", "hi", "lo")
        NU = BATCH * QT

        def head_item(h):
            return 0 if h == 0 else h + 1

        def w_piece(kind, h, layer1=False):
            if layer1:
                src, dst = w_piece(kind, h)
                return src, W1["q"][:, :, h] if kind == "q" else W1[kind]
            if kind == "q":
                return raw[:, WQ0 + h * 512:WQ0 + (h + 1) * 512].rearrange("p (c k) -> p c k", c=DC), Wq[:, :, h]
            if kind == "k":
                return raw[:, WK0:WK0 + 512].rearrange("p (c k) -> p c k", c=DC), Wk
            if kind == "v":
                return raw[:, WV0:WV0 + 512].rearrange("p (c k) -> p c k", c=DC), Wv
            return raw[:, WO0:WO0 + 2048].rearrange("p (h k) -> p h k", h=4), Wo

        def split_hi(act, A, kind, g, h=0):
            src, dst = w_piece(kind, h, A is not A0)
            wait(act, A["raw_wo"] if kind == "o" else A["raw_qkv"], 16 * (g + 1))
            if A is A0:
                if kind == "q":
                    wait(act, R0["proj"], 10 * g - 5 + head_item(h) + 1)
                elif kind == "k":
                    wait(act, R0["proj"], 10 * g - 5 + 1 + 1)
                elif kind == "v":
                    wait(act, A0["vproj"], 2 * g)
                else:
                    wait(act, A0["yproj"], NU * g)
            nc.scalar.activation(dst[:, 0], src, ACT.Copy).then_inc(A[f"w{kind}_hi"], 1)

        def split_lo(pool, A, kind, g, h=0):
            src, dst = w_piece(kind, h, A is not A0)
            pool.wait_ge(A[f"w{kind}_hi"], (4 * g + h if kind == "q" else g) + 1)
            nc.gpsimd.tensor_tensor(dst[:, 1], src, f32(dst[:, 0]), ALU.subtract).then_inc(A[f"w{kind}_lo"], 1)

        PIECES = {0: [("o", 0, 0)], 1: [("q", 0, 1), ("k", 0, 1)], 2: [("q", 1, 1), ("v", 0, 1)],
                  3: [("q", 2, 1)], 4: [("q", 3, 1)]}

        def groups(eng, body):
            body(0, True, False)
            with eng.Fori(1, KVH0 - 1) as g:
                body(g, False, False)
            body(KVH0 - 1, False, True)

        def items0(bb, j):
            its = [(5 * bb + head_item(j), "q", j)]
            if j == 0:
                its.append((5 * bb + 1, "k", 0))
            return its

        def rope_act1(act, r, src, slot):
            act.wait_ge(R0["proj"], r + 1)
            wait(act, R0["rot"], r - 1)
            nc.scalar.activation(qs[0:64, slot, :], src[64:128, :], ACT.Copy)
            nc.scalar.activation(qs[64:128, slot, :], src[0:64, :], ACT.Copy).then_inc(R0["swap"], 1)

        def slot_of(k, b, j):
            return (5 * b + (1 if k == "k" else head_item(j))) % 2

        def src0(k):
            return PS[:, 6, :] if k == "q" else PS[:, 7, :]

        def dst0(k, b, j, s):
            return qT[:, b, s, j, :] if k == "q" else kT[:, b, s, :]

        def pe_proj_item(pe, g, bb, b, k, j, r):
            if k == "q":
                pe.wait_ge(A0["wq_lo"], 4 * g + j + 1)
                if j == 0:
                    wait(pe, R0["swap"], r)
                    wait(pe, R0["cos"], r)
                elif j == 1:
                    wait(pe, R0["swap"], r - 1)
                    wait(pe, R0["cos"], r - 1)
                else:
                    wait(pe, R0["swap"], r)
                    wait(pe, R0["cos"], r)
            else:
                pe.wait_ge(A0["wk_lo"], g + 1)
                wait(pe, A0["v_lo"], bb)
            w = Wq[:, :, j] if k == "q" else Wk
            mm3(src0(k), lambda a, c: w[:, a, c, :], lambda m, c: xT[:, m, c, b * SEQ:(b + 1) * SEQ], DC)\
                .then_inc(R0["proj"], 1)

        def pe_v(pe, g, bb, b, r):
            pe.wait_ge(A0["wv_lo"], g + 1)
            pe.wait_ge(R0["swap"], 5 * bb + 2)
            pe.wait_ge(R0["cos"], 5 * bb + 2)
            mm3(PS[:, 7, :], lambda a, c: Wv[:, a, c, :], lambda m, c: xT[:, m, c, b * SEQ:(b + 1) * SEQ], DC)\
                .then_inc(A0["vproj"], 1)

        def pe_vturn(pe, bb):
            pe.wait_ge(A0["vcopy"], bb + 1)
            for j in range(QT):
                last = nc.tensor.transpose(PS[:, 7, j * P:(j + 1) * P], vtmp[:, j * P:(j + 1) * P], ident)
            last.then_inc(A0["vturned"], 1)

        def pe_attn0(pe):
            def body(g, first, last_group):
                for u in range(NU):
                    b, i = u // QT, u % QT
                    n = NU * g + u
                    bb = 2 * g + b
                    pe.wait_ge(R0["lo"], 5 * bb + 5)
                    wait(pe, A0["masked"], n)
                    lo = 1 if i == 0 else 0
                    for h in range(G0):
                        dst = PS[:, h // 2, (h % 2) * 256 + lo * P:(h % 2) * 256 + 256]
                        last = mm3(dst, lambda a, c: qT[:, b, a, h, i * P:(i + 1) * P],
                                   lambda m, c: kT[:, b, m, (i - 1 + lo) * P:(i + 1) * P], 1)
                    last.then_inc(A0["scores"], 1)
                    if not (first and u == 0):
                        turn_p(n - 1, (u - 1) % QT)
                    nb, j = (b + 1) % 2, i
                    ng = g if b == 0 else g + 1
                    has_next = not (last_group and b == 1)
                    if has_next:
                        pe_proj_item(pe, ng, bb + 1, nb, "q", j, 5 * (bb + 1) + head_item(j))
                    if not (first and u == 0):
                        pv(n - 1, (u - 1) % QT, ((u - 1) // QT) % 2)
                    if has_next:
                        if j == 0:
                            pe_proj_item(pe, ng, bb + 1, nb, "k", 0, 5 * (bb + 1) + 1)
                        if j == 1:
                            pe_v(pe, ng, bb + 1, nb, 0)
                        if j == 2:
                            pe_vturn(pe, bb + 1)
                    if not (first and u == 0):
                        oproj(n - 1, g if u > 0 else g - 1)

            def turn_p(n, i):
                pe.wait_ge(A0["pnorm"], n + 1)
                for kb in range(1 if i == 0 else 0, 2):
                    for h in range(G0):
                        last = nc.tensor.transpose(PS[:, 2 + kb, h * P:(h + 1) * P],
                                                   Sm[:, par2(i), h, kb * P:(kb + 1) * P], ident)
                last.then_inc(A0["turned"], 1)

            def par2(i):
                return i % 2

            def pv(n, i, b):
                pe.wait_ge(A0["pt_lo"], n + 1)
                wait(pe, A0["o_lo"], n)
                k0 = 1 if i == 0 else 0
                mm3(PS[:, 4, :], lambda a, c: V[:, b, a, i - 1 + k0 + c, :], lambda m, c: PT[:, m, k0 + c, :],
                    2 - k0).then_inc(A0["pv"], 1)

            def oproj(n, g):
                pe.wait_ge(A0["wo_lo"], g + 1)
                pe.wait_ge(A0["o_lo"], n + 1)
                wait(pe, A0["yadd"], n)
                mm3(PS[:, 5, :], lambda a, c: OT[:, a, c, :], lambda m, c: Wo[:, m, c, :], G0)\
                    .then_inc(A0["yproj"], 1)

            for j in range(G0):
                pe_proj_item(pe, 0, 0, 0, "q", j, head_item(j))
                if j == 0:
                    pe_proj_item(pe, 0, 0, 0, "k", 0, 1)
                if j == 1:
                    pe_v(pe, 0, 0, 0, 0)
                if j == 2:
                    pe_vturn(pe, 0)
            pe.wait_ge(A0["v_lo"], 1)
            groups(pe, body)
            n = NU * KVH0
            turn_p(n - 1, QT - 1)
            pv(n - 1, QT - 1, 1)
            oproj(n - 1, KVH0 - 1)
            pe.wait_ge(A0["mean_sum"], 6 * KVH0 + 1)
            nc.tensor.matmul(PS[:, 6, 0:3], ones, sums, start=True, stop=True).then_inc(A0["coeff_ps"], 1)

        def act_attn0(act):
            def rope_hi(r, k, b, j):
                act.wait_ge(R0["rot"], r + 1)
                nc.scalar.activation(dst0(k, b, j, 0), rot, ACT.Copy).then_inc(R0["hi"], 1)

            def vcopy(bb):
                act.wait_ge(A0["vproj"], bb + 1)
                nc.scalar.activation(vtmp, PS[:, 7, :], ACT.Copy).then_inc(A0["vcopy"], 1)

            def v_hi(bb, b):
                act.wait_ge(A0["vturned"], bb + 1)
                nc.scalar.activation(V[:, b, 0], PS[:, 7, :].rearrange("p (j k) -> p j k", j=QT), ACT.Copy)\
                    .then_inc(A0["v_hi"], 1)

            def pt_hi(n, i):
                act.wait_ge(A0["turned"], n + 1)
                k0 = 1 if i == 0 else 0
                nc.scalar.activation(PT[:, 0, k0:2, :], PS[:, 2 + k0:4, :], ACT.Copy).then_inc(A0["pt_hi"], 1)

            def o_hi(n):
                act.wait_ge(A0["pv"], n + 1)
                nc.scalar.activation(OT[:, 0], PS[:, 4, :].rearrange("p (h k) -> p h k", h=4), ACT.Copy)\
                    .then_inc(A0["o_hi"], 1)

            def mean_abs(g, s):
                act.wait_ge(A0["mean_d"], 6 * g + s + 1)
                wait(act, A0["mean_sum"], 6 * (g - 1) + s + 1 + 1)
                nc.scalar.activation(mch[:, s % 2, 0, :], mch[:, s % 2, 0, :], ACT.Abs,
                                     accum_out=part[:, s:s + 1]).then_inc(A0["mean_abs"], 1)

            for h in range(G0):
                split_hi(act, A0, "q", 0, h)
            for k in ("k", "v", "o"):
                split_hi(act, A0, k, 0)
            for j in range(G0):
                for r, k, h in items0(0, j):
                    rope_act1(act, r, src0(k), slot_of(k, 0, j))
                    rope_hi(r, k, 0, j)
                if j == 1:
                    vcopy(0)
                if j == 2:
                    v_hi(0, 0)

            def body(g, first, last_group):
                for u in range(NU):
                    b, i = u // QT, u % QT
                    n = NU * g + u
                    bb = 2 * g + b
                    nb, j = (b + 1) % 2, i
                    has_next = not (last_group and b == 1)
                    if not (first and u == 0):
                        pt_hi(n - 1, (u - 1) % QT)
                    its = items0(bb + 1, j) if has_next else []
                    if its:
                        rope_act1(act, its[0][0], src0("q"), slot_of("q", nb, j))
                    if not (first and u == 0):
                        o_hi(n - 1)
                    act.wait_ge(A0["negmax"], n + 1)
                    k0 = 1 if i == 0 else 0
                    for h in range(G0):
                        sl = Sm[:, u % 2, h, k0 * P:256]
                        last = nc.scalar.activation(sl, sl, ACT.Exp, bias=negmax[:, h:h + 1], scale=SCALE0,
                                                    accum_out=rsum[:, h:h + 1])
                    last.then_inc(A0["exp"], 1)
                    if its:
                        rope_hi(its[0][0], "q", nb, j)
                    if len(its) > 1:
                        rope_act1(act, its[1][0], src0("k"), slot_of("k", nb, j))
                        rope_hi(its[1][0], "k", nb, j)
                    if has_next and j == 1:
                        vcopy(bb + 1)
                    if has_next and j == 2:
                        v_hi(bb + 1, nb)
                    for kind, h, ahead in PIECES.get(u, []):
                        if (ahead and last_group) or (first and not ahead):
                            continue
                        split_hi(act, A0, kind, g + ahead, h)
                    if u < 6:
                        mean_abs(g, u)

            groups(act, body)
            n = NU * KVH0
            pt_hi(n - 1, QT - 1)
            o_hi(n - 1)

        def pool_attn0(pool):
            def rope_sin(r, slot):
                pool.wait_ge(R0["swap"], r + 1)
                nc.gpsimd.tensor_tensor(qs[:, slot, :], qs[:, slot, :], stab, ALU.mult).then_inc(R0["sin"], 1)

            def pnorm(n, i):
                pool.wait_ge(A0["rinv"], n + 1)
                k0 = 1 if i == 0 else 0
                sl = Sm[:, i % 2, :, k0 * P:256]
                nc.gpsimd.tensor_tensor(sl, sl, rinv[:, 0:4].unsqueeze(2).to_broadcast([P, G0, (2 - k0) * P]),
                                        ALU.mult).then_inc(A0["pnorm"], 1)

            def mean(g, s):
                pool.wait_ge(A0[f"mean_in{s % 2}"], 16 * (3 * g + s // 2 + 1))
                nc.gpsimd.tensor_tensor(mch[:, s % 2, 0, :], mch[:, s % 2, 0, :], mch[:, s % 2, 1, :],
                                        ALU.subtract).then_inc(A0["mean_d"], 1)

            def mean_add(g, s):
                m = s // 2
                pool.wait_ge(A0["mean_abs"], 6 * g + s + 1)
                pool.wait_ge(A0["mean_sum"], 6 * g + s + 1)
                nc.gpsimd.tensor_tensor(sums[:, m:m + 1], sums[:, m:m + 1], part[:, s:s + 1], ALU.add)\
                    .then_inc(A0["mean_sum"], 1)

            nc.gpsimd.memset(sums, 0.0).then_inc(A0["mean_sum"], 1)
            pool.wait_ge(s_const, CONST_DMAS * 16)
            for h in range(G0):
                split_lo(pool, A0, "q", 0, h)
            for k in ("k", "v", "o"):
                split_lo(pool, A0, k, 0)
            for j in range(G0):
                for r, k, h in items0(0, j):
                    rope_sin(r, slot_of(k, 0, j))

            def body(g, first, last_group):
                for u in range(NU):
                    b, i = u // QT, u % QT
                    n = NU * g + u
                    bb = 2 * g + b
                    nb, j = (b + 1) % 2, i
                    has_next = not (last_group and b == 1)
                    its = items0(bb + 1, j) if has_next else []
                    if its:
                        rope_sin(its[0][0], slot_of("q", nb, j))
                    pnorm(n, i)
                    if len(its) > 1:
                        rope_sin(its[1][0], slot_of("k", nb, j))
                    for kind, h, ahead in PIECES.get(u, []):
                        if (ahead and last_group) or (first and not ahead):
                            continue
                        split_lo(pool, A0, kind, g + ahead, h)
                    if u < 6:
                        mean(g, u)
                    if 1 <= u < 7:
                        mean_add(g, u - 1)

            groups(pool, body)

        def dve_attn0(dve):
            def rope_cos(r, k):
                dve.wait_ge(R0["swap"], r + 1)
                wait(dve, R0["rot"], r)
                nc.vector.tensor_tensor(tcos, src0(k), ctab, ALU.mult).then_inc(R0["cos"], 1)

            def rope_rot(r, slot):
                dve.wait_ge(R0["sin"], r + 1)
                dve.wait_ge(R0["cos"], r + 1)
                wait(dve, R0["hi"], r)
                wait(dve, R0["lo"], r)
                nc.vector.tensor_tensor(rot, tcos, qs[:, slot, :], ALU.add).then_inc(R0["rot"], 1)

            def rope_lo(r, k, b, j):
                dve.wait_ge(R0["hi"], r + 1)
                nc.vector.tensor_tensor(dst0(k, b, j, 1), rot, f32(dst0(k, b, j, 0)), ALU.subtract)\
                    .then_inc(R0["lo"], 1)

            def v_lo(bb, b):
                dve.wait_ge(A0["v_hi"], bb + 1)
                nc.vector.tensor_tensor(V[:, b, 1], PS[:, 7, :].rearrange("p (j k) -> p j k", j=QT),
                                        f32(V[:, b, 0]), ALU.subtract).then_inc(A0["v_lo"], 1)

            def yadd(n, t):
                dve.wait_ge(A0["yproj"], n + 1)
                nc.vector.tensor_tensor(y[:, t, :], PS[:, 5, :], y[:, t, :], ALU.add).then_inc(A0["yadd"], 1)

            def pt_lo(n, i):
                dve.wait_ge(A0["pt_hi"], n + 1)
                k0 = 1 if i == 0 else 0
                nc.vector.tensor_tensor(PT[:, 1, k0:2, :], PS[:, 2 + k0:4, :], f32(PT[:, 0, k0:2, :]),
                                        ALU.subtract).then_inc(A0["pt_lo"], 1)

            def o_lo(n):
                dve.wait_ge(A0["o_hi"], n + 1)
                nc.vector.tensor_tensor(OT[:, 1], PS[:, 4, :].rearrange("p (h k) -> p h k", h=4), f32(OT[:, 0]),
                                        ALU.subtract).then_inc(A0["o_lo"], 1)

            for j in range(G0):
                for r, k, h in items0(0, j):
                    rope_cos(r, k)
                    rope_rot(r, slot_of(k, 0, j))
                    rope_lo(r, k, 0, j)
                if j == 2:
                    v_lo(0, 0)

            def body(g, first, last_group):
                for u in range(NU):
                    b, i = u // QT, u % QT
                    n = NU * g + u
                    bb = 2 * g + b
                    nb, j = (b + 1) % 2, i
                    has_next = not (last_group and b == 1)
                    its = items0(bb + 1, j) if has_next else []
                    if not (first and u < 2):
                        yadd(n - 2, (u - 2) % NU)
                    k0 = 1 if i == 0 else 0
                    dve.wait_ge(A0["scores"], n + 1)
                    src = PS[:, 0:2, :].rearrange("p a (h k) -> p (a h) k", h=2)[:, :, k0 * P:256]
                    nc.vector.tensor_tensor(Sm[:, u % 2, :, k0 * P:256], src,
                                            mask0[:, k0 * P:256].unsqueeze(1).to_broadcast([P, G0, (2 - k0) * P]),
                                            ALU.add).then_inc(A0["masked"], 1)
                    if not (first and u == 0):
                        pt_lo(n - 1, (u - 1) % QT)
                    dve.wait_ge(A0["masked"], n + 1)
                    wait(dve, A0["exp"], n)
                    nc.vector.tensor_reduce(negmax[:, 0:4], Sm[:, u % 2, :, k0 * P:256], AX.X, ALU.max)\
                        .then_inc(A0["maxed"], 1)
                    if its:
                        rope_cos(its[0][0], "q")
                    dve.wait_ge(A0["maxed"], n + 1)
                    nc.vector.tensor_scalar(negmax[:, 0:4], negmax[:, 0:4], -SCALE0, None, ALU.mult)\
                        .then_inc(A0["negmax"], 1)
                    if not (first and u == 0):
                        o_lo(n - 1)
                    if its:
                        rope_rot(its[0][0], slot_of("q", nb, j))
                    dve.wait_ge(A0["exp"], n + 1)
                    wait(dve, A0["pnorm"], n)
                    nc.vector.reciprocal(rinv[:, 0:4], rsum[:, 0:4]).then_inc(A0["rinv"], 1)
                    if its:
                        rope_lo(its[0][0], "q", nb, j)
                    if len(its) > 1:
                        rope_cos(its[1][0], "k")
                        rope_rot(its[1][0], slot_of("k", nb, j))
                        rope_lo(its[1][0], "k", nb, j)
                    if has_next and j == 2:
                        v_lo(bb + 1, nb)

            groups(dve, body)
            n = NU * KVH0
            yadd(n - 2, NU - 2)
            pt_lo(n - 1, QT - 1)
            o_lo(n - 1)
            yadd(n - 1, NU - 1)
            dve.wait_ge(A0["coeff_ps"], 1)
            nc.vector.tensor_scalar(coeff, PS[:, 6, 0:3], 1.0 / (INT0 * D), None, ALU.mult).then_inc(A0["coeff"], 1)

        def sp_attn0(sp):
            def mean(g, s):
                wait(sp, A0["mean_abs"], 6 * g + s - 1)
                sp.dma_start(mch[:, s % 2], mean_w[slice_at(6 * g + s)].rearrange("o p w k -> p (o w) k"))\
                    .then_inc(A0[f"mean_in{s % 2}"], 16)

            def slice_at(v):
                return bass.ds(v, 1)

            def weights(g):
                wait(sp, A0["wq_lo"], 4 * g)
                wait(sp, A0["wk_lo"], g)
                wait(sp, A0["wv_lo"], g)
                sp.dma_start(raw[:, 0:WO0], attn0_w[slice_at(g), :, 0:WO0].rearrange("o p k -> p (o k)"))\
                    .then_inc(A0["raw_qkv"], 16)
                wait(sp, A0["wo_lo"], g)
                sp.dma_start(raw[:, WO0:WCOLS], attn0_w[slice_at(g), :, WO0:WCOLS].rearrange("o p k -> p (o k)"))\
                    .then_inc(A0["raw_wo"], 16)

            weights(0)

            def body(g, first, last_group):
                mean(g, 0)
                mean(g, 1)
                if not last_group:
                    weights(g + 1)
                for s in range(2, 6):
                    mean(g, s)

            groups(sp, body)

        def ffn_sems(tag):
            return names(tag, "raw0", "raw1", "d", "sign", "w", "w13_hi", "w13_lo", "w2_hi", "w2_lo", "gate", "silu", "h",
                         "h_hi", "h_lo", "down", "yadd", "ad")

        F0, F1 = ffn_sems("f0"), ffn_sems("f1")

        def tiles(eng, nt, body):
            body(0, 0, True)
            body(1, 1, False)
            body(2, 0, False)
            pairs = (nt - 1) // 2
            with eng.Fori(1, pairs) as p:
                body(2 * p + 1, 1, False)
                body(2 * p + 2, 0, False)
            if (nt - 1) % 2:
                body(nt - 1, (nt - 1) % 2, False)

        def sp_ffn(sp, F, nt, wdram, diff, before):
            before(sp)

            def load(j, s, first):
                if not first:
                    if diff:
                        wait(sp, F["w2_lo"], j - 1)
                    else:
                        wait(sp, F["h_lo"], 2 * (j - 1))
                sp.dma_start(raww_flat[:, s, 0:wdram.shape[2]], wdram[bass.ds(j, 1)].rearrange("o p k -> p (o k)"))\
                    .then_inc(F[f"raw{s}"], 16)

            load(0, 0, True)
            load(1, 1, True)
            pairs = (nt - 2) // 2
            with sp.Fori(1, 1 + pairs) as p:
                load(2 * p, 0, False)
                load(2 * p + 1, 1, False)
            if nt % 2:
                load(nt - 1, 0, False)

        def pool_ffn(pool, F, nt, diff):
            def loaded(pool, j, s):
                n = 8 * (j + 2 - s)
                pool.wait_ge(F[f"raw{s}"], n)

            def prep(j, s):
                if diff:
                    loaded(pool, j, s)
                    nc.gpsimd.tensor_tensor(raww[:, s, 0], raww[:, s, 0], raww[:, s, 1], ALU.subtract)\
                        .then_inc(F["d"], 1)
                else:
                    loaded(pool, j, s)
                    nc.gpsimd.tensor_tensor(raww[:, s, 0, 1024:1536], raww[:, s, 0, 1024:1536], adrow, ALU.mult)\
                        .then_inc(F["w"], 1)

            def w13_lo(j, s):
                pool.wait_ge(F["w13_hi"], j + 1)
                nc.gpsimd.tensor_tensor(W13[:, s, 1].rearrange("p m c k -> p (m c k)"), raww[:, s, 0, 0:1024],
                                        f32(W13[:, s, 0].rearrange("p m c k -> p (m c k)")), ALU.subtract)\
                    .then_inc(F["w13_lo"], 1)

            def w2_lo(j, s):
                pool.wait_ge(F["w2_hi"], j + 1)
                nc.gpsimd.tensor_tensor(W2[:, s, 1], raww[:, s, 0, 1024:1536], f32(W2[:, s, 0]), ALU.subtract)\
                    .then_inc(F["w2_lo"], 1)

            def h_lo(j, s, b):
                pool.wait_ge(F["h_hi"], 2 * j + b + 1)
                sl = slice(b * SEQ, (b + 1) * SEQ)
                nc.gpsimd.tensor_tensor(hT[:, s, 1, sl], hh[:, b], f32(hT[:, s, 0, sl]), ALU.subtract)\
                    .then_inc(F["h_lo"], 1)

            prep(0, 0)
            w13_lo(0, 0)

            def body(j, s, first, last=False):
                w2_lo(j, s)
                if not last:
                    prep(j + 1, 1 - s)
                h_lo(j, s, 0)
                if not last:
                    w13_lo(j + 1, 1 - s)
                h_lo(j, s, 1)

            tiles(pool, nt - 1, body)
            body(nt - 1, (nt - 1) % 2, False, True)

        def act_ffn(act, F, nt, diff):
            def sign(j, s):
                if diff:
                    act.wait_ge(F["d"], j + 1)
                    nc.scalar.activation(raww[:, s, 0], raww[:, s, 0], ACT.Sign).then_inc(F["sign"], 1)

            def w13_hi(j, s):
                act.wait_ge(F["w"], j + 1)
                wait(act, F["gate"], 2 * (j - 1))
                nc.scalar.activation(W13[:, s, 0].rearrange("p m c k -> p (m c k)"), raww[:, s, 0, 0:1024],
                                     ACT.Copy).then_inc(F["w13_hi"], 1)

            def w2_hi(j, s):
                wait(act, F["down"], TT * (j - 1))
                nc.scalar.activation(W2[:, s, 0], raww[:, s, 0, 1024:1536], ACT.Copy).then_inc(F["w2_hi"], 1)

            def silu(j, b, tile_scale):
                act.wait_ge(F["gate"], 2 * j + b + 1)
                wait(act, F["h"], 2 * (j - 1) + b + 1)
                nc.scalar.activation(sg[:, b], PS[:, 2 * b, :], ACT.Silu, scale=tile_scale).then_inc(F["silu"], 1)

            def h_hi(j, s, b):
                act.wait_ge(F["h"], 2 * j + b + 1)
                wait(act, F["down"], TT * (j - 1))
                nc.scalar.activation(hT[:, s, 0, b * SEQ:(b + 1) * SEQ], hh[:, b], ACT.Copy).then_inc(F["h_hi"], 1)

            sign(0, 0)
            w13_hi(0, 0)

            def body(j, s, first, last=False):
                w2_hi(j, s)
                sc = 1.0 if diff else scale_g[:, s]
                silu(j, 0, sc)
                if not last:
                    sign(j + 1, 1 - s)
                h_hi(j, s, 0)
                silu(j, 1, sc)
                if not last:
                    w13_hi(j + 1, 1 - s)
                h_hi(j, s, 1)

            tiles(act, nt - 1, body)
            body(nt - 1, (nt - 1) % 2, False, True)

        def dve_ffn(dve, F, nt, diff):
            def combine(j, s):
                if diff:
                    dve.wait_ge(F["sign"], j + 1)
                    for m in range(3):
                        sl = slice(512 * m, 512 * (m + 1))
                        last = nc.vector.scalar_tensor_tensor(raww[:, s, 0, sl], raww[:, s, 0, sl], coeff[:, m:m + 1],
                                                              raww[:, s, 1, sl], ALU.mult, ALU.add)
                    last.then_inc(F["w"], 1)

            def h(j, s, b):
                dve.wait_ge(F["silu"], 2 * j + b + 1)
                wait(dve, F["h_lo"], 2 * (j - 1) + b + 1)
                if diff:
                    ins = nc.vector.tensor_tensor(hh[:, b], PS[:, 2 * b + 1, :], sg[:, b], ALU.mult)
                else:
                    ins = nc.vector.scalar_tensor_tensor(hh[:, b], PS[:, 2 * b + 1, :], scale_u[:, s],
                                                         sg[:, b], ALU.mult, ALU.mult)
                ins.then_inc(F["h"], 1)

            def yadd(j, t):
                dve.wait_ge(F["down"], TT * j + t + 1)
                nc.vector.tensor_tensor(y[:, t, :], PS[:, 4 + t % 4, :], y[:, t, :], ALU.add).then_inc(F["yadd"], 1)

            if diff:
                dve.wait_ge(A0["coeff"], 1)
            combine(0, 0)

            def body(j, s, first, last=False):
                h(j, s, 0)
                h(j, s, 1)
                if not last:
                    combine(j + 1, 1 - s)
                if not first:
                    for t in range(TT):
                        yadd(j - 1, t)

            tiles(dve, nt - 1, body)
            body(nt - 1, (nt - 1) % 2, False, True)
            for t in range(TT):
                yadd(nt - 1, t)

        def pe_ffn(pe, F, nt):
            def gate(j, s, b):
                pe.wait_ge(F["w13_lo"], j + 1)
                wait(pe, F["h"], 2 * (j - 1) + b + 1)
                for m in range(2):
                    last = mm3(PS[:, 2 * b + m, :], lambda a, c: W13[:, s, a, m, c, :],
                               lambda q, c: xT[:, q, c, b * SEQ:(b + 1) * SEQ], DC)
                last.then_inc(F["gate"], 1)

            def down(j, s):
                pe.wait_ge(F["w2_lo"], j + 1)
                pe.wait_ge(F["h_lo"], 2 * j + 2)
                for t in range(TT):
                    wait(pe, F["yadd"], TT * j + t - 3)
                    mm3(PS[:, 4 + t % 4, :], lambda a, c: hT[:, s, a, t * P:(t + 1) * P],
                        lambda q, c: W2[:, s, q, :], 1).then_inc(F["down"], 1)

            def body(j, s, first):
                gate(j, s, 0)
                gate(j, s, 1)
                if not first:
                    down(j - 1, 1 - s)

            tiles(pe, nt, body)
            down(nt - 1, (nt - 1) % 2)

        A1 = names("a1", "raw_qkv", "raw_wo", "wq_hi", "wq_lo", "wk_hi", "wk_lo", "wv_hi", "wv_lo", "wo_hi", "wo_lo",
                   "tables", "vproj", "v", "vz", "stored0", "stored1", "kst", "qst0", "qst1", "mask", "mask_r",
                   "scores", "evac", "tiny", "thr", "acc", "cut", "masked", "pick", "tau", "flag_ps", "exp", "final",
                   "rinv", "pnorm", "turned", "pt", "pv", "o_hi", "o_lo", "yproj", "yadd")
        R1 = names("r1", "proj", "swap", "cos", "sin", "rot", "hi", "lo")
        NI = 5 * BATCH
        NB = 2 * TT

        def tile_of(x):
            n = x // 2
            return n, n % QT, x % 2, (n % QT + 1) * P

        def before(x, k=1):
            return k * sum(1 for v in range(x) if tile_of(v)[1] > 0)

        def tcount(x, q, kb):
            return sum(4 * (tile_of(v)[1] + 1) for v in range(x)) + q * (tile_of(x)[1] + 1) + kb

        def sp_attn1(sp):
            sp.wait_ge(F0["yadd"], TT * NT0)
            sp.wait_ge(T["fed"], TT * 2 + 1)
            sp.dma_start(raw[:, 0:WO0], attn1_w[:, 0:WO0]).then_inc(A1["raw_qkv"], 16)
            sp.dma_start(raw[:, WO0:WCOLS], attn1_w[:, WO0:WCOLS]).then_inc(A1["raw_wo"], 16)
            sp.dma_start(AF[:, rope1_at:rope1_at + 1024], rope1).then_inc(A1["tables"], 16)
            sp.dma_start(ztab, quant[:, 0:6]).then_inc(A1["mask"], 16)
            sp.dma_start(iota16, quant[:, 8:24]).then_inc(A1["mask"], 16)
            sp.dma_start(mask0[:, 0:P], consts[:, 768:896]).then_inc(A1["mask"], 16)
            for r in range(NI):
                b, j = r // 5, r % 5
                sp.wait_ge(R1["lo"], r + 1)
                for s in range(2):
                    sp.dma_start(scr[b, j, s], f32(rq[:, r % 2, s, :])).then_inc(A1[f"stored{r % 2}"], 16)
            sp.wait_ge(A1["v"], TT)
            for s in range(2):
                sp.wait_ge(A1[f"stored{s}"], 16 * NI)
            for n in range(TT):
                b, i = n // QT, n % QT
                if i == 0:
                    if b > 0:
                        sp.wait_ge(A1["scores"], QT * 32)
                    for a, s in enumerate((0, 1, 0)):
                        src = scr[b, 4, s].rearrange("(c h) t -> c h t", c=HD1)
                        sp.dma_start(f32(kst[a * HD1:(a + 1) * HD1]), src).then_inc(A1["kst"], 16)
                if n >= 2:
                    sp.wait_ge(A1["scores"], 32 * (n - 1))
                for j in range(4):
                    for a, s in enumerate((0, 0, 1)):
                        src = scr[b, j, s].rearrange("(c h) t -> c h t", c=HD1)[:, :, i * P:(i + 1) * P]
                        sp.dma_start(f32(qst[a * HD1:(a + 1) * HD1, n % 2, 8 * j:8 * j + 8]), src)\
                            .then_inc(A1[f"qst{n % 2}"], 16)

        def pe_attn1(pe):
            for r in range(NI):
                b, j = r // 5, r % 5
                if j < 4:
                    pe.wait_ge(A1["wq_lo"], j + 1)
                else:
                    pe.wait_ge(A1["wk_lo"], 1)
                wait(pe, R1["cos"], r - 1)
                w = W1["q"][:, :, j] if j < 4 else W1["k"]
                mm3(PS[:, 6 + r % 2, :], lambda a, c: w[:, a, c, :], lambda m, c: xT[:, m, c, b * SEQ:(b + 1) * SEQ],
                    DC).then_inc(R1["proj"], 1)
            pe.wait_ge(A1["wv_lo"], 1)
            for t in range(TT):
                wait(pe, A1["v"], t - 1)
                mm3(PS[:, 4 + t % 2, 0:P], lambda a, c: xT[:, a, c, t * P:(t + 1) * P],
                    lambda m, c: W1["v"][:, m, c, :], DC).then_inc(A1["vproj"], 1)
            pe.wait_ge(A1["mask_r"], 2)

            def scores(x, q):
                n, i, hf, W = tile_of(x)
                if q == 0 and hf == 0:
                    pe.wait_ge(A1["kst"], 48 * (n // QT + 1))
                    pe.wait_ge(A1[f"qst{n % 2}"], 16 * 12 * (n // 2 + 1))
                for h in range(G1):
                    head = hf * 16 + 4 * q + h
                    wait(pe, A1["evac"], 16 * x + 4 * q + h - 3)
                    nc.tensor.matmul(PS[:, h, 0:W], qst[0:48, n % 2, head, :], kst[0:48, head // G1, 0:W],
                                     start=True, stop=False)
                    nc.tensor.matmul(PS[:, h, W - P:W], ident_r, mask_r, start=False, stop=True)\
                        .then_inc(A1["scores"], 1)

            def values(x, q):
                n, i, hf, W = tile_of(x)
                pe.wait_ge(A1["pnorm"], 4 * x + q + 1)
                for kb in range(i + 1):
                    tn = tcount(x, q, kb)
                    wait(pe, A1["pt"], tn - 1)
                    for h in range(G1):
                        last = nc.tensor.transpose(PS[:, 4 + tn % 2, h * P:(h + 1) * P],
                                                   P1[:, q % 2, h, kb * P:(kb + 1) * P], ident)
                    last.then_inc(A1["turned"], 1)
                    if kb >= 1:
                        product(x, q, kb - 1)
                product(x, q, i)

            def product(x, q, kb):
                n, i, hf, W = tile_of(x)
                tn = tcount(x, q, kb)
                kv = 4 * hf + q
                pe.wait_ge(A1["pt"], tn + 1)
                if kv == 0 and kb == 0:
                    pe.wait_ge(A1["vz"], n // QT + 1)
                    wait(pe, A1["o_lo"], n)
                nc.tensor.matmul(PS[:, 6, :], Vz[:, kb, kv * P:(kv + 1) * P], PT1[:, tn % 2, :],
                                 start=(kv == 0 and kb == 0), stop=(kv == KVH1 - 1 and kb == i))\
                    .then_inc(A1["pv"], 1)

            def project(n):
                pe.wait_ge(A1["wo_lo"], 1)
                pe.wait_ge(A1["o_lo"], n + 1)
                wait(pe, A1["yadd"], n)
                mm3(PS[:, 7, :], lambda a, c: OT1[:, a, c, :], lambda m, c: W1["o"][:, m, c, :], G1)\
                    .then_inc(A1["yproj"], 1)

            for x in range(-1, NB + 1):
                xp = x - 1
                if xp >= 0 and tile_of(xp)[1] > 0:
                    pe.wait_ge(A1["cut"], before(xp) + 1)
                    nc.tensor.matmul(PS[:, 7, 0:1], ones, flag_row, start=True, stop=True)\
                        .then_inc(A1["flag_ps"], 1)
                for q in range(4):
                    if x + 1 < NB:
                        scores(x + 1, q)
                    if xp >= 0:
                        values(xp, q)
                if xp >= 0 and xp % 2:
                    project(xp // 2)

        def act_attn1(act):
            for h in range(4):
                split_hi(act, A1, "q", 0, h)
            for k in ("k", "v", "o"):
                split_hi(act, A1, k, 0)
            for r in range(NI):
                src = PS[:, 6 + r % 2, :]
                act.wait_ge(R1["proj"], r + 1)
                wait(act, R1["rot"], r - 1)
                nc.scalar.activation(qs[0:64, r % 2, :], src[64:128, :], ACT.Copy)
                nc.scalar.activation(qs[64:128, r % 2, :], src[0:64, :], ACT.Copy).then_inc(R1["swap"], 1)
                act.wait_ge(R1["rot"], r + 1)
                wait(act, A1[f"stored{r % 2}"], 32 * (r // 2))
                nc.scalar.activation(rq[:, r % 2, 0, :], rot, ACT.Copy).then_inc(R1["hi"], 1)
            for t in range(TT):
                act.wait_ge(A1["vproj"], t + 1)
                if t == 0:
                    act.wait_ge(R1["rot"], NI)
                nc.scalar.activation(Vc[:, t, :], PS[:, 4 + t % 2, 0:P], ACT.Copy).then_inc(A1["v"], 1)
            act.wait_ge(A1["vproj"], TT)
            act.wait_ge(A1["mask"], 48)
            nc.scalar.activation(ident_r, ident, ACT.Copy).then_inc(A1["mask_r"], 1)
            nc.scalar.activation(mask_r, mask0[:, 0:P], ACT.Copy).then_inc(A1["mask_r"], 1)

            def count(x, r):
                n, i, hf, W = tile_of(x)
                act.wait_ge(A1["thr"], ROUNDS * before(x) + r + 1)
                k = 16 * (ROUNDS * before(x) + r)
                for h in range(16):
                    wait(act, A1["acc"], k + h - 1)
                    nc.scalar.activation(junk[h % 2][:, 0:W], S1[x % 2][:, h, 0:W], ACT.Sign,
                                         bias=st["nthr"][:, x % 2, h:h + 1],
                                         accum_out=st["acc"][:, x % 2, h:h + 1]).then_inc(A1["acc"], 1)

            def exp(x, q):
                n, i, hf, W = tile_of(x)
                act.wait_ge(A1["tau"], x + 1)
                un = 4 * x + q
                if un >= 2:
                    xx, qq = (x, q - 2) if q >= 2 else (x - 1, q + 2)
                    act.wait_ge(A1["turned"], tcount(xx, qq, tile_of(xx)[1]) + 1)
                for h in range(G1):
                    hd = 4 * q + h
                    kw = {} if i > 0 else {"accum_out": rsum1[:, hd:hd + 1]}
                    last = nc.scalar.activation(P1[:, q % 2, h, 0:W], S1[x % 2][:, hd, 0:W], ACT.Exp,
                                                bias=st["nmax"][:, x % 2, hd:hd + 1], scale=SCALE1, **kw)
                last.then_inc(A1["exp"], 1)

            def pt(x, q):
                for kb in range(tile_of(x)[1] + 1):
                    tn = tcount(x, q, kb)
                    act.wait_ge(A1["turned"], tn + 1)
                    wait(act, A1["pv"], tn - 1)
                    nc.scalar.activation(PT1[:, tn % 2, :], PS[:, 4 + tn % 2, :], ACT.Copy).then_inc(A1["pt"], 1)

            for x in range(0, NB + 1):
                xp = x - 1
                if x < NB and tile_of(x)[1] > 0:
                    for r in range(ROUNDS):
                        count(x, r)
                if xp >= 0:
                    exp(xp, 0)
                    exp(xp, 1)
                    pt(xp, 0)
                    exp(xp, 2)
                    pt(xp, 1)
                    exp(xp, 3)
                    pt(xp, 2)
                    pt(xp, 3)
                    if xp % 2:
                        n = xp // 2
                        act.wait_ge(A1["pv"], tcount(xp, 3, n % QT) + 1)
                        wait(act, A1["yproj"], n)
                        nc.scalar.activation(OT1[:, 0], PS[:, 6, :].rearrange("p (h k) -> p h k", h=4), ACT.Copy)\
                            .then_inc(A1["o_hi"], 1)

        def pool_attn1(pool):
            for h in range(4):
                split_lo(pool, A1, "q", 0, h)
            for k in ("k", "v", "o"):
                split_lo(pool, A1, k, 0)
            pool.wait_ge(A1["tables"], 16)
            for r in range(NI):
                pool.wait_ge(R1["swap"], r + 1)
                nc.gpsimd.tensor_tensor(qs[:, r % 2, :], qs[:, r % 2, :], stab, ALU.mult).then_inc(R1["sin"], 1)
            nm = [0]

            def below(x, h):
                n, i, hf, W = tile_of(x)
                k = 16 * before(x) + h
                wait(pool, A1["pick"], 3 * (k - 2) + 3)
                nc.gpsimd.tensor_scalar(X1[:, h % 2, 0:W], S1[x % 2][:, h, 0:W], st["thr"][:, x % 2, h:h + 1],
                                        DROPPED, ALU.is_ge, ALU.mult).then_inc(A1["masked"], 1)
                pool.wait_ge(A1["masked"], 2 * k + 1)
                nc.gpsimd.tensor_tensor(X1[:, h % 2, 0:W], X1[:, h % 2, 0:W], S1[x % 2][:, h, 0:W], ALU.add)\
                    .then_inc(A1["masked"], 1)

            def norm(x, q):
                n, i, hf, W = tile_of(x)
                pool.wait_ge(A1["rinv"], 4 * x + q + 1)
                sl = P1[:, q % 2, :, 0:W]
                nc.gpsimd.tensor_tensor(sl, sl, rinv1[:, 4 * q:4 * q + 4].unsqueeze(2).to_broadcast([P, G1, W]),
                                        ALU.mult).then_inc(A1["pnorm"], 1)

            for x in range(0, NB + 1):
                xp = x - 1
                if xp >= 0 and tile_of(xp)[1] > 0:
                    pool.wait_ge(A1["thr"], ROUNDS * before(xp) + ROUNDS)
                    for h in range(16):
                        below(xp, h)
                if xp >= 0:
                    for q in range(4):
                        norm(xp, q)

        def dve_attn1(dve):
            v = nc.vector
            nc.vector.memset(Vz, 0.0).then_inc(A1["tiny"], 1)
            dve.wait_ge(A1["tables"], 16)
            for r in range(NI):
                dve.wait_ge(R1["swap"], r + 1)
                wait(dve, R1["rot"], r)
                v.tensor_tensor(tcos, PS[:, 6 + r % 2, :], ctab, ALU.mult).then_inc(R1["cos"], 1)
                dve.wait_ge(R1["sin"], r + 1)
                dve.wait_ge(R1["cos"], r + 1)
                wait(dve, R1["hi"], r)
                wait(dve, R1["lo"], r)
                v.tensor_tensor(rot, tcos, qs[:, r % 2, :], ALU.add).then_inc(R1["rot"], 1)
                dve.wait_ge(R1["hi"], r + 1)
                v.tensor_tensor(rq[:, r % 2, 1, :], rot, f32(rq[:, r % 2, 0, :]), ALU.subtract)\
                    .then_inc(R1["lo"], 1)
            dve.wait_ge(A1["v"], TT)
            dve.wait_ge(A1["wo_lo"], 1)
            dve.wait_ge(A1["mask"], 48)
            dve.wait_ge(A1["mask_r"], 2)
            for s in range(2):
                dve.wait_ge(A1[f"stored{s}"], 16 * NI)
            tiny = [1]

            def step(ins):
                ins.then_inc(A1["tiny"], 1)
                tiny[0] += 1
                dve.wait_ge(A1["tiny"], tiny[0])

            def evac(x, q):
                n, i, hf, W = tile_of(x)
                if x >= 2:
                    dve.wait_ge(A1["exp"], 4 * (x - 2) + q + 1)
                    if tile_of(x - 2)[1] > 0:
                        dve.wait_ge(A1["final"], 4 * before(x - 2) + q + 1)
                for h in range(4 * q, 4 * q + 4):
                    dve.wait_ge(A1["scores"], 16 * x + h + 1)
                    v.tensor_scalar(S1[x % 2][:, h, 0:W], PS[:, h % 4, 0:W], 0.0, TAKEN, ALU.add, ALU.max,
                                    accum_out=st["rmax"][:, x % 2, h:h + 1]).then_inc(A1["evac"], 1)
                if i > 0:
                    for h in range(4 * q, 4 * q + 4):
                        dve.wait_ge(A1["evac"], 16 * x + h + 1)
                        last = v.bn_stats(stat6[:, h, :], S1[x % 2][:, h, 0:P])
                    step(last)

            def start(x):
                n, i, hf, W = tile_of(x)
                dve.wait_ge(A1["evac"], 16 * x + 16)
                step(v.tensor_scalar(st["nmax"][:, x % 2], st["rmax"][:, x % 2], -SCALE1, None, ALU.mult))
                if i == 0:
                    return
                me, mo, ve, vo = (stat6[:, :, k] for k in (1, 4, 2, 5))
                step(v.tensor_tensor(st["msum"], me, mo, ALU.add))
                step(v.tensor_tensor(st["mdiff"], me, mo, ALU.subtract))
                step(v.tensor_tensor(st["mdiff"], st["mdiff"], st["mdiff"], ALU.mult))
                step(v.tensor_tensor(st["vsum"], ve, vo, ALU.add))
                step(v.scalar_tensor_tensor(st["vsum"], st["mdiff"], P / 4.0, st["vsum"], ALU.mult, ALU.add))
                step(v.scalar_tensor_tensor(st["spread"], st["msum"], -0.5, st["rmax"][:, x % 2], ALU.mult, ALU.add))
                step(v.tensor_scalar(st["spread"], st["spread"], 0.36, 1e-30, ALU.mult, ALU.max))
                step(v.reciprocal(st["recip"], st["spread"]))
                step(v.scalar_tensor_tensor(st["vsum"], st["vsum"], 1.0 / P, st["recip"], ALU.mult, ALU.mult))
                step(v.tensor_tensor(st["spread"], st["spread"], st["vsum"], ALU.add))
                step(v.tensor_scalar(st["step"], st["spread"], ztab[:, i - 1:i], None, ALU.mult))
                step(v.scalar_tensor_tensor(st["thr"][:, x % 2], st["msum"], 0.5, st["step"], ALU.mult, ALU.add))
                step(v.tensor_scalar(st["slope"], st["spread"], ztab[:, 2 + i:3 + i], None, ALU.mult))
                v.tensor_scalar(st["nthr"][:, x % 2], st["thr"][:, x % 2], -1.0, None, ALU.mult)\
                    .then_inc(A1["thr"], 1)

            def update(x, r):
                n, i, hf, W = tile_of(x)
                aim = 2.0 * AIM - W
                a, t = st["acc"][:, x % 2], st["thr"][:, x % 2]
                dve.wait_ge(A1["acc"], 16 * (ROUNDS * before(x) + r + 1))
                step(v.tensor_scalar(st["diff"], a, aim, None, ALU.subtract))
                step(v.tensor_tensor(st["bad"], st["diff"], st["diff"], ALU.mult))
                step(v.tensor_scalar(st["bad"], st["bad"], (WINDOW - 1.0) ** 2 + 1, None, ALU.is_gt))
                if r == 0:
                    step(v.tensor_tensor(st["step"], st["diff"], st["slope"], ALU.mult))
                    step(v.scalar_tensor_tensor(st["tmp"], st["step"], 3.0, t, ALU.mult, ALU.add))
                    step(v.tensor_tensor(st["tl"], st["tmp"], t, ALU.min))
                    step(v.tensor_tensor(st["th"], st["tmp"], t, ALU.max))
                    step(v.tensor_scalar(st["tmp"], st["diff"], -2.0, aim, ALU.mult, ALU.add))
                    step(v.tensor_tensor(st["al"], st["tmp"], a, ALU.max))
                    step(v.tensor_tensor(st["ah"], st["tmp"], a, ALU.min))
                else:
                    step(v.tensor_scalar(st["over"], st["diff"], 0.0, None, ALU.is_gt))
                    step(v.tensor_scalar(st["under"], st["diff"], 0.0, None, ALU.is_le))
                    over, under = (st[k].bitcast(mybir.dt.uint32) for k in ("over", "under"))
                    step(v.copy_predicated(st["tl"], over, t))
                    step(v.copy_predicated(st["al"], over, a))
                    step(v.copy_predicated(st["th"], under, t))
                    step(v.copy_predicated(st["ah"], under, a))
                    step(v.tensor_tensor(st["tmp"], st["al"], st["ah"], ALU.subtract))
                    step(v.tensor_scalar(st["tmp"], st["tmp"], 1.0, None, ALU.max))
                    step(v.reciprocal(st["tmp"], st["tmp"]))
                    step(v.tensor_tensor(st["step"], st["th"], st["tl"], ALU.subtract))
                    step(v.scalar_tensor_tensor(st["step"], st["al"], aim, st["step"], ALU.subtract, ALU.mult))
                    step(v.tensor_tensor(st["step"], st["step"], st["tmp"], ALU.mult))
                    step(v.tensor_tensor(st["step"], st["step"], st["tl"], ALU.add))
                    step(v.tensor_tensor(st["step"], st["step"], t, ALU.subtract))
                step(v.tensor_tensor(st["step"], st["step"], st["bad"], ALU.mult))
                step(v.tensor_tensor(t, t, st["step"], ALU.add))
                v.tensor_scalar(st["nthr"][:, x % 2], t, -1.0, None, ALU.mult).then_inc(A1["thr"], 1)

            def pick(x, q):
                n, i, hf, W = tile_of(x)
                for h in range(4 * q, 4 * q + 4):
                    k = 16 * before(x) + h
                    wk = X1[:, h % 2, 0:W]
                    dve.wait_ge(A1["masked"], 2 * k + 2)
                    v.max(best[:, h, 0:8], wk).then_inc(A1["pick"], 1)
                    dve.wait_ge(A1["pick"], 3 * k + 1)
                    v.match_replace(wk, best[:, h, 0:8], wk, TAKEN).then_inc(A1["pick"], 1)
                    dve.wait_ge(A1["pick"], 3 * k + 2)
                    v.max(best[:, h, 8:16], wk).then_inc(A1["pick"], 1)

            def cut(x):
                n, i, hf, W = tile_of(x)
                dve.wait_ge(A1["acc"], 16 * ROUNDS * (before(x) + 1))
                step(v.tensor_scalar(st["tmp"], st["acc"][:, x % 2], -0.5, TOPK - W / 2.0, ALU.mult, ALU.add))
                step(v.tensor_tensor(hit, iota16.unsqueeze(1).to_broadcast([P, 16, 16]),
                                     st["tmp"].unsqueeze(2).to_broadcast([P, 16, 16]), ALU.is_equal))
                dve.wait_ge(A1["pick"], 3 * (16 * before(x) + 16))
                step(v.tensor_tensor(val, hit, best, ALU.mult))
                step(v.tensor_reduce(st["tau"][:, x % 2], val, AX.X, ALU.add))
                step(v.tensor_tensor(val[:, :, 0:15], hit[:, :, 0:15], best[:, :, 1:16], ALU.mult))
                step(v.tensor_reduce(st["over"], val[:, :, 0:15], AX.X, ALU.add))
                step(v.tensor_reduce(st["under"], hit[:, :, 0:15], AX.X, ALU.add))
                step(v.tensor_tensor(st["over"], st["over"], st["tau"][:, x % 2], ALU.is_lt))
                step(v.tensor_tensor(st["over"], st["over"], st["under"], ALU.mult))
                v.tensor_reduce(flag_row, st["over"], AX.X, ALU.add).then_inc(A1["cut"], 1)

            def resolve(x):
                n, i, hf, W = tile_of(x)
                dve.wait_ge(A1["flag_ps"], before(x) + 1)
                step(v.tensor_copy(flag_int, PS[0:1, 7, 0:1]))
                wait(dve, A1["turned"], tcount(x, 0, 0))
                good = dve.value_load(flag_int)
                with dve.If(good != RESOLVED):
                    for h in range(16):
                        row, wk = S1[x % 2][:, h, 0:W], P1[:, 0, 0, 0:W]
                        v.tensor_copy(wk, row)
                        dve.drain()
                        with dve.Fori(0, TOPK // 8):
                            v.max(best[:, h, 0:8], wk)
                            dve.drain()
                            v.match_replace(wk, best[:, h, 0:8], wk, TAKEN)
                            dve.drain()
                        v.tensor_scalar(wk, wk, TAKEN, DROPPED, ALU.not_equal, ALU.mult)
                        dve.drain()
                        v.tensor_tensor(row, row, wk, ALU.add)
                        dve.drain()
                    v.memset(st["tau"][:, x % 2], -1.0e38)
                    dve.drain()
                v.tensor_copy(flag_row, flag_row).then_inc(A1["tau"], 1)

            def final(x, q):
                n, i, hf, W = tile_of(x)
                dve.wait_ge(A1["exp"], 4 * x + q + 1)
                if i > 0:
                    for h in range(4 * q, 4 * q + 4):
                        pr = P1[:, q % 2, h % 4, 0:W]
                        last = v.scalar_tensor_tensor(pr, S1[x % 2][:, h, 0:W], st["tau"][:, x % 2, h:h + 1], pr,
                                                      ALU.is_ge, ALU.mult, accum_out=rsum1[:, h:h + 1])
                    last.then_inc(A1["final"], 1)
                    dve.wait_ge(A1["final"], 4 * before(x) + q + 1)
                wait(dve, A1["pnorm"], 4 * (x - 1) + q + 1)
                v.reciprocal(rinv1[:, 4 * q:4 * q + 4], rsum1[:, 4 * q:4 * q + 4]).then_inc(A1["rinv"], 1)

            for x in range(-1, NB + 1):
                xp = x - 1
                search = 0 <= x < NB and tile_of(x)[1] > 0
                topk = xp >= 0 and tile_of(xp)[1] > 0
                for r in range(4):
                    if topk:
                        pick(xp, r)
                    if search and r < ROUNDS - 1:
                        update(x, r)
                if topk:
                    cut(xp)
                if xp >= 0 and xp % (2 * QT) == 0:
                    b = xp // (2 * QT)
                    if b > 0:
                        dve.wait_ge(A1["pv"], tcount(xp, 0, 0))
                    dve.wait_ge(A1["tiny"], 1)
                    dst = Vz.rearrange("p j (v c) -> p j v c", c=P + HD1)[:, :, :, 0:HD1]
                    src = Vc[:, b * QT:(b + 1) * QT, :].rearrange("p j (v c) -> p j v c", c=HD1)
                    v.tensor_copy(dst, src).then_inc(A1["vz"], 1)
                if topk:
                    resolve(xp)
                elif xp >= 0:
                    v.tensor_copy(st["tau"][:, xp % 2], st["nmax"][:, xp % 2]).then_inc(A1["tau"], 1)
                for q in range(4):
                    if xp >= 0:
                        final(xp, q)
                    if x + 1 < NB:
                        evac(x + 1, q)
                if x + 1 < NB:
                    start(x + 1)
                if xp >= 0 and xp % 2:
                    n = xp // 2
                    dve.wait_ge(A1["o_hi"], n + 1)
                    v.tensor_tensor(OT1[:, 1], PS[:, 6, :].rearrange("p (h k) -> p h k", h=4), f32(OT1[:, 0]),
                                    ALU.subtract).then_inc(A1["o_lo"], 1)
                    dve.wait_ge(A1["yproj"], n + 1)
                    v.tensor_tensor(y[:, n, :], PS[:, 7, :], y[:, n, :], ALU.add).then_inc(A1["yadd"], 1)

        CONST_DMAS = 3

        block = ctx.enter_context(nc.Block())

        @block.sync
        def _(sp):
            for t in range(TT):
                sp.dma_start(y[:, t, :], x[t * P:(t + 1) * P, :]).then_inc(s_x, 16)
            sp.dma_start(ident, consts[:, 0:128]).then_inc(s_const, 16)
            sp.dma_start(mask0, consts[:, 128:384]).then_inc(s_const, 16)
            sp.dma_start(AF[:, base + WCOLS:base + WCOLS + 1024], rope0).then_inc(s_const, 16)
            sp_attn0(sp)

            def free0(sp):
                sp.wait_ge(A0["mean_abs"], 6 * KVH0)
                sp.wait_ge(A0["yadd"], NU * KVH0)
            if stop_after >= 2:
                sp_ffn(sp, F0, NT0, ffn0_w, True, free0)
            if stop_after >= 3:
                sp_attn1(sp)

            def free1(sp):
                sp.wait_ge(A1["yadd"], TT)
                sp.dma_start(adrow, ad_rows).then_inc(F1["ad"], 16)
            if stop_after >= 4:
                sp_ffn(sp, F1, NT1, ffn1_w, False, free1)
            for t in range(TT):
                sp.wait_ge(T["fed"], TT * min(stop_after, 4) + t + 1)
                sp.dma_start(out[t * P:(t + 1) * P, :], y[:, t, :]).then_inc(s_out, 16)
            sp.wait_ge(s_out, 16 * TT)

        @block.tensor
        def _(pe):
            pe.wait_ge(s_const, 16 * CONST_DMAS)
            turn_pe(pe, 0)
            pe.wait_ge(s_ready, 1)
            pe_attn0(pe)
            turn_pe(pe, 1)
            if stop_after >= 2:
                pe_ffn(pe, F0, NT0)
                turn_pe(pe, 2)
            if stop_after >= 3:
                pe_attn1(pe)
                turn_pe(pe, 3)
            if stop_after >= 4:
                pe_ffn(pe, F1, NT1)

        @block.scalar
        def _(act):
            turn_act(act, 0)
            act_attn0(act)
            norm_act(act, 1)
            turn_act(act, 1)
            if stop_after >= 2:
                act_ffn(act, F0, NT0, True)
                norm_act(act, 2)
                turn_act(act, 2)
            if stop_after >= 3:
                act_attn1(act)
                norm_act(act, 3)
                turn_act(act, 3)
            if stop_after >= 4:
                act.wait_ge(F1["ad"], 16)
                act_ffn(act, F1, NT1, False)
                norm_act(act, 4)

        @block.gpsimd
        def _(pool):
            pool_attn0(pool)
            if stop_after >= 2:
                pool_ffn(pool, F0, NT0, True)
            if stop_after >= 3:
                pool_attn1(pool)
            if stop_after >= 4:
                pool.wait_ge(F1["ad"], 16)
                pool_ffn(pool, F1, NT1, False)

        @block.vector
        def _(dve):
            nc.vector.memset(ones, 1.0).then_inc(s_ready, 1)
            for t in range(TT):
                dve.wait_ge(s_x, 16 * TT)
                nc.vector.tensor_copy(nwt[:, 0:1], y[:, t, 0:1]).then_inc(T["fed"], 1)
                dve.wait_ge(T["fed"], t + 1)
            for t in range(TT):
                turn_dve(dve, 0, t)
            dve_attn0(dve)

            norm_dve(dve, 1, A0["yadd"], NU * KVH0)
            if stop_after >= 2:
                dve_ffn(dve, F0, NT0, True)

                norm_dve(dve, 2, F0["yadd"], TT * NT0)
            if stop_after >= 3:
                dve_attn1(dve)

                norm_dve(dve, 3, A1["yadd"], TT)
            if stop_after >= 4:
                dve.wait_ge(F1["ad"], 16)
                dve_ffn(dve, F1, NT1, False)

                norm_dve(dve, 4, F1["yadd"], TT * NT1, turns=False)


def _constants():
    i = np.arange(P)
    ident = np.eye(P, dtype=np.float32)
    neg = np.float32(NEG)
    prev = np.where(i[None, :] > i[:, None], np.float32(0), neg)
    diag = np.where(i[None, :] <= i[:, None], np.float32(0), neg)
    consts = np.concatenate([ident, prev, diag, np.zeros((P, 384), np.float32),
                             np.maximum(diag, np.float32(DROPPED))], axis=1).astype(np.float32)

    def table(inv_freq, freq_of_row):
        ang = np.arange(SEQ, dtype=np.float32)[None, :] * inv_freq[freq_of_row][:, None]
        sign = np.where(np.arange(P) < 64, np.float32(-1), np.float32(1))[:, None]
        return np.concatenate([np.cos(ang), np.sin(ang) * sign], axis=1).astype(np.float32)

    half0 = HD0 // 2
    f0 = (np.float32(10000.0) ** (-np.arange(half0, dtype=np.float32) / np.float32(half0))).astype(np.float32)
    f1 = (np.float32(1.0) / np.float32(10000.0) ** (np.arange(0, HD1, 2, dtype=np.float32) / np.float32(HD1)))
    rope0 = table(f0, np.arange(P) % half0)
    rope1 = table(f1.astype(np.float32), (np.arange(P) % 64) // 8)
    return consts, rope0, rope1


def _normal_quantile(p):
    lo, hi = -8.0, 8.0
    for _ in range(60):
        mid = 0.5 * (lo + hi)
        lo, hi = (mid, hi) if 0.5 * (1.0 + math.erf(mid / math.sqrt(2.0))) < p else (lo, mid)
    return 0.5 * (lo + hi)


def _quantiles():
    q = np.arange(P)[:, None] + P * np.arange(1, QT)[None, :] + 1.0
    z = np.vectorize(_normal_quantile)(1.0 - AIM / q)
    slope = 0.25 * np.sqrt(2 * np.pi) * np.exp(z * z / 2) / q
    one_to_16 = np.broadcast_to(np.arange(1.0, 17.0), (P, 16))
    return np.concatenate([0.5 * z, slope, np.zeros((P, 2)), one_to_16], axis=1).astype(np.float32)


def _chunks(w):
    n = w.shape[1] // P
    return w.reshape(DC, P, n, P).transpose(2, 1, 0, 3)


def _layout(i):
    wq, wk, wv = (_chunks(np.asarray(i[k])) for k in ("L0_attn_wq", "L0_attn_wk", "L0_attn_wv"))
    wo = np.asarray(i["L0_attn_wo"]).reshape(KVH0, G0, P, D).transpose(0, 2, 1, 3).reshape(KVH0, P, G0 * D)
    wq = wq.reshape(KVH0, G0, P, DC * P).transpose(0, 2, 1, 3).reshape(KVH0, P, G0 * DC * P)
    attn0 = np.concatenate([wq, wk.reshape(KVH0, P, -1), wv.reshape(KVH0, P, -1), wo], axis=2)

    def ffn(w1, w3, w2, nt):
        pad = nt * P - w1.shape[0]
        w1, w3 = (np.pad(w, ((0, pad), (0, 0))) for w in (w1, w3))
        w2 = np.pad(w2, ((0, 0), (0, pad)))
        g, u = (_chunks(w.T).reshape(nt, P, D) for w in (w1, w3))
        return np.concatenate([g, u, w2.T.reshape(nt, P, D)], axis=2)

    a = lambda n: np.asarray(i[n])
    ffn0 = np.stack([ffn(a("L0_ffn_w1"), a("L0_ffn_w3"), a("L0_ffn_w2"), NT0),
                     ffn(a("L0_ffn_mean_w1"), a("L0_ffn_mean_w3"), a("L0_ffn_mean_w2"), NT0)], axis=2).reshape(NT0, P, 2 * FCOLS)
    ffn1 = ffn(a("L1_ffn_Wg"), a("L1_ffn_Wu"), a("L1_ffn_Wd"), NT1)
    pairs = [np.stack([a(f"L0_ffn_{w}").reshape(KVH0, 2, P, MCH), a(f"L0_ffn_mean_{w}").reshape(KVH0, 2, P, MCH)], axis=3)
             for w in ("w1", "w3", "w2")]
    mean = np.stack(pairs, axis=1).reshape(KVH0 * 6, P, 2, MCH)

    def heads_last(w, n):
        return w.reshape(n // 8, 8, HD1, D).transpose(0, 2, 1, 3).reshape(n // 8 * P, D)
    q1 = _chunks(heads_last(a("L1_attn_Wq"), 32).T).transpose(1, 0, 2, 3).reshape(P, 4 * D)
    k1 = _chunks(heads_last(a("L1_attn_Wk"), 8).T).transpose(1, 0, 2, 3).reshape(P, D)
    v1 = _chunks(a("L1_attn_Wv").T).transpose(1, 0, 2, 3).reshape(P, D)
    o1 = a("L1_attn_Wo").T.reshape(KVH1, G1, HD1, D).transpose(0, 2, 1, 3).reshape(P, G1 * D)
    attn1 = np.concatenate([q1, k1, v1, o1], axis=1)

    pad = NT1 * P - INT1
    scales = [np.pad(a(n), (0, pad)).reshape(NT1, P, 1) for n in ("L1_ffn_ag", "L1_ffn_au")]
    ffn1 = np.concatenate([ffn1] + scales, axis=2)
    rows = np.broadcast_to(a("L1_ffn_ad")[None, :], (P, D))
    consts, rope0, rope1 = _constants()
    return {"x": a("L0_attn_x").reshape(TOK, D), "attn0_w": attn0, "ffn0_w": ffn0, "mean_w": mean, "attn1_w": attn1,
            "ffn1_w": ffn1, "ad_rows": rows, "quant": _quantiles(), "consts": consts, "rope0": rope0, "rope1": rope1}


STOP = 99


def kernel(**inputs):
    import concourse.bacc as _bacc
    from concourse.bass_utils import run_bass_kernel_spmd as _run

    nc = _bacc.Bacc("TRN2", target_bir_lowering=False, num_devices=1)
    arrays, args = {}, []
    for name, a in _layout(inputs).items():
        a = np.ascontiguousarray(a)
        arrays[f"in_{name}"] = a
        args.append(nc.dram_tensor(f"in_{name}", a.shape, mybir.dt.from_np(a.dtype), kind="ExternalInput").ap())
    args.append(nc.dram_tensor("out_0", (TOK, D), F32, kind="ExternalOutput").ap())
    build_kernel(nc, *args, stop_after=STOP)
    r = _run(nc, [arrays], core_ids=[0])
    return r.results[0]["out_0"].reshape(BATCH, SEQ, D)
```

```python
from contextlib import ExitStack

import math

import numpy as np
import concourse.bass as bass
from concourse import mybir

F32 = mybir.dt.float32
F32R = mybir.dt.float32r
ALU = mybir.AluOpType
ACT = mybir.ActivationFunctionType
AX = mybir.AxisListType

P = 128
D = 512
DC = D // P
BATCH, SEQ = 2, 512
TOK = BATCH * SEQ
TT = TOK // P
QT = SEQ // P
KVH0, G0, HD0 = 8, 4, 128
SCALE0 = float(HD0) ** -0.5
WQ0, WK0, WV0, WO0 = 0, 2048, 2560, 3072
WCOLS = 5120
KVH1, G1, HD1 = 8, 4, 16
SCALE1 = 0.25
TOPK = 128
RESOLVED = P * 16
WINDOW = 15
AIM = TOPK - (WINDOW + 1) // 2
ROUNDS = 4
PRIOR = 8.0
ACC_OF = (0, 1, 0, 2)
INT0, INT1 = 1792, 1376
NT0 = INT0 // P
NT1 = -(-INT1 // P)
FCOLS = 3 * D
MCH = 448
NEG = -3.4028234663852886e38
DROPPED = -1.6e38
TAKEN = -3.0e38
EPS = 1e-5
MAGIC_PASSES = ((0, 0), (0, 1), (1, 0))


def build_kernel(nc, x, attn0_w, ffn0_w, mean_w, attn1_w, ffn1_w, ad_rows, quant, consts, rope0, rope1, out,
                 stop_after=99):
    ctx = ExitStack()
    with ctx:
        def sem(name):
            return ctx.enter_context(nc.semaphore(name))

        with nc.sbuf_tensor("XT", [P, 8192], F32R) as XT:
            pass
        XT1 = ctx.enter_context(nc.sbuf_tensor("XT1", [P, 4096], F32R))
        SG = ctx.enter_context(nc.sbuf_tensor("SG", [P, 8192], mybir.dt.bfloat16))
        AF = ctx.enter_context(nc.sbuf_tensor("AF", [P, 19300], F32))
        with nc.sbuf_tensor("AR", [P, 25600], F32R) as AR:
            pass
        AR1 = ctx.enter_context(nc.sbuf_tensor("AR1", [P, 10240], F32R))
        BF = ctx.enter_context(nc.sbuf_tensor("BF", [P, 15360], F32))
        PS = ctx.enter_context(nc.psum_tensor("PS", [P, 8, 512], F32))
        scr = nc.dram_tensor("rope_scratch", (BATCH, 5, 2, P, SEQ), F32, kind="Internal").ap()

        def f32(view):
            return view.bitcast(F32)

        y = AF[:, 0:4096].rearrange("p (t d) -> p t d", t=TT)
        ident = AF[:, 4096:4224]
        eps = AF[:, 4224:4225]
        zeros = AF[:, 4225:4226]
        sums = AF[:, 4228:4231]
        coeff = AF[:, 4232:4235]
        part = AF[:, 4236:4242]
        stats = AF[:, 4244:4244 + 48].rearrange("p (t s) -> p t s", t=TT)
        mv = AF[:, 4292:4308].rearrange("p (t s) -> p t s", t=TT)
        var = AF[:, 4308:4316]
        sd = AF[:, 4316:4324]
        rstd = AF[:, 4324:4332]
        nwt = AF[:, 4332:4340]
        negmax = AF[:, 4340:4356]
        rsum = AF[:, 4356:4372]
        rinv = AF[:, 4372:4388]
        top8 = AF[:, 4388:4396]
        ones = AF[:, 4396:4524]
        base = 4608
        raw = AF[:, base:base + WCOLS]
        o = base + WCOLS
        ctab, stab = AF[:, o:o + 512], AF[:, o + 512:o + 1024]
        mask0 = AF[:, o + 1024:o + 1280]
        o += 1280
        Sm = AF[:, o:o + 2048].rearrange("p (r h k) -> p r h k", r=2, h=4)
        o += 2048
        qs = AF[:, o:o + 1024].rearrange("p (r k) -> p r k", r=2)
        tcos, rot = AF[:, o + 1024:o + 1536], AF[:, o + 1536:o + 2048]
        vtmp = AF[:, o + 2048:o + 2560]
        mch = AF[:, o + 2560:o + 2560 + 4 * MCH].rearrange("p (r w k) -> p r w k", r=2, w=2)
        assert o + 2560 + 4 * MCH <= 19300
        raww = AF[:, base:base + 4 * FCOLS].rearrange("p (r w k) -> p r w k", r=2, w=2)
        raww_flat = AF[:, base:base + 4 * FCOLS].rearrange("p (r k) -> p r k", r=2)
        scale_g, scale_u = raww[:, :, 1, 0:1], raww[:, :, 1, 1:2]
        o = base + 4 * FCOLS
        sg = AF[:, o:o + 1024].rearrange("p (b k) -> p b k", b=2)
        hh = AF[:, o + 1024:o + 2048].rearrange("p (b k) -> p b k", b=2)
        adrow = AF[:, o + 2048:o + 2560]
        rope1_at = base + WCOLS
        xT = XT[:, 0:8192].rearrange("p (s c k) -> p s c k", s=2, c=DC)
        Wq = AR[:, 0:4096].rearrange("p (s h c k) -> p s h c k", s=2, h=4, c=DC)
        Wk = AR[:, 4096:5120].rearrange("p (s c k) -> p s c k", s=2, c=DC)
        Wv = AR[:, 5120:6144].rearrange("p (s c k) -> p s c k", s=2, c=DC)
        Wo = AR[:, 6144:10240].rearrange("p (s h k) -> p s h k", s=2, h=4)
        qT = AR[:, 10240:18432].rearrange("p (r s h k) -> p r s h k", r=2, s=2, h=4)
        kT = AR[:, 18432:20480].rearrange("p (r s k) -> p r s k", r=2, s=2)
        V = AR[:, 20480:22528].rearrange("p (r s j k) -> p r s j k", r=2, s=2, j=QT)
        PT = AR[:, 22528:24576].rearrange("p (s j k) -> p s j k", s=2, j=2)
        OT = AR[:, 24576:25600].rearrange("p (s h k) -> p s h k", s=2, h=4)
        W13 = AR[:, 0:4096].rearrange("p (r s m c k) -> p r s m c k", r=2, s=2, m=2, c=DC)
        W2 = AR[:, 4096:6144].rearrange("p (r s k) -> p r s k", r=2, s=2)
        hT = AR[:, 6144:10240].rearrange("p (r s k) -> p r s k", r=2, s=2)
        W1 = {"q": AR1[:, 0:4096].rearrange("p (s h c k) -> p s h c k", s=2, h=4, c=DC),
              "k": AR1[:, 4096:5120].rearrange("p (s c k) -> p s c k", s=2, c=DC),
              "v": AR1[:, 5120:6144].rearrange("p (s c k) -> p s c k", s=2, c=DC),
              "o": AR1[:, 6144:10240].rearrange("p (s h k) -> p s h k", s=2, h=4)}
        qst = XT1.rearrange("p (r h k) -> p r h k", r=2, h=16)
        sgn = SG.rearrange("p (h k) -> p h k", h=16)
        kst = AR1[:, 0:4096].rearrange("p (h k) -> p h k", h=KVH1)
        OT1 = AR1[:, 4096:5120].rearrange("p (s h k) -> p s h k", s=2, h=4)
        ident_r, mask_r = AR1[:, 5120:5248], AR1[:, 5248:5376]
        S1 = [AF[:, base:base + 8192].rearrange("p (h k) -> p h k", h=16),
              BF[:, 0:8192].rearrange("p (h k) -> p h k", h=16)]
        rq = BF[:, 0:2048].bitcast(F32R).rearrange("p (r s k) -> p r s k", r=2, s=2)
        Vz = BF[:, 8192:12800].rearrange("p (j k) -> p j k", j=QT)
        X1 = BF[:, 12800:13824].rearrange("p (r k) -> p r k", r=2)
        o = base + 8192
        P1 = AF[:, o:o + 4096].rearrange("p (r h k) -> p r h k", r=2, h=4)
        PT1 = AF[:, o + 4096:o + 5120].rearrange("p (r k) -> p r k", r=2)
        Vc = AF[:, o + 5120:o + 6144].rearrange("p (t k) -> p t k", t=TT)
        assert o + 6144 <= 19300
        small = BF[:, 13824:15360]
        names16 = ("nslope", "step", "drop", "scaled", "square", "err", "spread", "msum", "mdiff", "vsum")
        st = {n: small[:, 16 * k:16 * k + 16] for k, n in enumerate(names16)}
        o = 16 * len(names16)
        acc = small[:, o:o + 48].rearrange("p (r h) -> p r h", r=3)
        o += 48
        for n in ("nthr", "rmax", "nmax", "tau"):
            st[n] = small[:, o:o + 32].rearrange("p (r h) -> p r h", r=2)
            o += 32
        stat6 = small[:, o:o + 96].rearrange("p (h s) -> p h s", h=16)
        ztab = small[:, o + 96:o + 102]
        iota16 = small[:, o + 104:o + 120]
        best = small[:, o + 128:o + 384].rearrange("p (h s) -> p h s", h=16)
        hit = small[:, o + 384:o + 640].rearrange("p (h s) -> p h s", h=16)[:, :, 0:WINDOW]
        val = small[:, o + 640:o + 896].rearrange("p (h s) -> p h s", h=16)[:, :, 0:WINDOW]
        flag_row = small[:, o + 896:o + 897]
        flag_int = small[0:1, o + 897:o + 898].bitcast(mybir.dt.int32)
        assert o + 898 <= 1280
        junk = [AF[:, base + 14336:base + 14592].bitcast(mybir.dt.bfloat16), small[:, 1280:1536].bitcast(mybir.dt.bfloat16)]
        rsum1, rinv1 = AF[:, 4528:4544], AF[:, 4544:4560]

        s_const = sem("s_const")
        s_ready = sem("s_ready")
        s_x = sem("s_x")
        s_out = sem("s_out")

        def wait(eng, s, v):
            if isinstance(v, int) and v <= 0:
                return
            eng.wait_ge(s, v)

        def mm3(dst, lhs, rhs, n, flags=True, more=False, first=True):
            k = 0
            last = None
            for c in range(n):
                for a, m in MAGIC_PASSES:
                    last = nc.tensor.matmul(dst, lhs(a, c), rhs(m, c), start=(first and k == 0),
                                            stop=(k == 3 * n - 1 and not more))
                    k += 1
            return last

        def names(tag, *ns):
            return {n: sem(f"{tag}_{n}") for n in ns}

        def turn_pe(pe, k):
            for t in range(TT):
                pe.wait_ge(T["fed"], TT * k + t + 1)
                wait(pe, T["low"], TT * k + t - 1 if t >= 2 else TT * k)
                for c in range(DC):
                    last = nc.tensor.transpose(PS[:, t % 2, c * P:(c + 1) * P], y[:, t, c * P:(c + 1) * P], ident)
                last.then_inc(T["turned"], 1)
            pe.wait_ge(T["low"], TT * (k + 1))

        def turn_act(act, k):
            for t in range(TT):
                act.wait_ge(T["turned"], TT * k + t + 1)
                nc.scalar.activation(xT[:, 0, :, t * P:(t + 1) * P],
                                     PS[:, t % 2, :].rearrange("p (c k) -> p c k", c=DC),
                                     ACT.Copy).then_inc(T["high"], 1)

        def turn_dve(dve, k, t):
            dve.wait_ge(T["high"], TT * k + t + 1)
            nc.vector.tensor_tensor(xT[:, 1, :, t * P:(t + 1) * P],
                                    PS[:, t % 2, :].rearrange("p (c k) -> p c k", c=DC),
                                    f32(xT[:, 0, :, t * P:(t + 1) * P]), ALU.subtract).then_inc(T["low"], 1)

        def norm_stats(dve, k, place, t, sem_added, n_added):
            dve.wait_ge(sem_added, n_added)
            nc.vector.bn_stats(stats[:, t, :], y[:, t, :]).then_inc(N["stats"], 1)
            dve.wait_ge(N["stats"], TT * (k - 1) + place + 1)
            nc.vector.bn_aggr(mv[:, t, :], stats[:, t, :]).then_inc(N["aggr"], 1)

        def norm_dve(dve, k, turns=True):
            a, v = TT * (k - 1), 6 * (k - 1)
            dve.wait_ge(N["aggr"], a + TT)
            nc.vector.tensor_scalar(var, mv[:, :, 1], EPS, None, ALU.add).then_inc(N["var"], 1)
            dve.wait_ge(N["sqrt"], k)
            nc.vector.reciprocal(rstd, sd).then_inc(N["var"], 1)
            dve.wait_ge(N["var"], v + 2)
            nc.vector.tensor_tensor(nwt, rstd, rstd, ALU.mult).then_inc(N["var"], 1)
            dve.wait_ge(N["var"], v + 3)
            nc.vector.tensor_tensor(nwt, nwt, var, ALU.mult).then_inc(N["var"], 1)
            dve.wait_ge(N["var"], v + 4)
            nc.vector.tensor_scalar(nwt, nwt, -0.5, 1.5, ALU.mult, ALU.add).then_inc(N["var"], 1)
            dve.wait_ge(N["var"], v + 5)
            nc.vector.tensor_tensor(rstd, rstd, nwt, ALU.mult).then_inc(N["var"], 1)
            dve.wait_ge(N["var"], v + 6)
            for t in range(TT):
                nc.vector.tensor_scalar(y[:, t, :], y[:, t, :], mv[:, t, 0:1], rstd[:, t:t + 1],
                                        ALU.subtract, ALU.mult).then_inc(T["fed"], 1)
                if t >= 1 and turns:
                    turn_dve(dve, k, t - 1)
            if turns:
                turn_dve(dve, k, TT - 1)

        def norm_act(act, k):
            act.wait_ge(N["var"], 6 * (k - 1) + 1)
            nc.scalar.activation(sd, var, ACT.Sqrt).then_inc(N["sqrt"], 1)

        T = names("turn", "fed", "turned", "high", "low")
        N = names("norm", "stats", "aggr", "var", "sqrt")

        A0 = names("a0", "raw_qkv", "raw_wo", "wq_hi", "wq_lo", "wk_hi", "wk_lo", "wv_hi", "wv_lo", "wo_hi", "wo_lo",
                   "scores", "masked", "maxed", "negmax", "exp", "rinv", "pnorm", "turned", "pt_hi", "pt_lo", "pv",
                   "o_hi", "o_lo", "yproj", "yadd", "vproj", "vcopy", "vturned", "v_hi", "v_lo",
                   "mean_in0", "mean_in1", "mean_d", "mean_abs", "mean_sum", "coeff_ps", "coeff")
        R0 = names("r0", "proj", "swap", "cos", "sin", "rot", "hi", "lo")
        NU = BATCH * QT

        def head_item(h):
            return 0 if h == 0 else h + 1

        def w_piece(kind, h, layer1=False):
            if layer1:
                src, dst = w_piece(kind, h)
                return src, W1["q"][:, :, h] if kind == "q" else W1[kind]
            if kind == "q":
                return raw[:, WQ0 + h * 512:WQ0 + (h + 1) * 512].rearrange("p (c k) -> p c k", c=DC), Wq[:, :, h]
            if kind == "k":
                return raw[:, WK0:WK0 + 512].rearrange("p (c k) -> p c k", c=DC), Wk
            if kind == "v":
                return raw[:, WV0:WV0 + 512].rearrange("p (c k) -> p c k", c=DC), Wv
            return raw[:, WO0:WO0 + 2048].rearrange("p (h k) -> p h k", h=4), Wo

        def split_hi(act, A, kind, g, h=0):
            src, dst = w_piece(kind, h, A is not A0)
            wait(act, A["raw_wo"] if kind == "o" else A["raw_qkv"], 16 * (g + 1))
            if A is A0:
                if kind == "q":
                    wait(act, R0["proj"], 10 * g - 5 + head_item(h) + 1)
                elif kind == "k":
                    wait(act, R0["proj"], 10 * g - 5 + 1 + 1)
                elif kind == "v":
                    wait(act, A0["vproj"], 2 * g)
                else:
                    wait(act, A0["yproj"], NU * g)
            nc.scalar.activation(dst[:, 0], src, ACT.Copy).then_inc(A[f"w{kind}_hi"], 1)

        def split_lo(pool, A, kind, g, h=0):
            src, dst = w_piece(kind, h, A is not A0)
            pool.wait_ge(A[f"w{kind}_hi"], (4 * g + h if kind == "q" else g) + 1)
            nc.gpsimd.tensor_tensor(dst[:, 1], src, f32(dst[:, 0]), ALU.subtract).then_inc(A[f"w{kind}_lo"], 1)

        PIECES = {1: [("o", 0, 0)], 2: [("q", 0, 1), ("k", 0, 1)], 3: [("q", 1, 1), ("v", 0, 1)],
                  4: [("q", 2, 1)], 5: [("q", 3, 1)]}

        def groups(eng, body):
            body(0, True, False)
            with eng.Fori(1, KVH0 - 1) as g:
                body(g, False, False)
            body(KVH0 - 1, False, True)

        def items0(bb, j):
            its = [(5 * bb + head_item(j), "q", j)]
            if j == 0:
                its.append((5 * bb + 1, "k", 0))
            return its

        def rope_act1(act, r, src, slot):
            act.wait_ge(R0["proj"], r + 1)
            wait(act, R0["rot"], r - 1)
            nc.scalar.activation(qs[0:64, slot, :], src[64:128, :], ACT.Copy)
            nc.scalar.activation(qs[64:128, slot, :], src[0:64, :], ACT.Copy).then_inc(R0["swap"], 1)

        def slot_of(k, b, j):
            return (5 * b + (1 if k == "k" else head_item(j))) % 2

        def src0(k):
            return PS[:, 6, :] if k == "q" else PS[:, 7, :]

        def dst0(k, b, j, s):
            return qT[:, b, s, j, :] if k == "q" else kT[:, b, s, :]

        def pe_proj_item(pe, g, bb, b, k, j, r):
            if k == "q":
                pe.wait_ge(A0["wq_lo"], 4 * g + j + 1)
                if j == 0:
                    wait(pe, R0["swap"], r)
                    wait(pe, R0["cos"], r)
                elif j == 1:
                    wait(pe, R0["swap"], r - 1)
                    wait(pe, R0["cos"], r - 1)
                else:
                    wait(pe, R0["swap"], r)
                    wait(pe, R0["cos"], r)
            else:
                pe.wait_ge(A0["wk_lo"], g + 1)
                wait(pe, A0["v_lo"], bb)
            w = Wq[:, :, j] if k == "q" else Wk
            mm3(src0(k), lambda a, c: w[:, a, c, :], lambda m, c: xT[:, m, c, b * SEQ:(b + 1) * SEQ], DC)\
                .then_inc(R0["proj"], 1)

        def pe_v(pe, g, bb, b, r):
            pe.wait_ge(A0["wv_lo"], g + 1)
            pe.wait_ge(R0["swap"], 5 * bb + 2)
            pe.wait_ge(R0["cos"], 5 * bb + 2)
            mm3(PS[:, 7, :], lambda a, c: Wv[:, a, c, :], lambda m, c: xT[:, m, c, b * SEQ:(b + 1) * SEQ], DC)\
                .then_inc(A0["vproj"], 1)

        def pe_vturn(pe, bb):
            pe.wait_ge(A0["vcopy"], bb + 1)
            for j in range(QT):
                last = nc.tensor.transpose(PS[:, 7, j * P:(j + 1) * P], vtmp[:, j * P:(j + 1) * P], ident)
            last.then_inc(A0["vturned"], 1)

        def pe_attn0(pe):
            def body(g, first, last_group):
                for u in range(NU):
                    b, i = u // QT, u % QT
                    n = NU * g + u
                    bb = 2 * g + b
                    pe.wait_ge(R0["lo"], 5 * bb + 5)
                    wait(pe, A0["masked"], n)
                    lo = 1 if i == 0 else 0
                    for h in range(G0):
                        dst = PS[:, h // 2, (h % 2) * 256 + lo * P:(h % 2) * 256 + 256]
                        last = mm3(dst, lambda a, c: qT[:, b, a, h, i * P:(i + 1) * P],
                                   lambda m, c: kT[:, b, m, (i - 1 + lo) * P:(i + 1) * P], 1)
                    last.then_inc(A0["scores"], 1)
                    if not (first and u == 0):
                        turn_p(n - 1, (u - 1) % QT)
                    nb, j = (b + 1) % 2, i
                    ng = g if b == 0 else g + 1
                    has_next = not (last_group and b == 1)
                    if has_next:
                        pe_proj_item(pe, ng, bb + 1, nb, "q", j, 5 * (bb + 1) + head_item(j))
                    if not (first and u < 2):
                        oproj(n - 2, g if u > 1 else g - 1)
                    if not (first and u == 0):
                        pv(n - 1, (u - 1) % QT, ((u - 1) // QT) % 2)
                    if has_next:
                        if j == 0:
                            pe_proj_item(pe, ng, bb + 1, nb, "k", 0, 5 * (bb + 1) + 1)
                        if j == 1:
                            pe_v(pe, ng, bb + 1, nb, 0)
                        if j == 2:
                            pe_vturn(pe, bb + 1)

            def turn_p(n, i):
                pe.wait_ge(A0["pnorm"], n + 1)
                for kb in range(1 if i == 0 else 0, 2):
                    for h in range(G0):
                        last = nc.tensor.transpose(PS[:, 2 + kb, h * P:(h + 1) * P],
                                                   Sm[:, par2(i), h, kb * P:(kb + 1) * P], ident)
                last.then_inc(A0["turned"], 1)

            def par2(i):
                return i % 2

            def pv(n, i, b):
                pe.wait_ge(A0["pt_lo"], n + 1)
                wait(pe, A0["o_lo"], n)
                k0 = 1 if i == 0 else 0
                mm3(PS[:, 4, :], lambda a, c: V[:, b, a, i - 1 + k0 + c, :], lambda m, c: PT[:, m, k0 + c, :],
                    2 - k0).then_inc(A0["pv"], 1)

            def oproj(n, g):
                pe.wait_ge(A0["wo_lo"], g + 1)
                pe.wait_ge(A0["o_lo"], n + 1)
                wait(pe, A0["yadd"], n)
                mm3(PS[:, 5, :], lambda a, c: OT[:, a, c, :], lambda m, c: Wo[:, m, c, :], G0)\
                    .then_inc(A0["yproj"], 1)

            for j in range(G0):
                pe_proj_item(pe, 0, 0, 0, "q", j, head_item(j))
                if j == 0:
                    pe_proj_item(pe, 0, 0, 0, "k", 0, 1)
                if j == 1:
                    pe_v(pe, 0, 0, 0, 0)
                if j == 2:
                    pe_vturn(pe, 0)
            pe.wait_ge(A0["v_lo"], 1)
            groups(pe, body)
            n = NU * KVH0
            turn_p(n - 1, QT - 1)
            oproj(n - 2, KVH0 - 1)
            pv(n - 1, QT - 1, 1)
            oproj(n - 1, KVH0 - 1)
            pe.wait_ge(A0["mean_sum"], 6 * KVH0 + 1)
            nc.tensor.matmul(PS[:, 6, 0:3], ones, sums, start=True, stop=True).then_inc(A0["coeff_ps"], 1)

        def act_attn0(act):
            def rope_hi(r, k, b, j):
                act.wait_ge(R0["rot"], r + 1)
                nc.scalar.activation(dst0(k, b, j, 0), rot, ACT.Copy).then_inc(R0["hi"], 1)

            def vcopy(bb):
                act.wait_ge(A0["vproj"], bb + 1)
                nc.scalar.activation(vtmp, PS[:, 7, :], ACT.Copy).then_inc(A0["vcopy"], 1)

            def v_hi(bb, b):
                act.wait_ge(A0["vturned"], bb + 1)
                nc.scalar.activation(V[:, b, 0], PS[:, 7, :].rearrange("p (j k) -> p j k", j=QT), ACT.Copy)\
                    .then_inc(A0["v_hi"], 1)

            def pt_hi(n, i):
                act.wait_ge(A0["turned"], n + 1)
                k0 = 1 if i == 0 else 0
                nc.scalar.activation(PT[:, 0, k0:2, :], PS[:, 2 + k0:4, :], ACT.Copy).then_inc(A0["pt_hi"], 1)

            def o_hi(n):
                act.wait_ge(A0["pv"], n + 1)
                nc.scalar.activation(OT[:, 0], PS[:, 4, :].rearrange("p (h k) -> p h k", h=4), ACT.Copy)\
                    .then_inc(A0["o_hi"], 1)

            def mean_abs(g, s):
                act.wait_ge(A0["mean_d"], 6 * g + s + 1)
                wait(act, A0["mean_sum"], 6 * (g - 1) + s + 1 + 1)
                nc.scalar.activation(mch[:, s % 2, 0, :], mch[:, s % 2, 0, :], ACT.Abs,
                                     accum_out=part[:, s:s + 1]).then_inc(A0["mean_abs"], 1)

            for h in range(G0):
                split_hi(act, A0, "q", 0, h)
            for k in ("k", "v", "o"):
                split_hi(act, A0, k, 0)
            for j in range(G0):
                for r, k, h in items0(0, j):
                    rope_act1(act, r, src0(k), slot_of(k, 0, j))
                    rope_hi(r, k, 0, j)
                if j == 1:
                    vcopy(0)
                if j == 2:
                    v_hi(0, 0)

            def body(g, first, last_group):
                for u in range(NU):
                    b, i = u // QT, u % QT
                    n = NU * g + u
                    bb = 2 * g + b
                    nb, j = (b + 1) % 2, i
                    has_next = not (last_group and b == 1)
                    if not (first and u == 0):
                        pt_hi(n - 1, (u - 1) % QT)
                    its = items0(bb + 1, j) if has_next else []
                    if its:
                        rope_act1(act, its[0][0], src0("q"), slot_of("q", nb, j))
                    if 1 <= u < 7:
                        mean_abs(g, u - 1)
                    act.wait_ge(A0["negmax"], n + 1)
                    k0 = 1 if i == 0 else 0
                    for h in range(G0):
                        sl = Sm[:, u % 2, h, k0 * P:256]
                        last = nc.scalar.activation(sl, sl, ACT.Exp, bias=negmax[:, h:h + 1], scale=SCALE0,
                                                    accum_out=rsum[:, h:h + 1])
                    last.then_inc(A0["exp"], 1)
                    if its:
                        rope_hi(its[0][0], "q", nb, j)
                    if not (first and u == 0):
                        o_hi(n - 1)
                    if len(its) > 1:
                        rope_act1(act, its[1][0], src0("k"), slot_of("k", nb, j))
                        rope_hi(its[1][0], "k", nb, j)
                    if has_next and j == 1:
                        vcopy(bb + 1)
                    if has_next and j == 2:
                        v_hi(bb + 1, nb)
                    for kind, h, ahead in PIECES.get(u, []):
                        if (ahead and last_group) or (first and not ahead):
                            continue
                        split_hi(act, A0, kind, g + ahead, h)

            groups(act, body)
            n = NU * KVH0
            pt_hi(n - 1, QT - 1)
            o_hi(n - 1)

        def pool_attn0(pool):
            def rope_sin(r, slot):
                pool.wait_ge(R0["swap"], r + 1)
                nc.gpsimd.tensor_tensor(qs[:, slot, :], qs[:, slot, :], stab, ALU.mult).then_inc(R0["sin"], 1)

            def pnorm(n, i):
                pool.wait_ge(A0["rinv"], n + 1)
                k0 = 1 if i == 0 else 0
                sl = Sm[:, i % 2, :, k0 * P:256]
                nc.gpsimd.tensor_tensor(sl, sl, rinv[:, 0:4].unsqueeze(2).to_broadcast([P, G0, (2 - k0) * P]),
                                        ALU.mult).then_inc(A0["pnorm"], 1)

            def mean(g, s):
                pool.wait_ge(A0[f"mean_in{s % 2}"], 16 * (3 * g + s // 2 + 1))
                nc.gpsimd.tensor_tensor(mch[:, s % 2, 0, :], mch[:, s % 2, 0, :], mch[:, s % 2, 1, :],
                                        ALU.subtract).then_inc(A0["mean_d"], 1)

            def mean_add(g, s):
                m = s // 2
                pool.wait_ge(A0["mean_abs"], 6 * g + s + 1)
                pool.wait_ge(A0["mean_sum"], 6 * g + s + 1)
                nc.gpsimd.tensor_tensor(sums[:, m:m + 1], sums[:, m:m + 1], part[:, s:s + 1], ALU.add)\
                    .then_inc(A0["mean_sum"], 1)

            nc.gpsimd.memset(sums, 0.0).then_inc(A0["mean_sum"], 1)
            pool.wait_ge(s_const, CONST_DMAS * 16)
            for h in range(G0):
                split_lo(pool, A0, "q", 0, h)
            for k in ("k", "v", "o"):
                split_lo(pool, A0, k, 0)
            for j in range(G0):
                for r, k, h in items0(0, j):
                    rope_sin(r, slot_of(k, 0, j))

            def body(g, first, last_group):
                for u in range(NU):
                    b, i = u // QT, u % QT
                    n = NU * g + u
                    bb = 2 * g + b
                    nb, j = (b + 1) % 2, i
                    has_next = not (last_group and b == 1)
                    its = items0(bb + 1, j) if has_next else []
                    if its:
                        rope_sin(its[0][0], slot_of("q", nb, j))
                    pnorm(n, i)
                    if len(its) > 1:
                        rope_sin(its[1][0], slot_of("k", nb, j))
                    for kind, h, ahead in PIECES.get(u, []):
                        if (ahead and last_group) or (first and not ahead):
                            continue
                        split_lo(pool, A0, kind, g + ahead, h)
                    if u < 6:
                        mean(g, u)
                    if 1 <= u < 7:
                        mean_add(g, u - 1)

            groups(pool, body)

        def dve_attn0(dve):
            def rope_cos(r, k):
                dve.wait_ge(R0["swap"], r + 1)
                wait(dve, R0["rot"], r)
                nc.vector.tensor_tensor(tcos, src0(k), ctab, ALU.mult).then_inc(R0["cos"], 1)

            def rope_rot(r, slot):
                dve.wait_ge(R0["sin"], r + 1)
                dve.wait_ge(R0["cos"], r + 1)
                wait(dve, R0["hi"], r)
                wait(dve, R0["lo"], r)
                nc.vector.tensor_tensor(rot, tcos, qs[:, slot, :], ALU.add).then_inc(R0["rot"], 1)

            def rope_lo(r, k, b, j):
                dve.wait_ge(R0["hi"], r + 1)
                nc.vector.tensor_tensor(dst0(k, b, j, 1), rot, f32(dst0(k, b, j, 0)), ALU.subtract)\
                    .then_inc(R0["lo"], 1)

            def v_lo(bb, b):
                dve.wait_ge(A0["v_hi"], bb + 1)
                nc.vector.tensor_tensor(V[:, b, 1], PS[:, 7, :].rearrange("p (j k) -> p j k", j=QT),
                                        f32(V[:, b, 0]), ALU.subtract).then_inc(A0["v_lo"], 1)

            def yadd(n, t):
                dve.wait_ge(A0["yproj"], n + 1)
                nc.vector.tensor_tensor(y[:, t, :], PS[:, 5, :], y[:, t, :], ALU.add).then_inc(A0["yadd"], 1)

            def pt_lo(n, i):
                dve.wait_ge(A0["pt_hi"], n + 1)
                k0 = 1 if i == 0 else 0
                nc.vector.tensor_tensor(PT[:, 1, k0:2, :], PS[:, 2 + k0:4, :], f32(PT[:, 0, k0:2, :]),
                                        ALU.subtract).then_inc(A0["pt_lo"], 1)

            def o_lo(n):
                dve.wait_ge(A0["o_hi"], n + 1)
                nc.vector.tensor_tensor(OT[:, 1], PS[:, 4, :].rearrange("p (h k) -> p h k", h=4), f32(OT[:, 0]),
                                        ALU.subtract).then_inc(A0["o_lo"], 1)

            for j in range(G0):
                for r, k, h in items0(0, j):
                    rope_cos(r, k)
                    rope_rot(r, slot_of(k, 0, j))
                    rope_lo(r, k, 0, j)
                if j == 2:
                    v_lo(0, 0)

            def body(g, first, last_group):
                for u in range(NU):
                    b, i = u // QT, u % QT
                    n = NU * g + u
                    bb = 2 * g + b
                    nb, j = (b + 1) % 2, i
                    has_next = not (last_group and b == 1)
                    its = items0(bb + 1, j) if has_next else []
                    if not (first and u < 3):
                        yadd(n - 3, (u - 3) % NU)
                    if last_group and u >= 3:
                        norm_stats(dve, 1, u - 3, u - 3, A0["yadd"], n - 2)
                    k0 = 1 if i == 0 else 0
                    dve.wait_ge(A0["scores"], n + 1)
                    src = PS[:, 0:2, :].rearrange("p a (h k) -> p (a h) k", h=2)[:, :, k0 * P:256]
                    nc.vector.tensor_tensor(Sm[:, u % 2, :, k0 * P:256], src,
                                            mask0[:, k0 * P:256].unsqueeze(1).to_broadcast([P, G0, (2 - k0) * P]),
                                            ALU.add).then_inc(A0["masked"], 1)
                    if not (first and u == 0):
                        pt_lo(n - 1, (u - 1) % QT)
                    dve.wait_ge(A0["masked"], n + 1)
                    wait(dve, A0["exp"], n)
                    nc.vector.tensor_reduce(negmax[:, 0:4], Sm[:, u % 2, :, k0 * P:256], AX.X, ALU.max)\
                        .then_inc(A0["maxed"], 1)
                    if its:
                        rope_cos(its[0][0], "q")
                    dve.wait_ge(A0["maxed"], n + 1)
                    nc.vector.tensor_scalar(negmax[:, 0:4], negmax[:, 0:4], -SCALE0, None, ALU.mult)\
                        .then_inc(A0["negmax"], 1)
                    if its:
                        rope_rot(its[0][0], slot_of("q", nb, j))
                    dve.wait_ge(A0["exp"], n + 1)
                    wait(dve, A0["pnorm"], n)
                    nc.vector.reciprocal(rinv[:, 0:4], rsum[:, 0:4]).then_inc(A0["rinv"], 1)
                    if its:
                        rope_lo(its[0][0], "q", nb, j)
                    if not (first and u == 0):
                        o_lo(n - 1)
                    if len(its) > 1:
                        rope_cos(its[1][0], "k")
                        rope_rot(its[1][0], slot_of("k", nb, j))
                        rope_lo(its[1][0], "k", nb, j)
                    if has_next and j == 2:
                        v_lo(bb + 1, nb)

            groups(dve, body)
            n = NU * KVH0
            yadd(n - 3, NU - 3)
            pt_lo(n - 1, QT - 1)
            norm_stats(dve, 1, NU - 3, NU - 3, A0["yadd"], n - 2)
            yadd(n - 2, NU - 2)
            o_lo(n - 1)
            norm_stats(dve, 1, NU - 2, NU - 2, A0["yadd"], n - 1)
            yadd(n - 1, NU - 1)
            norm_stats(dve, 1, NU - 1, NU - 1, A0["yadd"], n)
            dve.wait_ge(A0["coeff_ps"], 1)
            nc.vector.tensor_scalar(coeff, PS[:, 6, 0:3], 1.0 / (INT0 * D), None, ALU.mult).then_inc(A0["coeff"], 1)

        def sp_attn0(sp):
            def mean(g, s):
                wait(sp, A0["mean_abs"], 6 * g + s - 1)
                sp.dma_start(mch[:, s % 2], mean_w[slice_at(6 * g + s)].rearrange("o p w k -> p (o w) k"))\
                    .then_inc(A0[f"mean_in{s % 2}"], 16)

            def slice_at(v):
                return bass.ds(v, 1)

            def weights(g):
                wait(sp, A0["wq_lo"], 4 * g)
                wait(sp, A0["wk_lo"], g)
                wait(sp, A0["wv_lo"], g)
                sp.dma_start(raw[:, 0:WO0], attn0_w[slice_at(g), :, 0:WO0].rearrange("o p k -> p (o k)"))\
                    .then_inc(A0["raw_qkv"], 16)
                wait(sp, A0["wo_lo"], g)
                sp.dma_start(raw[:, WO0:WCOLS], attn0_w[slice_at(g), :, WO0:WCOLS].rearrange("o p k -> p (o k)"))\
                    .then_inc(A0["raw_wo"], 16)

            weights(0)

            def body(g, first, last_group):
                mean(g, 0)
                mean(g, 1)
                if not last_group:
                    weights(g + 1)
                for s in range(2, 6):
                    mean(g, s)

            groups(sp, body)

        def ffn_sems(tag):
            return names(tag, "raw0", "raw1", "d", "sign", "w", "w13_hi", "w13_lo", "w2_hi", "w2_lo", "gate", "silu", "h",
                         "h_hi", "h_lo", "down", "yadd", "ad")

        F0, F1 = ffn_sems("f0"), ffn_sems("f1")

        def tiles(eng, nt, body):
            body(0, 0, True)
            body(1, 1, False)
            body(2, 0, False)
            pairs = (nt - 1) // 2
            with eng.Fori(1, pairs) as p:
                body(2 * p + 1, 1, False)
                body(2 * p + 2, 0, False)
            if (nt - 1) % 2:
                body(nt - 1, (nt - 1) % 2, False)

        def sp_ffn(sp, F, nt, wdram, diff, before):
            before(sp)

            def load(j, s, first):
                if not first:
                    if diff:
                        wait(sp, F["w2_lo"], j - 1)
                    else:
                        wait(sp, F["h_lo"], 2 * (j - 1))
                sp.dma_start(raww_flat[:, s, 0:wdram.shape[2]], wdram[bass.ds(j, 1)].rearrange("o p k -> p (o k)"))\
                    .then_inc(F[f"raw{s}"], 16)

            load(0, 0, True)
            load(1, 1, True)
            pairs = (nt - 2) // 2
            with sp.Fori(1, 1 + pairs) as p:
                load(2 * p, 0, False)
                load(2 * p + 1, 1, False)
            if nt % 2:
                load(nt - 1, 0, False)

        def pool_ffn(pool, F, nt, diff):
            def loaded(pool, j, s):
                n = 8 * (j + 2 - s)
                pool.wait_ge(F[f"raw{s}"], n)

            def prep(j, s):
                if diff:
                    loaded(pool, j, s)
                    nc.gpsimd.tensor_tensor(raww[:, s, 0], raww[:, s, 0], raww[:, s, 1], ALU.subtract)\
                        .then_inc(F["d"], 1)
                else:
                    loaded(pool, j, s)
                    nc.gpsimd.tensor_tensor(raww[:, s, 0, 1024:1536], raww[:, s, 0, 1024:1536], adrow, ALU.mult)\
                        .then_inc(F["w"], 1)

            def w13_lo(j, s):
                pool.wait_ge(F["w13_hi"], j + 1)
                nc.gpsimd.tensor_tensor(W13[:, s, 1].rearrange("p m c k -> p (m c k)"), raww[:, s, 0, 0:1024],
                                        f32(W13[:, s, 0].rearrange("p m c k -> p (m c k)")), ALU.subtract)\
                    .then_inc(F["w13_lo"], 1)

            def w2_lo(j, s):
                pool.wait_ge(F["w2_hi"], j + 1)
                nc.gpsimd.tensor_tensor(W2[:, s, 1], raww[:, s, 0, 1024:1536], f32(W2[:, s, 0]), ALU.subtract)\
                    .then_inc(F["w2_lo"], 1)

            def h_lo(j, s, b):
                pool.wait_ge(F["h_hi"], 2 * j + b + 1)
                sl = slice(b * SEQ, (b + 1) * SEQ)
                nc.gpsimd.tensor_tensor(hT[:, s, 1, sl], hh[:, b], f32(hT[:, s, 0, sl]), ALU.subtract)\
                    .then_inc(F["h_lo"], 1)

            prep(0, 0)
            w13_lo(0, 0)

            def body(j, s, first, last=False):
                w2_lo(j, s)
                if not last:
                    prep(j + 1, 1 - s)
                h_lo(j, s, 0)
                if not last:
                    w13_lo(j + 1, 1 - s)
                h_lo(j, s, 1)

            tiles(pool, nt - 1, body)
            body(nt - 1, (nt - 1) % 2, False, True)

        def act_ffn(act, F, nt, diff):
            def sign(j, s):
                if diff:
                    act.wait_ge(F["d"], j + 1)
                    nc.scalar.activation(raww[:, s, 0], raww[:, s, 0], ACT.Sign).then_inc(F["sign"], 1)

            def w13_hi(j, s):
                act.wait_ge(F["w"], j + 1)
                wait(act, F["gate"], 2 * (j - 1))
                nc.scalar.activation(W13[:, s, 0].rearrange("p m c k -> p (m c k)"), raww[:, s, 0, 0:1024],
                                     ACT.Copy).then_inc(F["w13_hi"], 1)

            def w2_hi(j, s):
                wait(act, F["down"], TT * (j - 1))
                nc.scalar.activation(W2[:, s, 0], raww[:, s, 0, 1024:1536], ACT.Copy).then_inc(F["w2_hi"], 1)

            def silu(j, b, tile_scale):
                act.wait_ge(F["gate"], 2 * j + b + 1)
                wait(act, F["h"], 2 * (j - 1) + b + 1)
                nc.scalar.activation(sg[:, b], PS[:, 2 * b, :], ACT.Silu, scale=tile_scale).then_inc(F["silu"], 1)

            def h_hi(j, s, b):
                act.wait_ge(F["h"], 2 * j + b + 1)
                wait(act, F["down"], TT * (j - 1))
                nc.scalar.activation(hT[:, s, 0, b * SEQ:(b + 1) * SEQ], hh[:, b], ACT.Copy).then_inc(F["h_hi"], 1)

            sign(0, 0)
            w13_hi(0, 0)

            def body(j, s, first, last=False):
                w2_hi(j, s)
                sc = 1.0 if diff else scale_g[:, s]
                silu(j, 0, sc)
                if not last:
                    sign(j + 1, 1 - s)
                h_hi(j, s, 0)
                silu(j, 1, sc)
                if not last:
                    w13_hi(j + 1, 1 - s)
                h_hi(j, s, 1)

            tiles(act, nt - 1, body)
            body(nt - 1, (nt - 1) % 2, False, True)

        def dve_ffn(dve, F, nt, diff, k):
            def combine(j, s):
                if diff:
                    dve.wait_ge(F["sign"], j + 1)
                    for m in range(3):
                        sl = slice(512 * m, 512 * (m + 1))
                        last = nc.vector.scalar_tensor_tensor(raww[:, s, 0, sl], raww[:, s, 0, sl], coeff[:, m:m + 1],
                                                              raww[:, s, 1, sl], ALU.mult, ALU.add)
                    last.then_inc(F["w"], 1)

            def h(j, s, b):
                dve.wait_ge(F["silu"], 2 * j + b + 1)
                wait(dve, F["h_lo"], 2 * (j - 1) + b + 1)
                if diff:
                    ins = nc.vector.tensor_tensor(hh[:, b], PS[:, 2 * b + 1, :], sg[:, b], ALU.mult)
                else:
                    ins = nc.vector.scalar_tensor_tensor(hh[:, b], PS[:, 2 * b + 1, :], scale_u[:, s],
                                                         sg[:, b], ALU.mult, ALU.mult)
                ins.then_inc(F["h"], 1)

            def yadd(j, t):
                dve.wait_ge(F["down"], TT * j + t + 1)
                nc.vector.tensor_tensor(y[:, t, :], PS[:, 4 + t % 4, :], y[:, t, :], ALU.add).then_inc(F["yadd"], 1)

            if diff:
                dve.wait_ge(A0["coeff"], 1)
            combine(0, 0)

            def body(j, s, first, last=False):
                h(j, s, 0)
                h(j, s, 1)
                if not last:
                    combine(j + 1, 1 - s)
                if not first:
                    for t in range(TT):
                        yadd(j - 1, t)

            tiles(dve, nt - 1, body)
            body(nt - 1, (nt - 1) % 2, False, True)
            for t in range(TT):
                yadd(nt - 1, t)
                if t >= 1:
                    norm_stats(dve, k, t - 1, t - 1, F["yadd"], TT * (nt - 1) + t)
            norm_stats(dve, k, TT - 1, TT - 1, F["yadd"], TT * nt)

        def pe_ffn(pe, F, nt):
            def gate(j, s, b):
                pe.wait_ge(F["w13_lo"], j + 1)
                wait(pe, F["h"], 2 * (j - 1) + b + 1)
                for m in range(2):
                    last = mm3(PS[:, 2 * b + m, :], lambda a, c: W13[:, s, a, m, c, :],
                               lambda q, c: xT[:, q, c, b * SEQ:(b + 1) * SEQ], DC)
                last.then_inc(F["gate"], 1)

            def down(j, s):
                pe.wait_ge(F["w2_lo"], j + 1)
                pe.wait_ge(F["h_lo"], 2 * j + 2)
                for t in range(TT):
                    wait(pe, F["yadd"], TT * j + t - 3)
                    mm3(PS[:, 4 + t % 4, :], lambda a, c: hT[:, s, a, t * P:(t + 1) * P],
                        lambda q, c: W2[:, s, q, :], 1).then_inc(F["down"], 1)

            def body(j, s, first):
                gate(j, s, 0)
                gate(j, s, 1)
                if not first:
                    down(j - 1, 1 - s)

            tiles(pe, nt, body)
            down(nt - 1, (nt - 1) % 2)

        A1 = names("a1", "raw_qkv", "raw_wo", "wq_hi", "wq_lo", "wk_hi", "wk_lo", "wv_hi", "wv_lo", "wo_hi", "wo_lo",
                   "tables", "vproj", "v", "vz", "stored0", "stored1", "kst", "qst0", "qst1", "mask", "mask_r",
                   "scores", "evac", "tiny", "stat", "nmax", "thr", "acc", "cut", "below", "pick", "tau", "flag_ps", "exp", "final",
                   "rinv", "pnorm", "turned", "pt", "pv", "o_hi", "o_lo", "yproj", "yadd")
        R1 = names("r1", "proj", "swap", "cos", "sin", "rot", "hi", "lo")
        NI = 5 * BATCH
        NB = 2 * TT

        TILES1 = [0, 1, 2, 3, 5, 6, 7, 4]

        def tile_of(x):
            n = x // 2
            i = TILES1[n] % QT if x < NB else 0
            return n, i, x % 2, (i + 1) * P

        def before(x, k=1):
            return k * sum(1 for v in range(x) if tile_of(v)[1] > 0)

        def stat_keys(i):
            return P * min(i, 2)

        def tcount(x, q, kb):
            return sum(4 * (tile_of(v)[1] + 1) for v in range(x)) + q * (tile_of(x)[1] + 1) + kb

        def sp_attn1(sp):
            sp.wait_ge(F0["yadd"], TT * NT0)
            sp.wait_ge(T["fed"], TT * 2 + 1)
            sp.dma_start(raw[:, 0:WO0], attn1_w[:, 0:WO0]).then_inc(A1["raw_qkv"], 16)
            sp.dma_start(raw[:, WO0:WCOLS], attn1_w[:, WO0:WCOLS]).then_inc(A1["raw_wo"], 16)
            sp.dma_start(AF[:, rope1_at:rope1_at + 1024], rope1).then_inc(A1["tables"], 16)
            sp.dma_start(ztab, quant[:, 0:6]).then_inc(A1["mask"], 16)
            sp.dma_start(iota16, quant[:, 8:24]).then_inc(A1["mask"], 16)
            sp.dma_start(mask0[:, 0:P], consts[:, 768:896]).then_inc(A1["mask"], 16)
            for r in range(NI):
                b, j = r // 5, r % 5
                sp.wait_ge(R1["lo"], r + 1)
                for s in range(2):
                    sp.dma_start(scr[b, j, s], f32(rq[:, r % 2, s, :])).then_inc(A1[f"stored{r % 2}"], 16)
            sp.wait_ge(A1["v"], TT)
            for s in range(2):
                sp.wait_ge(A1[f"stored{s}"], 16 * NI)
            for n in range(TT):
                b, i = n // QT, tile_of(2 * n)[1]
                if n % QT == 0:
                    if b > 0:
                        sp.wait_ge(A1["scores"], QT * 32)
                    for a, s in enumerate((0, 1, 0)):
                        src = scr[b, 4, s].rearrange("(c h) t -> c h t", c=HD1)
                        sp.dma_start(f32(kst[a * HD1:(a + 1) * HD1]), src).then_inc(A1["kst"], 16)
                for x in (2 * n, 2 * n + 1):
                    if x >= 2:
                        sp.wait_ge(A1["scores"], 16 * (x - 1))
                    for j in range(2):
                        for a, s in enumerate((0, 0, 1)):
                            src = scr[b, 2 * (x % 2) + j, s].rearrange("(c h) t -> c h t", c=HD1)
                            sp.dma_start(f32(qst[a * HD1:(a + 1) * HD1, x % 2, 8 * j:8 * j + 8]),
                                         src[:, :, i * P:(i + 1) * P]).then_inc(A1[f"qst{x % 2}"], 16)

        def pe_attn1(pe):
            for r in range(NI):
                b, j = r // 5, r % 5
                if j < 4:
                    pe.wait_ge(A1["wq_lo"], j + 1)
                else:
                    pe.wait_ge(A1["wk_lo"], 1)
                wait(pe, R1["cos"], r - 1)
                w = W1["q"][:, :, j] if j < 4 else W1["k"]
                mm3(PS[:, 6 + r % 2, :], lambda a, c: w[:, a, c, :], lambda m, c: xT[:, m, c, b * SEQ:(b + 1) * SEQ],
                    DC).then_inc(R1["proj"], 1)
                t = r - 2
                if t < 0:
                    continue
                pe.wait_ge(A1["wv_lo"], 1)
                wait(pe, A1["v"], t - 1)
                mm3(PS[:, 4 + t % 2, 0:P], lambda a, c: xT[:, a, c, t * P:(t + 1) * P],
                    lambda m, c: W1["v"][:, m, c, :], DC).then_inc(A1["vproj"], 1)
            pe.wait_ge(A1["mask_r"], 2)

            def scores(x, q):
                n, i, hf, W = tile_of(x)
                if q == 0:
                    pe.wait_ge(A1["kst"], 48 * (n // QT + 1))
                    pe.wait_ge(A1[f"qst{x % 2}"], 16 * 6 * (x // 2 + 1))
                for h in range(G1):
                    head = hf * 16 + 4 * q + h
                    wait(pe, A1["evac"], 16 * x + 4 * q + h - 3)
                    nc.tensor.matmul(PS[:, h, 0:W], qst[0:48, x % 2, 4 * q + h, :], kst[0:48, head // G1, 0:W],
                                     start=True, stop=False)
                    nc.tensor.matmul(PS[:, h, W - P:W], ident_r, mask_r, start=False, stop=True)\
                        .then_inc(A1["scores"], 1)

            def values(x, q):
                n, i, hf, W = tile_of(x)
                pe.wait_ge(A1["pnorm"], 4 * x + q + 1)
                for kb in range(i + 1):
                    tn = tcount(x, q, kb)
                    wait(pe, A1["pt"], tn - 1)
                    for h in range(G1):
                        last = nc.tensor.transpose(PS[:, 4 + tn % 2, h * P:(h + 1) * P],
                                                   P1[:, q % 2, h, kb * P:(kb + 1) * P], ident)
                    last.then_inc(A1["turned"], 1)
                    if kb >= 1:
                        product(x, q, kb - 1)
                product(x, q, i)

            def product(x, q, kb):
                n, i, hf, W = tile_of(x)
                tn = tcount(x, q, kb)
                kv = 4 * hf + q
                pe.wait_ge(A1["pt"], tn + 1)
                if kv == 0 and kb == 0:
                    pe.wait_ge(A1["vz"], n // QT + 1)
                    wait(pe, A1["o_lo"], n)
                nc.tensor.matmul(PS[:, 6, :], Vz[:, kb, kv * P:(kv + 1) * P], PT1[:, tn % 2, :],
                                 start=(kv == 0 and kb == 0), stop=(kv == KVH1 - 1 and kb == i))\
                    .then_inc(A1["pv"], 1)

            def project(n):
                pe.wait_ge(A1["wo_lo"], 1)
                pe.wait_ge(A1["o_lo"], n + 1)
                wait(pe, A1["yadd"], n)
                mm3(PS[:, 7, :], lambda a, c: OT1[:, a, c, :], lambda m, c: W1["o"][:, m, c, :], G1)\
                    .then_inc(A1["yproj"], 1)

            for x in range(-1, NB + 2):
                xp = x - 1
                if x + 1 < NB:
                    scores(x + 1, 0)
                if xp >= 1 and (xp - 1) % 2:
                    project((xp - 1) // 2)
                if 0 <= xp < NB and tile_of(xp)[1] > 0:
                    pe.wait_ge(A1["cut"], before(xp) + 1)
                    nc.tensor.matmul(PS[:, 7, 0:1], ones, flag_row, start=True, stop=True)\
                        .then_inc(A1["flag_ps"], 1)
                for q in range(4):
                    if x + 1 < NB and q < 3:
                        scores(x + 1, q + 1)
                    if 0 <= xp < NB:
                        values(xp, q)

        def act_attn1(act):
            for h in range(4):
                split_hi(act, A1, "q", 0, h)
            for k in ("k", "v", "o"):
                split_hi(act, A1, k, 0)
            for r in range(NI):
                src = PS[:, 6 + r % 2, :]
                act.wait_ge(R1["proj"], r + 1)
                wait(act, R1["rot"], r - 1)
                nc.scalar.activation(qs[0:64, r % 2, :], src[64:128, :], ACT.Copy)
                nc.scalar.activation(qs[64:128, r % 2, :], src[0:64, :], ACT.Copy).then_inc(R1["swap"], 1)
                act.wait_ge(R1["rot"], r + 1)
                wait(act, A1[f"stored{r % 2}"], 32 * (r // 2))
                nc.scalar.activation(rq[:, r % 2, 0, :], rot, ACT.Copy).then_inc(R1["hi"], 1)
                t = r - 2
                if t < 0:
                    continue
                act.wait_ge(A1["vproj"], t + 1)
                nc.scalar.activation(Vc[:, t, :], PS[:, 4 + t % 2, 0:P], ACT.Copy).then_inc(A1["v"], 1)
            act.wait_ge(A1["vproj"], TT)
            act.wait_ge(A1["mask"], 48)
            nc.scalar.activation(ident_r, ident, ACT.Copy).then_inc(A1["mask_r"], 1)
            nc.scalar.activation(mask_r, mask0[:, 0:P], ACT.Copy).then_inc(A1["mask_r"], 1)

            def count(x, r, heads=range(16)):
                n, i, hf, W = tile_of(x)
                act.wait_ge(A1["thr"], ROUNDS * before(x) + r + 1)
                k = 16 * (ROUNDS * before(x) + r)
                for h in heads:
                    if r < ROUNDS - 1:
                        wait(act, A1["acc"], k + h - 1)
                        place = junk[h % 2]
                    else:
                        wait(act, A1["below"], 16 * (before(x) - 1) + h + 1)
                        place = sgn[:, h, :]
                    nc.scalar.activation(place[:, 0:W], S1[x % 2][:, h, 0:W], ACT.Sign,
                                         bias=st["nthr"][:, x % 2, h:h + 1],
                                         accum_out=acc[:, ACC_OF[r], h:h + 1]).then_inc(A1["acc"], 1)

            def exp(x, q):
                n, i, hf, W = tile_of(x)
                act.wait_ge(A1["nmax"], x + 1)
                act.wait_ge(A1["tau"], x + 1)
                un = 4 * x + q
                if un >= 2:
                    xx, qq = (x, q - 2) if q >= 2 else (x - 1, q + 2)
                    act.wait_ge(A1["turned"], tcount(xx, qq, tile_of(xx)[1]) + 1)
                for h in range(G1):
                    hd = 4 * q + h
                    kw = {} if i > 0 else {"accum_out": rsum1[:, hd:hd + 1]}
                    last = nc.scalar.activation(P1[:, q % 2, h, 0:W], S1[x % 2][:, hd, 0:W], ACT.Exp,
                                                bias=st["nmax"][:, x % 2, hd:hd + 1], scale=SCALE1, **kw)
                last.then_inc(A1["exp"], 1)

            def pt(x, q):
                for kb in range(tile_of(x)[1] + 1):
                    tn = tcount(x, q, kb)
                    act.wait_ge(A1["turned"], tn + 1)
                    wait(act, A1["pv"], tn - 1)
                    nc.scalar.activation(PT1[:, tn % 2, :], PS[:, 4 + tn % 2, :], ACT.Copy).then_inc(A1["pt"], 1)

            for x in range(0, NB + 2):
                xp = x - 1
                search = x < NB and tile_of(x)[1] > 0

                def last_round(q):
                    if search:
                        count(x, ROUNDS - 1, range(4 * q, 4 * q + 4))

                if search:
                    count(x, 0)
                if x >= 3 and x % 2:
                    n = (x - 3) // 2
                    act.wait_ge(A1["pv"], tcount(x - 1, 0, 0))
                    wait(act, A1["yproj"], n)
                    nc.scalar.activation(OT1[:, 0], PS[:, 6, :].rearrange("p (h k) -> p h k", h=4), ACT.Copy)\
                        .then_inc(A1["o_hi"], 1)
                if search:
                    for r in range(1, ROUNDS - 1):
                        count(x, r)
                if 0 <= xp < NB:
                    exp(xp, 0)
                    exp(xp, 1)
                    last_round(0)
                    pt(xp, 0)
                    exp(xp, 2)
                    last_round(1)
                    pt(xp, 1)
                    exp(xp, 3)
                    last_round(2)
                    pt(xp, 2)
                    last_round(3)
                    pt(xp, 3)
                else:
                    for q in range(4):
                        last_round(q)

        def pool_attn1(pool):
            for h in range(4):
                split_lo(pool, A1, "q", 0, h)
            for k in ("k", "v", "o"):
                split_lo(pool, A1, k, 0)
            pool.wait_ge(A1["tables"], 16)
            for r in range(NI):
                pool.wait_ge(R1["swap"], r + 1)
                nc.gpsimd.tensor_tensor(qs[:, r % 2, :], qs[:, r % 2, :], stab, ALU.mult).then_inc(R1["sin"], 1)

            def norm(x, q):
                n, i, hf, W = tile_of(x)
                pool.wait_ge(A1["rinv"], 4 * x + q + 1)
                sl = P1[:, q % 2, :, 0:W]
                nc.gpsimd.tensor_tensor(sl, sl, rinv1[:, 4 * q:4 * q + 4].unsqueeze(2).to_broadcast([P, G1, W]),
                                        ALU.mult).then_inc(A1["pnorm"], 1)

            for x in range(NB):
                for q in range(4):
                    norm(x, q)

        def dve_attn1(dve):
            v = nc.vector
            nc.vector.memset(Vz, 0.0).then_inc(A1["tiny"], 1)
            dve.wait_ge(A1["tables"], 16)
            for r in range(NI):
                dve.wait_ge(R1["swap"], r + 1)
                wait(dve, R1["rot"], r)
                v.tensor_tensor(tcos, PS[:, 6 + r % 2, :], ctab, ALU.mult).then_inc(R1["cos"], 1)
                dve.wait_ge(R1["sin"], r + 1)
                dve.wait_ge(R1["cos"], r + 1)
                wait(dve, R1["hi"], r)
                wait(dve, R1["lo"], r)
                v.tensor_tensor(rot, tcos, qs[:, r % 2, :], ALU.add).then_inc(R1["rot"], 1)
                dve.wait_ge(R1["hi"], r + 1)
                v.tensor_tensor(rq[:, r % 2, 1, :], rot, f32(rq[:, r % 2, 0, :]), ALU.subtract)\
                    .then_inc(R1["lo"], 1)
            dve.wait_ge(A1["v"], TT)
            dve.wait_ge(A1["wo_lo"], 1)
            dve.wait_ge(A1["mask"], 48)
            dve.wait_ge(A1["mask_r"], 2)
            for s in range(2):
                dve.wait_ge(A1[f"stored{s}"], 16 * NI)
            tiny = [1]

            def step(ins):
                ins.then_inc(A1["tiny"], 1)
                tiny[0] += 1
                dve.wait_ge(A1["tiny"], tiny[0])

            def evac(x, q):
                n, i, hf, W = tile_of(x)
                if x >= 2:
                    dve.wait_ge(A1["exp"], 4 * (x - 2) + q + 1)
                    if tile_of(x - 2)[1] > 0:
                        dve.wait_ge(A1["final"], 4 * before(x - 2) + q + 1)
                for h in range(4 * q, 4 * q + 4):
                    dve.wait_ge(A1["scores"], 16 * x + h + 1)
                    v.tensor_scalar(S1[x % 2][:, h, 0:W], PS[:, h % 4, 0:W], 0.0, TAKEN, ALU.add, ALU.max,
                                    accum_out=st["rmax"][:, x % 2, h:h + 1]).then_inc(A1["evac"], 1)
                if i > 0:
                    for h in range(4 * q, 4 * q + 4):
                        dve.wait_ge(A1["evac"], 16 * x + h + 1)
                        v.bn_stats(stat6[:, h, :], S1[x % 2][:, h, 0:stat_keys(i)]).then_inc(A1["stat"], 1)

            def start(x):
                n, i, hf, W = tile_of(x)
                dve.wait_ge(A1["evac"], 16 * x + 16)
                v.tensor_scalar(st["nmax"][:, x % 2], st["rmax"][:, x % 2], -SCALE1, None, ALU.mult)\
                    .then_inc(A1["nmax"], 1)
                if i == 0:
                    return
                N = stat_keys(i)
                dve.wait_ge(A1["stat"], 16 * before(x) + 16)
                me, mo, ve, vo = (stat6[:, :, k] for k in (1, 4, 2, 5))
                step(v.tensor_tensor(st["msum"], me, mo, ALU.add))
                step(v.tensor_tensor(st["mdiff"], me, mo, ALU.subtract))
                step(v.tensor_tensor(st["mdiff"], st["mdiff"], st["mdiff"], ALU.mult))
                step(v.tensor_tensor(st["vsum"], ve, vo, ALU.add))
                step(v.scalar_tensor_tensor(st["vsum"], st["mdiff"], N / 4.0, st["vsum"], ALU.mult, ALU.add))
                step(v.scalar_tensor_tensor(st["spread"], st["msum"], -0.5, st["rmax"][:, x % 2], ALU.mult, ALU.add))
                step(v.tensor_scalar(st["spread"], st["spread"], 0.36, 1e-30, ALU.mult, ALU.max))
                step(v.reciprocal(st["scaled"], st["spread"]))
                step(v.scalar_tensor_tensor(st["vsum"], st["vsum"], 1.0 / N, st["scaled"], ALU.mult, ALU.mult))
                step(v.tensor_tensor(st["spread"], st["spread"], st["vsum"], ALU.add))
                step(v.tensor_scalar(st["step"], st["spread"], ztab[:, i - 1:i], None, ALU.mult))
                step(v.tensor_scalar(st["nslope"], st["spread"], ztab[:, 2 + i:3 + i], None, ALU.mult))
                v.scalar_tensor_tensor(st["nthr"][:, x % 2], st["msum"], -0.5, st["step"], ALU.mult, ALU.add)\
                    .then_inc(A1["thr"], 1)

            def update(x, r):
                n, i, hf, W = tile_of(x)
                aim = 2.0 * AIM - W
                a, before_a, t = acc[:, ACC_OF[r]], acc[:, ACC_OF[r - 1]], st["nthr"][:, x % 2]
                dve.wait_ge(A1["acc"], 16 * (ROUNDS * before(x) + r + 1))
                if r < 2:
                    step(v.scalar_tensor_tensor(st["step"], a, aim, st["nslope"], ALU.subtract, ALU.mult))
                else:
                    step(v.tensor_tensor(st["drop"], before_a, a, ALU.subtract))
                    step(v.tensor_tensor(st["scaled"], st["step"], st["drop"], ALU.mult))
                    step(v.scalar_tensor_tensor(st["scaled"], st["nslope"], PRIOR, st["scaled"], ALU.mult, ALU.add))
                    step(v.tensor_tensor(st["square"], st["drop"], st["drop"], ALU.mult))
                    step(v.tensor_scalar(st["square"], st["square"], PRIOR, None, ALU.add))
                    step(v.reciprocal(st["square"], st["square"]))
                    step(v.tensor_tensor(st["scaled"], st["scaled"], st["square"], ALU.mult))
                    step(v.tensor_scalar(st["err"], a, aim, None, ALU.subtract))
                    step(v.tensor_tensor(st["step"], st["scaled"], st["err"], ALU.mult))
                    step(v.tensor_tensor(st["err"], st["err"], st["err"], ALU.mult))
                    step(v.scalar_tensor_tensor(st["step"], st["err"], (WINDOW - 1.0) ** 2 + 1, st["step"],
                                                ALU.is_gt, ALU.mult))
                v.tensor_tensor(t, t, st["step"], ALU.add).then_inc(A1["thr"], 1)

            def pick(x, q):
                n, i, hf, W = tile_of(x)
                for pair in (2 * q,):
                    for h in (pair, pair + 1):
                        wait(dve, A1["pick"], 3 * (16 * before(x) + pair) - 1 + h % 2)
                        dve.wait_ge(A1["acc"], 16 * (ROUNDS * before(x) + ROUNDS - 1) + h + 1)
                        v.scalar_tensor_tensor(X1[:, h % 2, 0:W], sgn[:, h, 0:W], DROPPED, S1[x % 2][:, h, 0:W],
                                               ALU.mult, ALU.min).then_inc(A1["below"], 1)
                    k = 16 * before(x) + pair
                    for h in (pair, pair + 1):
                        dve.wait_ge(A1["below"], 16 * before(x) + h + 1)
                        v.max(best[:, h, 0:8], X1[:, h % 2, 0:W]).then_inc(A1["pick"], 1)
                    for h in (pair, pair + 1):
                        wk = X1[:, h % 2, 0:W]
                        dve.wait_ge(A1["pick"], 3 * k + 1 + h % 2)
                        v.match_replace(wk, best[:, h, 0:8], wk, TAKEN).then_inc(A1["pick"], 1)
                    for h in (pair, pair + 1):
                        dve.wait_ge(A1["pick"], 3 * k + 3 + h % 2)
                        v.max(best[:, h, 8:16], X1[:, h % 2, 0:W]).then_inc(A1["pick"], 1)

            def cut(x):
                n, i, hf, W = tile_of(x)
                missing, after = rsum1, rsum1
                wait(dve, A1["pnorm"], 4 * x)
                dve.wait_ge(A1["acc"], 16 * ROUNDS * (before(x) + 1))
                step(v.tensor_scalar(missing, acc[:, ACC_OF[3]], -0.5, TOPK - W / 2.0, ALU.mult, ALU.add))
                step(v.tensor_tensor(hit, iota16.unsqueeze(1).to_broadcast([P, 16, 16])[:, :, 0:WINDOW],
                                     missing.unsqueeze(2).to_broadcast([P, 16, 16])[:, :, 0:WINDOW], ALU.is_equal))
                dve.wait_ge(A1["pick"], 3 * (16 * before(x) + 16))
                step(v.tensor_tensor(val, hit, best[:, :, 0:WINDOW], ALU.mult))
                step(v.tensor_reduce(st["tau"][:, x % 2], val, AX.X, ALU.add))
                step(v.tensor_tensor(val, hit, best[:, :, 1:WINDOW + 1], ALU.mult))
                step(v.tensor_reduce(after, val, AX.X, ALU.add))
                step(v.tensor_tensor(after, after, st["tau"][:, x % 2], ALU.is_lt))
                v.tensor_reduce(flag_row, after, AX.X, ALU.add).then_inc(A1["cut"], 1)

            def resolve(x):
                n, i, hf, W = tile_of(x)
                dve.wait_ge(A1["flag_ps"], before(x) + 1)
                step(v.tensor_copy(flag_int, PS[0:1, 7, 0:1]))
                wait(dve, A1["turned"], tcount(x, 0, 0))
                good = dve.value_load(flag_int)
                with dve.If(good != RESOLVED):
                    for h in range(16):
                        row, wk = S1[x % 2][:, h, 0:W], P1[:, 0, 0, 0:W]
                        v.tensor_copy(wk, row)
                        dve.drain()
                        with dve.Fori(0, TOPK // 8):
                            v.max(best[:, h, 0:8], wk)
                            dve.drain()
                            v.match_replace(wk, best[:, h, 0:8], wk, TAKEN)
                            dve.drain()
                        v.tensor_scalar(wk, wk, TAKEN, DROPPED, ALU.not_equal, ALU.mult)
                        dve.drain()
                        v.tensor_tensor(row, row, wk, ALU.add)
                        dve.drain()
                    v.memset(st["tau"][:, x % 2], -1.0e38)
                    dve.drain()
                v.tensor_copy(flag_row, flag_row).then_inc(A1["tau"], 1)

            def final(x, q):
                n, i, hf, W = tile_of(x)
                dve.wait_ge(A1["exp"], 4 * x + q + 1)
                if i > 0:
                    for h in range(4 * q, 4 * q + 4):
                        pr = P1[:, q % 2, h % 4, 0:W]
                        last = v.scalar_tensor_tensor(pr, S1[x % 2][:, h, 0:W], st["tau"][:, x % 2, h:h + 1], pr,
                                                      ALU.is_ge, ALU.mult, accum_out=rsum1[:, h:h + 1])
                    last.then_inc(A1["final"], 1)
                    dve.wait_ge(A1["final"], 4 * before(x) + q + 1)
                v.reciprocal(rinv1[:, 4 * q:4 * q + 4], rsum1[:, 4 * q:4 * q + 4]).then_inc(A1["rinv"], 1)

            for x in range(-1, NB + 2):
                xp = x - 1
                topk = 0 <= xp < NB and tile_of(xp)[1] > 0
                done = (x - 3) // 2 if x >= 3 and x % 2 else -1
                search = 0 <= x < NB and tile_of(x)[1] > 0
                for pair in range(8):
                    if topk:
                        pick(xp, pair)
                    if search and pair in (2, 5):
                        update(x, (pair - 2) // 3)
                    if done >= 0 and pair == 3:
                        dve.wait_ge(A1["o_hi"], done + 1)
                        v.tensor_tensor(OT1[:, 1], PS[:, 6, :].rearrange("p (h k) -> p h k", h=4), f32(OT1[:, 0]),
                                        ALU.subtract).then_inc(A1["o_lo"], 1)
                    if done >= 0 and pair == 7:
                        dve.wait_ge(A1["yproj"], done + 1)
                        t = TILES1[done]
                        v.tensor_tensor(y[:, t, :], PS[:, 7, :], y[:, t, :], ALU.add).then_inc(A1["yadd"], 1)
                        norm_stats(dve, 3, done, t, A1["yadd"], done + 1)
                if topk:
                    cut(xp)
                if search:
                    update(x, 2)
                if 0 <= xp < NB and xp % (2 * QT) == 0:
                    b = xp // (2 * QT)
                    if b > 0:
                        dve.wait_ge(A1["pv"], tcount(xp, 0, 0))
                    dve.wait_ge(A1["tiny"], 1)
                    dst = Vz.rearrange("p j (v c) -> p j v c", c=P + HD1)[:, :, :, 0:HD1]
                    src = Vc[:, b * QT:(b + 1) * QT, :].rearrange("p j (v c) -> p j v c", c=HD1)
                    v.tensor_copy(dst, src).then_inc(A1["vz"], 1)
                if topk:
                    resolve(xp)
                elif 0 <= xp < NB:
                    v.memset(st["tau"][:, xp % 2], 0.0).then_inc(A1["tau"], 1)
                for q in range(4):
                    if 0 <= xp < NB:
                        final(xp, q)
                    if x + 1 < NB:
                        evac(x + 1, q)
                if x + 1 < NB:
                    start(x + 1)

        CONST_DMAS = 3

        block = ctx.enter_context(nc.Block())

        @block.sync
        def _(sp):
            for t in range(TT):
                sp.dma_start(y[:, t, :], x[t * P:(t + 1) * P, :]).then_inc(s_x, 16)
            sp.dma_start(ident, consts[:, 0:128]).then_inc(s_const, 16)
            sp.dma_start(mask0, consts[:, 128:384]).then_inc(s_const, 16)
            sp.dma_start(AF[:, base + WCOLS:base + WCOLS + 1024], rope0).then_inc(s_const, 16)
            sp_attn0(sp)

            def free0(sp):
                sp.wait_ge(A0["mean_abs"], 6 * KVH0)
                sp.wait_ge(A0["yadd"], NU * KVH0)
            if stop_after >= 2:
                sp_ffn(sp, F0, NT0, ffn0_w, True, free0)
            if stop_after >= 3:
                sp_attn1(sp)

            def free1(sp):
                sp.wait_ge(A1["yadd"], TT)
                sp.dma_start(adrow, ad_rows).then_inc(F1["ad"], 16)
            if stop_after >= 4:
                sp_ffn(sp, F1, NT1, ffn1_w, False, free1)
            for t in range(TT):
                sp.wait_ge(T["fed"], TT * min(stop_after, 4) + t + 1)
                sp.dma_start(out[t * P:(t + 1) * P, :], y[:, t, :]).then_inc(s_out, 16)
            sp.wait_ge(s_out, 16 * TT)

        @block.tensor
        def _(pe):
            pe.wait_ge(s_const, 16 * CONST_DMAS)
            turn_pe(pe, 0)
            pe.wait_ge(s_ready, 1)
            pe_attn0(pe)
            turn_pe(pe, 1)
            if stop_after >= 2:
                pe_ffn(pe, F0, NT0)
                turn_pe(pe, 2)
            if stop_after >= 3:
                pe_attn1(pe)
                turn_pe(pe, 3)
            if stop_after >= 4:
                pe_ffn(pe, F1, NT1)

        @block.scalar
        def _(act):
            turn_act(act, 0)
            act_attn0(act)
            norm_act(act, 1)
            turn_act(act, 1)
            if stop_after >= 2:
                act_ffn(act, F0, NT0, True)
                norm_act(act, 2)
                turn_act(act, 2)
            if stop_after >= 3:
                act_attn1(act)
                norm_act(act, 3)
                turn_act(act, 3)
            if stop_after >= 4:
                act.wait_ge(F1["ad"], 16)
                act_ffn(act, F1, NT1, False)
                norm_act(act, 4)

        @block.gpsimd
        def _(pool):
            pool_attn0(pool)
            if stop_after >= 2:
                pool_ffn(pool, F0, NT0, True)
            if stop_after >= 3:
                pool_attn1(pool)
            if stop_after >= 4:
                pool.wait_ge(F1["ad"], 16)
                pool_ffn(pool, F1, NT1, False)

        @block.vector
        def _(dve):
            nc.vector.memset(ones, 1.0).then_inc(s_ready, 1)
            for t in range(TT):
                dve.wait_ge(s_x, 16 * TT)
                nc.vector.tensor_copy(nwt[:, 0:1], y[:, t, 0:1]).then_inc(T["fed"], 1)
                dve.wait_ge(T["fed"], t + 1)
            for t in range(TT):
                turn_dve(dve, 0, t)
            dve_attn0(dve)

            norm_dve(dve, 1)
            if stop_after >= 2:
                dve_ffn(dve, F0, NT0, True, 2)
                norm_dve(dve, 2)
            if stop_after >= 3:
                dve_attn1(dve)
                norm_dve(dve, 3)
            if stop_after >= 4:
                dve.wait_ge(F1["ad"], 16)
                dve_ffn(dve, F1, NT1, False, 4)
                norm_dve(dve, 4, turns=False)


def _constants():
    i = np.arange(P)
    ident = np.eye(P, dtype=np.float32)
    neg = np.float32(NEG)
    prev = np.where(i[None, :] > i[:, None], np.float32(0), neg)
    diag = np.where(i[None, :] <= i[:, None], np.float32(0), neg)
    consts = np.concatenate([ident, prev, diag, np.zeros((P, 384), np.float32),
                             np.maximum(diag, np.float32(DROPPED))], axis=1).astype(np.float32)

    def table(inv_freq, freq_of_row):
        ang = np.arange(SEQ, dtype=np.float32)[None, :] * inv_freq[freq_of_row][:, None]
        sign = np.where(np.arange(P) < 64, np.float32(-1), np.float32(1))[:, None]
        return np.concatenate([np.cos(ang), np.sin(ang) * sign], axis=1).astype(np.float32)

    half0 = HD0 // 2
    f0 = (np.float32(10000.0) ** (-np.arange(half0, dtype=np.float32) / np.float32(half0))).astype(np.float32)
    f1 = (np.float32(1.0) / np.float32(10000.0) ** (np.arange(0, HD1, 2, dtype=np.float32) / np.float32(HD1)))
    rope0 = table(f0, np.arange(P) % half0)
    rope1 = table(f1.astype(np.float32), (np.arange(P) % 64) // 8)
    return consts, rope0, rope1


def _normal_quantile(p):
    lo, hi = -8.0, 8.0
    for _ in range(60):
        mid = 0.5 * (lo + hi)
        lo, hi = (mid, hi) if 0.5 * (1.0 + math.erf(mid / math.sqrt(2.0))) < p else (lo, mid)
    return 0.5 * (lo + hi)


def _quantiles():
    q = np.arange(P)[:, None] + P * np.arange(1, QT)[None, :] + 1.0
    z = np.vectorize(_normal_quantile)(1.0 - AIM / q)
    slope = 0.25 * np.sqrt(2 * np.pi) * np.exp(z * z / 2) / q
    one_to_16 = np.broadcast_to(np.arange(1.0, 17.0), (P, 16))
    return np.concatenate([-0.5 * z, -slope, np.zeros((P, 2)), one_to_16], axis=1).astype(np.float32)


def _chunks(w):
    n = w.shape[1] // P
    return w.reshape(DC, P, n, P).transpose(2, 1, 0, 3)


def _layout(i):
    wq, wk, wv = (_chunks(np.asarray(i[k])) for k in ("L0_attn_wq", "L0_attn_wk", "L0_attn_wv"))
    wo = np.asarray(i["L0_attn_wo"]).reshape(KVH0, G0, P, D).transpose(0, 2, 1, 3).reshape(KVH0, P, G0 * D)
    wq = wq.reshape(KVH0, G0, P, DC * P).transpose(0, 2, 1, 3).reshape(KVH0, P, G0 * DC * P)
    attn0 = np.concatenate([wq, wk.reshape(KVH0, P, -1), wv.reshape(KVH0, P, -1), wo], axis=2)

    def ffn(w1, w3, w2, nt):
        pad = nt * P - w1.shape[0]
        w1, w3 = (np.pad(w, ((0, pad), (0, 0))) for w in (w1, w3))
        w2 = np.pad(w2, ((0, 0), (0, pad)))
        g, u = (_chunks(w.T).reshape(nt, P, D) for w in (w1, w3))
        return np.concatenate([g, u, w2.T.reshape(nt, P, D)], axis=2)

    a = lambda n: np.asarray(i[n])
    ffn0 = np.stack([ffn(a("L0_ffn_w1"), a("L0_ffn_w3"), a("L0_ffn_w2"), NT0),
                     ffn(a("L0_ffn_mean_w1"), a("L0_ffn_mean_w3"), a("L0_ffn_mean_w2"), NT0)], axis=2).reshape(NT0, P, 2 * FCOLS)
    ffn1 = ffn(a("L1_ffn_Wg"), a("L1_ffn_Wu"), a("L1_ffn_Wd"), NT1)
    pairs = [np.stack([a(f"L0_ffn_{w}").reshape(KVH0, 2, P, MCH), a(f"L0_ffn_mean_{w}").reshape(KVH0, 2, P, MCH)], axis=3)
             for w in ("w1", "w3", "w2")]
    mean = np.stack(pairs, axis=1).reshape(KVH0 * 6, P, 2, MCH)

    def heads_last(w, n):
        return w.reshape(n // 8, 8, HD1, D).transpose(0, 2, 1, 3).reshape(n // 8 * P, D)
    q1 = _chunks(heads_last(a("L1_attn_Wq"), 32).T).transpose(1, 0, 2, 3).reshape(P, 4 * D)
    k1 = _chunks(heads_last(a("L1_attn_Wk"), 8).T).transpose(1, 0, 2, 3).reshape(P, D)
    v1 = _chunks(a("L1_attn_Wv").T).transpose(1, 0, 2, 3).reshape(P, D)
    o1 = a("L1_attn_Wo").T.reshape(KVH1, G1, HD1, D).transpose(0, 2, 1, 3).reshape(P, G1 * D)
    attn1 = np.concatenate([q1, k1, v1, o1], axis=1)

    pad = NT1 * P - INT1
    scales = [np.pad(a(n), (0, pad)).reshape(NT1, P, 1) for n in ("L1_ffn_ag", "L1_ffn_au")]
    ffn1 = np.concatenate([ffn1] + scales, axis=2)
    rows = np.broadcast_to(a("L1_ffn_ad")[None, :], (P, D))
    consts, rope0, rope1 = _constants()
    return {"x": a("L0_attn_x").reshape(TOK, D), "attn0_w": attn0, "ffn0_w": ffn0, "mean_w": mean, "attn1_w": attn1,
            "ffn1_w": ffn1, "ad_rows": rows, "quant": _quantiles(), "consts": consts, "rope0": rope0, "rope1": rope1}


STOP = 99


def kernel(**inputs):
    import concourse.bacc as _bacc
    from concourse.bass_utils import run_bass_kernel_spmd as _run

    nc = _bacc.Bacc("TRN2", target_bir_lowering=False, num_devices=1)
    arrays, args = {}, []
    for name, a in _layout(inputs).items():
        a = np.ascontiguousarray(a)
        arrays[f"in_{name}"] = a
        args.append(nc.dram_tensor(f"in_{name}", a.shape, mybir.dt.from_np(a.dtype), kind="ExternalInput").ap())
    args.append(nc.dram_tensor("out_0", (TOK, D), F32, kind="ExternalOutput").ap())
    build_kernel(nc, *args, stop_after=STOP)
    r = _run(nc, [arrays], core_ids=[0])
    return r.results[0]["out_0"].reshape(BATCH, SEQ, D)
```
